# Optimizing a Trainium2 kernel written in Bass

```python
import numpy as np
import jax
import jax.numpy as jnp

def _softmax(x, axis=-1):
    return jax.nn.softmax(x, axis=axis)
def _gelu(x):
    return jax.nn.gelu(x, approximate=True)
def _silu(x):
    return jax.nn.silu(x)
def _sigmoid(x):
    return jax.nn.sigmoid(x)
def _layernorm(x, axis=-1, eps=1e-5):
    m = jnp.mean(x, axis=axis, keepdims=True)
    v = jnp.var(x, axis=axis, keepdims=True)
    return (x - m) / jnp.sqrt(v + eps)
def _scatter_add(tgt, idx, src, axis=0):
    return tgt.at[idx].add(src)
def _segment_sum(src, seg, n):
    return jax.ops.segment_sum(src, seg, n)

kernel_name = 'mk_conv_preact_d2_conv_nchw96_d9cb63'

def setup_inputs(seed: int = 0):
    np.random.seed(seed)
    _w = jnp.asarray
    def _rec_inputs():
        import jax
        import jax.numpy as jnp
        _gk = jax.random.key(seed)
        x = -0.0003744 + 1 * jax.random.normal(jax.random.fold_in(_gk, 1), (4, 96, 48, 48), jnp.float32)
        return x
    x = _rec_inputs()
    def _L0_conv_setup():
        import jax, jax.numpy as jnp
        import numpy as np
        K = 8
        LOCAL_WINDOW_RATIO = 0.25
        NEG = -1000000000.0
        LN_EPS = 1e-05
        NORM_EPS = 1e-12

        def _window_indices(H, W):
            lws = max(3, int(min(H, W) * LOCAL_WINDOW_RATIO))
            if lws % 2 == 0:
                lws += 1
            half = lws // 2
            off = jnp.arange(-half, half + 1)
            dy, dx = jnp.meshgrid(off, off, indexing='ij')
            dy = dy.reshape(-1)
            dx = dx.reshape(-1)
            py, px = jnp.meshgrid(jnp.arange(H), jnp.arange(W), indexing='ij')
            py = py.reshape(-1)
            px = px.reshape(-1)
            ny = py[:, None] + dy[None, :]
            nx = px[:, None] + dx[None, :]
            valid = (ny >= 0) & (ny < H) & (nx >= 0) & (nx < W)
            idx = jnp.clip(ny, 0, H - 1) * W + jnp.clip(nx, 0, W - 1)
            return (idx, valid)
        key = jax.random.key(seed)
        ks = jax.random.split(key, 5)
        B, C, H, W = (4, 96, 48, 48)
        return {'x': jax.random.normal(ks[0], (B, C, H, W), jnp.float32), 'w1': jax.random.normal(ks[1], (2 * C, C), jnp.float32) * 0.05, 'b1': jax.random.normal(ks[2], (2 * C,), jnp.float32) * 0.05, 'w2': jax.random.normal(ks[3], (C, 2 * C), jnp.float32) * 0.05, 'b2': jax.random.normal(ks[4], (C,), jnp.float32) * 0.05, 'ln_w': jnp.ones((C,), jnp.float32), 'ln_b': jnp.zeros((C,), jnp.float32)}
    _L0_conv_all = _L0_conv_setup()
    _L0_conv_in = {k: v for k, v in _L0_conv_all.items() if k in ('w1', 'b1', 'w2', 'b2', 'ln_w', 'ln_b', )}
    del _L0_conv_all

    def _L1_conv_setup():
        import jax, jax.numpy as jnp
        import numpy as np
        B, DM, H, W = (2, 96, 48, 48)
        E = 192
        R, N = (6, 16)

        def conv2d(x, w, b, groups=1, pad=0):
            out = jax.lax.conv_general_dilated(x, w, window_strides=(1, 1), padding=[(pad, pad), (pad, pad)], dimension_numbers=('NCHW', 'OIHW', 'NCHW'), feature_group_count=groups)
            return out + b[None, :, None, None]
        key = jax.random.key(seed)
        ks = jax.random.split(key, 24)
        f = lambda k, shape, s: jax.random.normal(k, shape, jnp.float32) * s
        inp = {'x': jax.random.normal(ks[0], (B, DM, H, W), jnp.float32), 'in_proj_w': f(ks[1], (2 * E, DM), 0.05), 'conv_w': f(ks[2], (E, 1, 3, 3), 0.2), 'conv_b': f(ks[3], (E,), 0.1), 'x_proj_w': f(ks[4], (4, R + 2 * N, E), 0.01), 'dt_proj_w': f(ks[5], (4, E, R), 0.01), 'dt_proj_b': jnp.full((4, E), -9.0) + f(ks[6], (4, E), 0.1), 'A_log': jnp.tile(jnp.log(jnp.arange(1, N + 1, dtype=jnp.float32))[None, None, :], (4, E, 1)), 'Ds': jnp.ones((4, E), jnp.float32), 'ln_g': jnp.ones(E, jnp.float32), 'ln_b': jnp.zeros(E, jnp.float32), 'c1_w': f(ks[7], (2 * E, E, 1, 1), 0.05), 'c1_b': jnp.zeros(2 * E), 'bn1_g': jnp.ones(2 * E), 'bn1_b': jnp.zeros(2 * E), 'bn1_m': jnp.zeros(2 * E), 'bn1_v': jnp.ones(2 * E), 'c2_w': f(ks[8], (2 * E, 1, 3, 3), 0.2), 'c2_b': jnp.zeros(2 * E), 'bn2_g': jnp.ones(2 * E), 'bn2_b': jnp.zeros(2 * E), 'bn2_m': jnp.zeros(2 * E), 'bn2_v': jnp.ones(2 * E), 'c3_w': f(ks[9], (E // 2, 2 * E, 1, 1), 0.05), 'c3_b': jnp.zeros(E // 2), 'se1_w': f(ks[10], (E // 4, E // 2), 0.1), 'se1_b': jnp.zeros(E // 4), 'se2_w': f(ks[11], (E // 2, E // 4), 0.1), 'se2_b': jnp.zeros(E // 2)}
        return inp
    _L1_conv_all = _L1_conv_setup()
    _L1_conv_in = {k: v for k, v in _L1_conv_all.items() if k in ('in_proj_w', 'conv_w', 'conv_b', 'x_proj_w', 'dt_proj_w', 'dt_proj_b', 'A_log', 'Ds', 'ln_g', 'ln_b', 'c1_w', 'c1_b', 'bn1_g', 'bn1_b', 'bn1_m', 'bn1_v', 'c2_w', 'c2_b', 'bn2_g', 'bn2_b', 'bn2_m', 'bn2_v', 'c3_w', 'c3_b', 'se1_w', 'se1_b', 'se2_w', 'se2_b', )}
    del _L1_conv_all

    return {
        "x": x,
        "L0_conv_w1": _L0_conv_in["w1"],
        "L0_conv_b1": _L0_conv_in["b1"],
        "L0_conv_w2": _L0_conv_in["w2"],
        "L0_conv_b2": _L0_conv_in["b2"],
        "L0_conv_ln_w": _L0_conv_in["ln_w"],
        "L0_conv_ln_b": _L0_conv_in["ln_b"],
        "L1_conv_in_proj_w": _L1_conv_in["in_proj_w"],
        "L1_conv_conv_w": _L1_conv_in["conv_w"],
        "L1_conv_conv_b": _L1_conv_in["conv_b"],
        "L1_conv_x_proj_w": _L1_conv_in["x_proj_w"],
        "L1_conv_dt_proj_w": _L1_conv_in["dt_proj_w"],
        "L1_conv_dt_proj_b": _L1_conv_in["dt_proj_b"],
        "L1_conv_A_log": _L1_conv_in["A_log"],
        "L1_conv_Ds": _L1_conv_in["Ds"],
        "L1_conv_ln_g": _L1_conv_in["ln_g"],
        "L1_conv_ln_b": _L1_conv_in["ln_b"],
        "L1_conv_c1_w": _L1_conv_in["c1_w"],
        "L1_conv_c1_b": _L1_conv_in["c1_b"],
        "L1_conv_bn1_g": _L1_conv_in["bn1_g"],
        "L1_conv_bn1_b": _L1_conv_in["bn1_b"],
        "L1_conv_bn1_m": _L1_conv_in["bn1_m"],
        "L1_conv_bn1_v": _L1_conv_in["bn1_v"],
        "L1_conv_c2_w": _L1_conv_in["c2_w"],
        "L1_conv_c2_b": _L1_conv_in["c2_b"],
        "L1_conv_bn2_g": _L1_conv_in["bn2_g"],
        "L1_conv_bn2_b": _L1_conv_in["bn2_b"],
        "L1_conv_bn2_m": _L1_conv_in["bn2_m"],
        "L1_conv_bn2_v": _L1_conv_in["bn2_v"],
        "L1_conv_c3_w": _L1_conv_in["c3_w"],
        "L1_conv_c3_b": _L1_conv_in["c3_b"],
        "L1_conv_se1_w": _L1_conv_in["se1_w"],
        "L1_conv_se1_b": _L1_conv_in["se1_b"],
        "L1_conv_se2_w": _L1_conv_in["se2_w"],
        "L1_conv_se2_b": _L1_conv_in["se2_b"],
    }

def reference(x, L0_conv_w1, L0_conv_b1, L0_conv_w2, L0_conv_b2, L0_conv_ln_w, L0_conv_ln_b, L1_conv_in_proj_w, L1_conv_conv_w, L1_conv_conv_b, L1_conv_x_proj_w, L1_conv_dt_proj_w, L1_conv_dt_proj_b, L1_conv_A_log, L1_conv_Ds, L1_conv_ln_g, L1_conv_ln_b, L1_conv_c1_w, L1_conv_c1_b, L1_conv_bn1_g, L1_conv_bn1_b, L1_conv_bn1_m, L1_conv_bn1_v, L1_conv_c2_w, L1_conv_c2_b, L1_conv_bn2_g, L1_conv_bn2_b, L1_conv_bn2_m, L1_conv_bn2_v, L1_conv_c3_w, L1_conv_c3_b, L1_conv_se1_w, L1_conv_se1_b, L1_conv_se2_w, L1_conv_se2_b):
    import jax
    import jax.numpy as jnp
    def _L0_conv_ref(x, w1, b1, w2, b2, ln_w, ln_b):
        import jax, jax.numpy as jnp
        import numpy as np
        K = 8
        LOCAL_WINDOW_RATIO = 0.25
        NEG = -1000000000.0
        LN_EPS = 1e-05
        NORM_EPS = 1e-12

        def _window_indices(H, W):
            lws = max(3, int(min(H, W) * LOCAL_WINDOW_RATIO))
            if lws % 2 == 0:
                lws += 1
            half = lws // 2
            off = jnp.arange(-half, half + 1)
            dy, dx = jnp.meshgrid(off, off, indexing='ij')
            dy = dy.reshape(-1)
            dx = dx.reshape(-1)
            py, px = jnp.meshgrid(jnp.arange(H), jnp.arange(W), indexing='ij')
            py = py.reshape(-1)
            px = px.reshape(-1)
            ny = py[:, None] + dy[None, :]
            nx = px[:, None] + dx[None, :]
            valid = (ny >= 0) & (ny < H) & (nx >= 0) & (nx < W)
            idx = jnp.clip(ny, 0, H - 1) * W + jnp.clip(nx, 0, W - 1)
            return (idx, valid)
        B, C, H, W = x.shape
        HW = H * W
        idx_w, valid = _window_indices(H, W)
        x_flat = x.transpose(0, 2, 3, 1).reshape(B, HW, C)
        n = jnp.linalg.norm(x_flat, axis=-1, keepdims=True)
        x_n = x_flat / jnp.maximum(n, NORM_EPS)
        win_n = x_n[:, idx_w, :]
        sims = jnp.einsum('bpc,bpwc->bpw', x_n, win_n)
        sims = jnp.where(valid[None], sims, NEG)
        top_sim, top_idx = jax.lax.top_k(sims, K)
        wts = jax.nn.softmax(top_sim, axis=-1)
        idx_g = jnp.take_along_axis(jnp.broadcast_to(idx_w[None], sims.shape), top_idx, axis=-1)
        feats = x_flat[jnp.arange(B)[:, None, None], idx_g]
        agg = jnp.einsum('bpk,bpkc->bpc', wts, feats)
        mu = jnp.mean(x_flat, axis=-1, keepdims=True)
        var = jnp.var(x_flat, axis=-1, keepdims=True)
        x_ln = (x_flat - mu) / jnp.sqrt(var + LN_EPS) * ln_w + ln_b
        enhanced = agg + x_ln
        h = jax.nn.relu(jnp.einsum('bpc,dc->bpd', enhanced, w1) + b1)
        ffn = jnp.einsum('bpd,cd->bpc', h, w2) + b2
        out = enhanced + ffn
        return out.reshape(B, H, W, C).transpose(0, 3, 1, 2)

    def _L1_conv_ref(x, in_proj_w, conv_w, conv_b, x_proj_w, dt_proj_w, dt_proj_b, A_log, Ds, ln_g, ln_b, c1_w, c1_b, bn1_g, bn1_b, bn1_m, bn1_v, c2_w, c2_b, bn2_g, bn2_b, bn2_m, bn2_v, c3_w, c3_b, se1_w, se1_b, se2_w, se2_b):
        import jax, jax.numpy as jnp
        import numpy as np
        B, DM, H, W = (2, 96, 48, 48)
        E = 192
        R, N = (6, 16)

        def conv2d(x, w, b, groups=1, pad=0):
            out = jax.lax.conv_general_dilated(x, w, window_strides=(1, 1), padding=[(pad, pad), (pad, pad)], dimension_numbers=('NCHW', 'OIHW', 'NCHW'), feature_group_count=groups)
            return out + b[None, :, None, None]
        Bs, _, Hs, Ws = x.shape
        L = Hs * Ws
        xz = jnp.einsum('bchw,oc->bohw', x, in_proj_w)
        xi, z = jnp.split(xz, 2, axis=1)
        xi = jax.nn.silu(conv2d(xi, conv_w, conv_b, groups=E, pad=1))
        xf = xi.reshape(Bs, E, L)
        xt = jnp.swapaxes(xi, 2, 3).reshape(Bs, E, L)
        xs = jnp.stack([xf, xf[..., ::-1], xt, xt[..., ::-1]], axis=1)
        dbc = jnp.einsum('bkcl,krc->bkrl', xs, x_proj_w)
        dlt, b, c = (dbc[:, :, :R], dbc[:, :, R:R + N], dbc[:, :, R + N:])
        dlt = jnp.einsum('bkrl,kdr->bkdl', dlt, dt_proj_w) + dt_proj_b[None, :, :, None]
        dlt = jax.nn.softplus(dlt)
        dA = dlt[..., None] * A_log[None, :, :, None, :]
        phi = jnp.exp(-jnp.cumsum(dA, axis=3))
        dbx = dlt[..., None] * jnp.swapaxes(b, 2, 3)[:, :, None] * xs[..., None]
        h = phi * jnp.cumsum(dbx / (phi + 1e-12), axis=3)
        y = jnp.einsum('bkdln,bknl->bkdl', h, c) + Ds[None, :, :, None]
        y1 = y[:, 0]
        y2 = y[:, 1, :, ::-1]
        y3 = jnp.swapaxes(y[:, 2].reshape(Bs, E, Ws, Hs), 2, 3).reshape(Bs, E, L)
        y4 = jnp.swapaxes(y[:, 3, :, ::-1].reshape(Bs, E, Ws, Hs), 2, 3).reshape(Bs, E, L)
        ys = (y1 + y2 + y3 + y4).reshape(Bs, E, Hs, Ws)
        yn = jnp.moveaxis(ys, 1, -1)
        mu = yn.mean(-1, keepdims=True)
        var = yn.var(-1, keepdims=True)
        yn = (yn - mu) / jnp.sqrt(var + 1e-05) * ln_g + ln_b
        u = jnp.moveaxis(yn, -1, 1) * z

        def bn(t, g, bb, m, v):
            return (t - m[None, :, None, None]) / jnp.sqrt(v + 1e-05)[None, :, None, None] * g[None, :, None, None] + bb[None, :, None, None]
        t = jax.nn.relu(bn(conv2d(u, c1_w, c1_b), bn1_g, bn1_b, bn1_m, bn1_v))
        t = jax.nn.relu(bn(conv2d(t, c2_w, c2_b, groups=2 * E, pad=1), bn2_g, bn2_b, bn2_m, bn2_v))
        t = conv2d(t, c3_w, c3_b)
        s = t.mean((2, 3))
        s = jax.nn.relu(s @ se1_w.T + se1_b)
        s = jax.nn.sigmoid(s @ se2_w.T + se2_b)
        return t + t * s[:, :, None, None]

    def _gn(v, G=32, eps=1e-5):
        B_, C_, H_, W_ = v.shape
        g = v.reshape(B_, G, C_ // G, H_, W_)
        m = jnp.mean(g, axis=(2, 3, 4), keepdims=True)
        s = jnp.var(g, axis=(2, 3, 4), keepdims=True)
        return ((g - m) / jnp.sqrt(s + eps)).reshape(v.shape)

    def _ln_c(v, eps=1e-6):
        m = jnp.mean(v, axis=1, keepdims=True)
        s = jnp.var(v, axis=1, keepdims=True)
        return (v - m) / jnp.sqrt(s + eps)

    def _ln_t(v, eps=1e-5):
        m = jnp.mean(v, axis=-1, keepdims=True)
        s = jnp.var(v, axis=-1, keepdims=True)
        return (v - m) / jnp.sqrt(s + eps)

    def _to_tokens(v):
        B_, C_, H_, W_ = v.shape
        return v.reshape(B_, C_, H_ * W_).transpose(0, 2, 1)
    def _from_tokens(t, like):
        B_, C_, H_, W_ = like.shape
        return t.transpose(0, 2, 1).reshape(B_, C_, H_, W_)

    x = x + _L0_conv_ref(_gn(x), L0_conv_w1, L0_conv_b1, L0_conv_w2, L0_conv_b2, L0_conv_ln_w, L0_conv_ln_b)
    x = x + _L1_conv_ref(_gn(x), L1_conv_in_proj_w, L1_conv_conv_w, L1_conv_conv_b, L1_conv_x_proj_w, L1_conv_dt_proj_w, L1_conv_dt_proj_b, L1_conv_A_log, L1_conv_Ds, L1_conv_ln_g, L1_conv_ln_b, L1_conv_c1_w, L1_conv_c1_b, L1_conv_bn1_g, L1_conv_bn1_b, L1_conv_bn1_m, L1_conv_bn1_v, L1_conv_c2_w, L1_conv_c2_b, L1_conv_bn2_g, L1_conv_bn2_b, L1_conv_bn2_m, L1_conv_bn2_v, L1_conv_c3_w, L1_conv_c3_b, L1_conv_se1_w, L1_conv_se1_b, L1_conv_se2_w, L1_conv_se2_b)
    return x


_drawn_inputs = setup_inputs


def setup_inputs(seed=0):
    import zlib

    import numpy as np

    out = dict(_drawn_inputs(seed))
    spreads = {'L0_conv_ln_w': (1.0, 0.2),
     'L0_conv_ln_b': (0.0, 0.1),
     'L1_conv_Ds': (1.0, 0.2),
     'L1_conv_ln_g': (1.0, 0.6),
     'L1_conv_ln_b': (0.0, 0.8),
     'L1_conv_c1_b': (0.0, 0.369),
     'L1_conv_bn1_g': (1.0, 0.6),
     'L1_conv_bn1_b': (0.0, 0.429),
     'L1_conv_bn1_m': (0.0, 0.338),
     'L1_conv_bn1_v': (1.0, 0.6),
     'L1_conv_c2_b': (0.0, 0.1),
     'L1_conv_bn2_g': (1.0, 0.6),
     'L1_conv_bn2_b': (0.0, 0.1),
     'L1_conv_bn2_m': (0.0, 0.1),
     'L1_conv_bn2_v': (1.0, 0.6),
     'L1_conv_c3_b': (0.0, 0.1),
     'L1_conv_se1_b': (0.0, 0.8),
     'L1_conv_se2_b': (0.0, 2.0)}
    factors = {'L0_conv_b1': 5.465,
     'L0_conv_b2': 2.829,
     'L1_conv_conv_w': 8.0,
     'L1_conv_conv_b': 8.0,
     'L1_conv_x_proj_w': 8.0,
     'L1_conv_dt_proj_w': 8.0,
     'L1_conv_dt_proj_b': 8.0,
     'L1_conv_A_log': 8.0,
     'L1_conv_se1_w': 8.0,
     'L1_conv_se2_w': 8.0}
    for name, (base, spread) in spreads.items():
        noise = np.random.default_rng([zlib.crc32(name.encode()), seed]).standard_normal(out[name].shape)
        drawn = base * np.exp(spread * noise) if base else spread * noise
        out[name] = jnp.asarray(drawn.astype(out[name].dtype))
    for name, factor in factors.items():
        out[name] = (out[name] * factor).astype(out[name].dtype)
    return out
```

```python
from contextlib import ExitStack

import concourse.bass as bass
from concourse import mybir

BATCH, C, H, W = 4, 96, 48, 48
L = H * W
E = 192
NSTATE = 16
RANK = 6
TOPK = 8
HALF_WIN = 6
ROWS = 8
CH = ROWS * W
NCH = L // CH
TQ_Y, TQ_X = 8, 16
KEY_Y, KEY_X = TQ_Y + 2 * HALF_WIN, TQ_X + 2 * HALF_WIN
KEYS = KEY_Y * KEY_X
KC = 4 * KEY_X
NKC = KEYS // KC
NT_Y, NT_X = H // TQ_Y, W // TQ_X
TILES = NT_Y * NT_X
PADW = W + 2
PADN = PADW * PADW
QS = 6
CUTS = [(0, 512), (512, 512), (1024, 512), (1536, 512), (2048, 256)]
NCUT = len(CUTS)
SLOT_B = [0, 1, 2, 0, 1]
SLOT_C = [2, 0, 1, 2, 1]
PER_TILE = 2 * NCUT
FREE_B = [-3, 0, -1, 1, 2]
FREE_C = [3, 4, 5, 6, 8]
RING_CREDIT = 4
LN_1E12 = 27.631021115928547
CUB_SCALE = 3 ** -0.5
LOG_MARGIN = 6e-8
NEG = -1e30
XR = 2 * RANK


def key_origin(i, j):
    return (min(max(TQ_Y * i - HALF_WIN, 0), H - KEY_Y), min(max(TQ_X * j - HALF_WIN, 0), W - KEY_X))


def kind(i, n):
    return 0 if i == 0 else (2 if i == n - 1 else 1)


PACK = [("ident", 128), ("gmean", C), ("mean96", C), ("sum96", C), ("mean192", 128),
        ("w1", 2 * C), ("w2", 2 * C), ("in_a", 128), ("in_b", 128), ("z_a", 128), ("z_b", 64),
        ("dtw", 3 * 128), ("b1", 2), ("b2", 1), ("ln0w", 1), ("ln0b", 1),
        ("convw", 18), ("convb", 2), ("dtb", QS), ("alog", QS * NSTATE), ("ds", 8),
        ("lng", 2), ("lnb", 2), ("c1b", 3), ("bn1g", 3), ("bn1b", 3), ("bn1m", 3), ("bn1v", 3),
        ("c2w", 27), ("c2b", 3), ("bn2g", 3), ("bn2b", 3), ("bn2m", 3), ("bn2v", 3),
        ("c3b", 1), ("se1b", 1), ("se2b", 1)]
BACK = [("c1a", 2 * E), ("c1bm", 2 * E), ("c3", 3 * C), ("se1", E // 4), ("se2", E // 2)]


def columns(table):
    at, out = 0, {}
    for name, width in table:
        out[name] = (at, width)
        at += width
    return out, at


PCOL, PWIDTH = columns(PACK)
BCOL, BWIDTH = columns(BACK)
XPM = 96 + XR
XPW = 3 * 4 * XPM


class Signal:

    def __init__(self, ctx, nc, name, per=1):
        self.sem = ctx.enter_context(nc.semaphore(name))
        self.per = per

    def at(self, b, k=None):
        return b * self.per + (self.per if k is None else k)


def build(nc, x, pack, back, xpw, masks, maskq, sels, out):
    f32, bf16 = mybir.dt.float32, mybir.dt.bfloat16
    ALU, ACT, AX = mybir.AluOpType, mybir.ActivationFunctionType, mybir.AxisListType

    with ExitStack() as ctx:
        def sb(name, shape, dt=f32):
            return ctx.enter_context(nc.sbuf_tensor(name, shape, dt))

        def sig(name, per=1):
            return Signal(ctx, nc, name, per)

        PK = sb("packed_weights", [128, PWIDTH])
        SEL = sb("state_selectors", [96, 3 * NSTATE * 128], bf16)
        MQ = sb("window_query_rows", [24, 128], bf16)
        X1 = sb("x_after_layer0", [C, L])
        XS = [sb(f"scan_input_{g}", [128, L]) for g in range(3)]
        PBC = sb("b_c_split_rows", [96, 4, L], bf16)
        RD = sb("dt_rows", [32 + XR, L])
        U = sb("work", [128, 11 * L])
        TW = sb("softplus_w", [128, L])
        TL = sb("softplus_l", [128, L])
        SM = sb("small", [128, 160])
        NA = sb("neg_a", [128, QS * NSTATE])
        PS = ctx.enter_context(nc.psum_tensor("psum", [128, 8, 512], f32))

        def w(name, rows=128, lo=0, n=None):
            at, width = PCOL[name]
            return PK[0:rows, at + lo:at + lo + (width - lo if n is None else n)]

        def wb(name, rows=128, lo=0, n=None):
            at, width = BCOL[name]
            return TW[0:rows, at + lo:at + lo + (width - lo if n is None else n)]

        def u(at, width=L, rows=128):
            return U[0:rows, at:at + width]

        def chunked(ap):
            return ap.rearrange("p (a b) -> p a b", b=CH)

        def image(ap):
            return ap.rearrange("p (h w) -> p h w", w=W)

        def ps6(rows, lo=0):
            return PS[lo:lo + rows, 0:NCH, 0:CH]

        def ps_rows(rows, lo=0):
            return ps6(rows, lo).rearrange("p a (r w) -> p a r w", w=W)

        def interior(pad):
            v = pad.rearrange("p (h w) -> p h w", w=PADW)[:, 1:1 + H, 1:1 + W]
            return v.rearrange("p (a r) w -> p a r w", r=ROWS)

        def one(name, rows=C, at=0):
            return w(name, rows, at, 1)

        def small(k, rows=C, n=1):
            return SM[0:rows, k:k + n]

        BN_STATS = 0
        MV, VC, DM, MG, STD, RSTD = 36, 38, 39, 40, 42, 44
        T_M8, T_NM, T_E8, T_Z, T_RZ = 46, 62, 64, 80, 82
        S1, B1C, S2, B2C, DSUM = 84, 87, 90, 93, 96
        TSUM, TMEAN, SE1, SE2, LNC = 98, 99, 100, 101, 102
        CT = 104
        EPS5, ONE, CUBB, CUBC = 120, 121, 122, 123

        XG, XN, XL, SQ, NR, DD = (k * L for k in range(6))
        HID = [3 * L, 4 * L]
        at = 6 * L
        tile_at = {}
        for name, width in [("query", 128), ("keys", KEYS), ("rest", KEYS), ("exp", KEYS), ("wts", KEYS),
                            ("keysT", NKC * C), ("wtsT", NKC * 128), ("diag", 128)]:
            tile_at[name] = (at, width)
            at += 2 * width
        assert at <= 11 * L

        def tb(name, t, rows=128):
            a, width = tile_at[name]
            return u(a + (t % 2) * width, width, rows)

        MK = PBC[0:24, 0:3, :].rearrange("p a n -> p (a n)")[:, 0:9 * KEYS]
        X0 = XS[0][0:C, :]

        FG = 0
        PAD = [L, L + PADN]
        FDIAG = L + 2 * PADN
        R1 = FDIAG + 18 * 128
        T2 = R1 + L
        XP = T2 + L // 2
        assert XP + XPW <= 11 * L
        mid = u(T2, L // 2, 96).bitcast(bf16)

        G = [k * L for k in range(4)]
        A = [4 * L, 5 * L]
        DL = [6 * L, 7 * L]
        CS = [8 * L, 9 * L]
        UX = 10 * L

        YA, YB, SA, SBQ, SD = (k * L for k in range(5))
        PAD2 = [5 * L + k * PADN for k in range(3)]
        ZG = PAD2[2] + PADN
        BDIAG = ZG + L
        assert BDIAG + 27 * 128 <= 11 * L
        MIX = [0, L, 2 * L]
        T3, OUT = 3 * L, 4 * L

        loaded = sig("weights_loaded")
        ready = sig("constants_ready")
        batch_free = sig("image_done")
        x_in, mask_in, xpw_in, back_in, stored = (sig(n) for n in
                                                  ("x_in", "masks_in", "xpw_in", "back_weights_in", "stored"))
        gn_stat, gn_mv, gn_mean, gn_mg, gn_dev, gn_vc, gn_var, gn_std, gn_rstd, xg_ready = (
            sig(n, p) for n, p in (("gn_stats", 2 * NCH), ("gn_channel", 2), ("gn_mean", 2), ("gn_mean_sb", 2),
                                   ("gn_dev", 2), ("gn_second", 2), ("gn_var", 2), ("gn_std", 2),
                                   ("gn_rstd", 2), ("gn_out", 2)))
        sq_ready, ssq_ready, nrm_ready, nrm_max, nrm_inv, xn_ready = (sig(n) for n in (
            "squares", "norm2_psum", "norm", "norm_max", "norm_inv", "unit_vectors"))
        mu_ready, dev_ready, dsq_ready, lvar_ready, lstd_ready, linv, lnorm, xl_ready = (sig(n) for n in (
            "ln0_mean", "ln0_dev", "ln0_dev2", "ln0_var", "ln0_std", "ln0_inv", "ln0_unit", "ln0_out"))
        q_ready, k_ready, s_ready, kt_psum, kt_sb, m8_ready, rest_ready, nm_ready, z_ready, exp_ready, exp2_ready, \
            wts_ready, rz_ready, diag_ready, wt_psum, wt_sb, agg_psum, enh_ready = (
                sig(n, TILES) for n in ("queries_copied", "keys_copied", "sims_psum", "keysT_psum", "keysT_sb",
                                        "top8", "rest_of_sims", "neg_max", "exp_sum", "exp_all", "exp_rest",
                                        "weights", "sum_inv", "diag_ready", "weightsT_psum", "weightsT_sb",
                                        "agg_psum", "enhanced"))
        hid_psum, hid_ready, ffn_psum, x1_part, x1_ready = (sig(n, p) for n, p in (
            ("hidden_psum", 2), ("hidden", 2), ("ffn_psum", 1), ("x1_partial", 1), ("x1", 1)))
        pad_zero, fdiag, xi_psum, xi_pad, conv_psum, xs_ready = (sig(n, p) for n, p in (
            ("pads_zero", 1), ("conv_diag", 1), ("xi_psum", 2), ("xi_padded", 2), ("conv_psum", 2),
            ("scan_inputs", 4)))
        xp_psum, hi_ready, r1_ready, mid_ready, mid_moved, lo_ready, rd_ready = (sig(n, p) for n, p in (
            ("x_proj_psum", 4), ("split_hi", 4), ("split_rest", 4), ("split_mid", 4), ("split_mid_moved", 4),
            ("split_lo", 4), ("dt_rows_ready", 2)))
        dt_psum, dt_sb, sp_abs, sp_exp, sp_square, sp_ln, sp_quad, sp_cubic, sp_log1p, dlt_ready, cs_ready, \
            ux_ready = (sig(n, p) for n, p in (
                ("dt_psum", QS * NCUT), ("dt_raw", QS * NCUT), ("softplus_abs", QS), ("softplus_exp", QS),
                ("softplus_square", QS), ("softplus_ln", QS), ("softplus_quadratic", QS), ("softplus_cubic", QS),
                ("softplus_log1p", QS), ("dlt", QS), ("dlt_cumsum", QS), ("dlt_x", QS)))
        NT = QS * NSTATE
        a_ready, g_ready, gu_ready, scanned, z_used = (sig(n, NT) for n in (
            "decay", "guard", "guard_dlt_x", "scanned", "y_tile_added"))
        ring_full, ring_used = (sig(n, NT * PER_TILE) for n in ("bc_chunk_in_psum", "bc_chunk_used"))
        y_sb = sig("y_group_out", 3)
        ys_psum, ys_sb, ymu_psum, yd_ready, ysq_ready, yvar_psum, ystd, yinv, yunit, yn_ready = (
            sig(n, p) for n, p in (("ys_psum", 2), ("ys", 2), ("y_mean", 1), ("y_dev", 2), ("y_dev2", 2),
                                   ("y_var", 1), ("y_std", 1), ("y_inv", 1), ("y_unit", 2), ("y_norm", 2)))
        zg_ready, z_psum, u_ready, pad2_zero, bdiag, c1_psum, c1_pad, c2_psum, mix_ready, c3_psum, t3_ready = (
            sig(n, p) for n, p in (("z_input", 1), ("z_psum", 2), ("gated", 2), ("pads2_zero", 1),
                                   ("conv2_diag", 1), ("c1_psum", 3), ("c1_padded", 3), ("c2_psum", 3),
                                   ("c2_out", 3), ("c3_psum", 1), ("c3_out", 1)))
        tmean, se1_psum, se1_ready, se2_psum, se2_ready, se_plus, out_ready = (sig(n) for n in (
            "t_mean", "se1_psum", "se1_out", "se2_psum", "se2_out", "se_factor", "out_ready"))
        settled = {e.engine: sig(f"settled_{k}") for k, e in
                   enumerate((nc.sync, nc.gpsimd, nc.scalar, nc.vector))}
        setup_v, setup_a = sig("setup_vector"), sig("setup_scalar")

        LOADS = 3 * 16
        CONSTS = 2

        def alone(eng, *waits):
            for signal, count in waits:
                eng.wait_ge(signal.sem, count)
            eng.sem_inc(settled[eng.engine].sem, 1)

        block = ctx.enter_context(nc.Block())

        @block.sync
        def _(sp):
            sp.dma_start(PK[:, :], pack).then_inc(loaded.sem, 16)
            sp.dma_start(SEL[:, :], sels).then_inc(loaded.sem, 16)
            sp.dma_start(MQ[:, :], maskq).then_inc(loaded.sem, 16)
            with sp.Fori(0, BATCH) as b:
                alone(sp, (batch_free, batch_free.at(b)))
                sp.dma_start(X0, x[bass.ds(b * C, C), :]).then_inc(x_in.sem, 16)
                sp.dma_start(MK, masks).then_inc(mask_in.sem, 16)
                sp.wait_ge(x1_ready.sem, x1_ready.at(b))
                sp.dma_start(u(XP, XPW), xpw).then_inc(xpw_in.sem, 16)
                sp.wait_ge(y_sb.sem, y_sb.at(b))
                sp.dma_start(TW[:, 0:BWIDTH], back).then_inc(back_in.sem, 16)
                alone(sp, (out_ready, out_ready.at(b)))
                sp.dma_start(out[bass.ds(b * C, C), :], u(OUT, L, C)).then_inc(stored.sem, 16)
                sp.wait_ge(stored.sem, b * 16 + 16)
                sp.sem_inc(batch_free.sem, 1)
            sp.wait_ge(stored.sem, 16 * BATCH)

        @block.gpsimd
        def _(pool):
            pool.sem_inc(batch_free.sem, 1)
            pool.sem_inc(ring_used.sem, RING_CREDIT)
            pool.sem_inc(scanned.sem, 2)
            pool.sem_inc(z_used.sem, 4)
            pool.sem_inc(ready.sem, 1)
            with pool.Fori(0, BATCH) as b:
                xn_img, xg_img = image(u(XN, L, C)), image(u(XG, L, C))

                def copies(t):
                    i, j = divmod(t, NT_X)
                    ky, kx = key_origin(i, j)
                    alone(pool, *([(kt_psum, kt_psum.at(b, t - 1))] if t >= 2 else []))
                    nc.gpsimd.tensor_copy(tb("query", t, C).rearrange("p (h w) -> p h w", w=TQ_X),
                                          xn_img[:, TQ_Y * i:TQ_Y * (i + 1), TQ_X * j:TQ_X * (j + 1)])\
                        .then_inc(q_ready.sem, 1)
                    nc.gpsimd.tensor_copy(tb("keys", t, C).rearrange("p (h w) -> p h w", w=KEY_X),
                                          xg_img[:, ky:ky + KEY_Y, kx:kx + KEY_X]).then_inc(k_ready.sem, 1)

                pool.wait_ge(xn_ready.sem, xn_ready.at(b))
                copies(0)
                for t in range(TILES):
                    if t + 1 < TILES:
                        copies(t + 1)
                    pool.wait_ge(exp2_ready.sem, exp2_ready.at(b, t + 1))
                    nc.gpsimd.tensor_tensor(tb("wts", t), tb("exp", t), tb("wts", t), ALU.subtract)\
                        .then_inc(wts_ready.sem, 1)
                alone(pool, (x1_ready, x1_ready.at(b)))
                nc.gpsimd.memset(u(PAD[0], 2 * PADN), 0.0).then_inc(pad_zero.sem, 1)
                for k in range(4):
                    alone(pool, (mid_ready, mid_ready.at(b, k + 1)))
                    nc.gpsimd.tensor_copy(PBC[32:64, k, :], mid[32:64, :]).then_inc(mid_moved.sem, 1)

                def cubic(q):
                    pool.wait_ge(sp_quad.sem, sp_quad.at(b, q + 1))
                    nc.gpsimd.tensor_tensor(TW[:, :], TW[:, :], u(CS[q % 2]), ALU.mult).then_inc(sp_cubic.sem, 1)

                def guard_times_ux(q, m):
                    for e in range(4):
                        n = m * 4 + e
                        pool.wait_ge(g_ready.sem, g_ready.at(b, q * NSTATE + n + 1))
                        nc.gpsimd.tensor_tensor(u(G[e]), u(G[e]), u(UX), ALU.mult).then_inc(gu_ready.sem, 1)

                cubic(0)
                for q in range(QS):
                    pool.wait_ge(dlt_ready.sem, dlt_ready.at(b, q + 1))
                    if q >= 1:
                        pool.wait_ge(gu_ready.sem, gu_ready.at(b, q * NSTATE))
                    nc.gpsimd.tensor_tensor(u(UX), u(DL[q % 2]), XS[q // 2][:, :], ALU.mult)\
                        .then_inc(ux_ready.sem, 1)
                    pool.wait_ge(ux_ready.sem, ux_ready.at(b, q + 1))
                    guard_times_ux(q, 0)
                    if q + 1 < QS:
                        cubic(q + 1)
                    with pool.Fori(1, 4) as m:
                        guard_times_ux(q, m)
                alone(pool, (ys_psum, ys_psum.at(b, 1)))
                nc.gpsimd.memset(u(PAD2[0], 3 * PADN), 0.0).then_inc(pad2_zero.sem, 1)

        @block.scalar
        def _(act):
            f = nc.scalar.activation
            act.wait_ge(loaded.sem, LOADS)
            act.wait_ge(setup_v.sem, 1)
            f(small(CT, 128, 3), w("bn1v"), ACT.Sqrt, bias=small(EPS5, 128)).then_inc(setup_a.sem, 1)
            f(small(CT + 3, 128, 3), w("bn2v"), ACT.Sqrt, bias=small(EPS5, 128)).then_inc(setup_a.sem, 1)
            f(NA[:, :], w("alog"), ACT.Copy, scale=-1.0).then_inc(setup_a.sem, 1)
            act.wait_ge(ready.sem, CONSTS)
            act.wait_ge(setup_a.sem, 3)

            with act.Fori(0, BATCH) as b:
                def group_norm(l):
                    act.wait_ge(gn_var.sem, gn_var.at(b, l + 1))
                    f(small(STD), PS[0:C, 7, 1:2], ACT.Sqrt, bias=small(EPS5)).then_inc(gn_std.sem, 1)

                group_norm(0)
                act.wait_ge(xg_ready.sem, xg_ready.at(b, 1))
                f(u(SQ, L, C), u(XG, L, C), ACT.Square).then_inc(sq_ready.sem, 1)
                act.wait_ge(ssq_ready.sem, ssq_ready.at(b))
                f(chunked(u(NR, L, C)), ps6(C), ACT.Sqrt).then_inc(nrm_ready.sem, 1)
                act.wait_ge(dev_ready.sem, dev_ready.at(b))
                f(u(SQ, L, C), u(DD, L, C), ACT.Square).then_inc(dsq_ready.sem, 1)
                act.wait_ge(lvar_ready.sem, lvar_ready.at(b))
                f(chunked(u(NR, L, C)), ps6(C), ACT.Sqrt, bias=small(EPS5)).then_inc(lstd_ready.sem, 1)

                for t in range(TILES):
                    p = t % 2
                    m8, nm = small(T_M8 + 8 * p, 128, 8), small(T_NM + p, 128)
                    act.wait_ge(m8_ready.sem, m8_ready.at(b, t + 1))
                    f(nm, m8[:, 0:1], ACT.Copy, scale=-1.0).then_inc(nm_ready.sem, 1)
                    act.wait_ge(nm_ready.sem, nm_ready.at(b, t + 1))
                    if t >= 2:
                        act.wait_ge(rz_ready.sem, rz_ready.at(b, t - 1))
                    f(small(T_E8 + 8 * p, 128, 8), m8, ACT.Exp, bias=nm,
                      accum_out=small(T_Z + p, 128)).then_inc(z_ready.sem, 1)
                    act.wait_ge(rest_ready.sem, rest_ready.at(b, t + 1))
                    if t >= 2:
                        act.wait_ge(wts_ready.sem, wts_ready.at(b, t - 1))
                    f(tb("exp", t).rearrange("p (a n) -> p a n", a=2), PS[:, 2 * p:2 * p + 2, 0:KEYS // 2],
                      ACT.Exp, bias=nm).then_inc(exp_ready.sem, 1)
                    if t >= 2:
                        act.wait_ge(wt_psum.sem, wt_psum.at(b, t - 1))
                    f(tb("wts", t), tb("rest", t), ACT.Exp, bias=nm).then_inc(exp2_ready.sem, 1)
                    act.wait_ge(kt_psum.sem, kt_psum.at(b, t + 1))
                    if t >= 2:
                        act.wait_ge(agg_psum.sem, agg_psum.at(b, t - 1))
                    f(tb("keysT", t, KC), PS[0:KC, 6, 0:NKC * C], ACT.Copy).then_inc(kt_sb.sem, 1)

                for k in range(2):
                    act.wait_ge(hid_psum.sem, hid_psum.at(b, k + 1))
                    f(chunked(u(HID[k], L, C)), ps6(C), ACT.Relu, bias=one("b1", C, k)).then_inc(hid_ready.sem, 1)

                group_norm(1)
                act.wait_ge(pad_zero.sem, pad_zero.at(b))
                for k in range(2):
                    act.wait_ge(xi_psum.sem, xi_psum.at(b, k + 1))
                    f(interior(u(PAD[k], PADN)), ps_rows(128), ACT.Copy).then_inc(xi_pad.sem, 1)
                act.wait_ge(conv_psum.sem, conv_psum.at(b, 1))
                f(chunked(XS[0][:, :]), ps6(128), ACT.Silu, bias=one("convb", 128, 0)).then_inc(xs_ready.sem, 1)
                f(XS[1][:, :].rearrange("p (w a r) -> p a r w", a=NCH, r=ROWS), ps_rows(128), ACT.Silu,
                  bias=one("convb", 128, 0)).then_inc(xs_ready.sem, 1)
                act.wait_ge(conv_psum.sem, conv_psum.at(b, 2))
                f(chunked(XS[2][0:64, :]), ps6(64), ACT.Silu, bias=one("convb", 64, 1)).then_inc(xs_ready.sem, 1)
                f(XS[2][64:128, :].rearrange("p (w a r) -> p a r w", a=NCH, r=ROWS), ps_rows(64, 64), ACT.Silu,
                  bias=PK[64:128, PCOL["convb"][0] + 1:PCOL["convb"][0] + 2]).then_inc(xs_ready.sem, 1)
                for k in range(4):
                    act.wait_ge(xp_psum.sem, xp_psum.at(b, k + 1))
                    f(chunked(PBC[:, k, :]), ps6(96), ACT.Copy).then_inc(hi_ready.sem, 1)
                    if k % 2 == 0:
                        s = k // 2
                        f(chunked(RD[32 * s:32 * s + XR, :]), ps6(XR, 96), ACT.Copy).then_inc(rd_ready.sem, 1)
                    act.wait_ge(r1_ready.sem, r1_ready.at(b, k + 1))
                    if k >= 1:
                        act.wait_ge(mid_moved.sem, mid_moved.at(b, k))
                        act.wait_ge(lo_ready.sem, lo_ready.at(b, k))
                    f(mid, u(R1, L, 96), ACT.Copy).then_inc(mid_ready.sem, 1)

                def softplus(q):
                    p = q % 2
                    for j, (c0, cw) in enumerate(CUTS):
                        act.wait_ge(dt_psum.sem, dt_psum.at(b, q * NCUT + j + 1))
                        f(U[:, DL[p] + c0:DL[p] + c0 + cw], PS[:, 5 + SLOT_B[j], 0:cw], ACT.Identity,
                          bias=one("dtb", 128, q)).then_inc(dt_sb.sem, 1)
                    act.wait_ge(dt_sb.sem, dt_sb.at(b, (q + 1) * NCUT))
                    if q >= 2:
                        act.wait_ge(cs_ready.sem, cs_ready.at(b, q - 1))
                    f(u(CS[p]), u(DL[p]), ACT.Abs).then_inc(sp_abs.sem, 1)
                    act.wait_ge(sp_abs.sem, sp_abs.at(b, q + 1))
                    f(u(CS[p]), u(CS[p]), ACT.Exp, scale=-1.0).then_inc(sp_exp.sem, 1)
                    act.wait_ge(sp_exp.sem, sp_exp.at(b, q + 1))
                    if q >= 1:
                        act.wait_ge(dlt_ready.sem, dlt_ready.at(b, q))
                    f(TW[:, :], u(CS[p]), ACT.Square, bias=small(CUBB, 128), scale=CUB_SCALE)\
                        .then_inc(sp_square.sem, 1)
                    f(TL[:, :], u(CS[p]), ACT.Ln, bias=small(ONE, 128)).then_inc(sp_ln.sem, 1)
                    act.wait_ge(sp_square.sem, sp_square.at(b, q + 1))
                    f(TW[:, :], TW[:, :], ACT.Identity, bias=small(CUBC, 128)).then_inc(sp_quad.sem, 1)

                act.wait_ge(lo_ready.sem, lo_ready.at(b))
                softplus(0)
                for q in range(QS):
                    if q + 1 < QS:
                        softplus(q + 1)
                    act.wait_ge(dlt_ready.sem, dlt_ready.at(b, q + 1))
                    act.wait_ge(cs_ready.sem, cs_ready.at(b, q + 1))
                    with act.Fori(0, 4) as m:
                        for e in range(4):
                            n = m * 4 + e
                            t = b * NT + q * NSTATE + n
                            col = NA[:, bass.ds(q * NSTATE + n, 1)]

                            def decay():
                                alone(act, (scanned, t + 1))
                                f(u(A[e % 2]), u(DL[q % 2]), ACT.Exp, scale=col).then_inc(a_ready.sem, 1)

                            def guard():
                                alone(act, (z_used, t + 1))
                                f(u(G[e]), u(CS[q % 2]), ACT.Sigmoid, scale=col,
                                  bias=small(LNC, 128)).then_inc(g_ready.sem, 1)

                            for part in ((guard, decay) if e % 2 == 0 else (decay, guard)):
                                part()

                act.wait_ge(y_sb.sem, y_sb.at(b))
                act.wait_ge(ys_psum.sem, ys_psum.at(b, 1))
                f(chunked(u(YA)), ps6(128), ACT.Identity, bias=small(DSUM, 128)).then_inc(ys_sb.sem, 1)
                act.wait_ge(ys_psum.sem, ys_psum.at(b, 2))
                f(chunked(u(YB, L, 64)), ps6(64), ACT.Identity, bias=small(DSUM + 1, 64)).then_inc(ys_sb.sem, 1)
                act.wait_ge(yd_ready.sem, yd_ready.at(b, 1))
                f(u(SA), u(YA), ACT.Square).then_inc(ysq_ready.sem, 1)
                act.wait_ge(yd_ready.sem, yd_ready.at(b, 2))
                f(u(SBQ, L, 64), u(YB, L, 64), ACT.Square).then_inc(ysq_ready.sem, 1)
                act.wait_ge(yvar_psum.sem, yvar_psum.at(b))
                f(chunked(u(SD)), ps6(128), ACT.Sqrt, bias=small(EPS5, 128)).then_inc(ystd.sem, 1)
                act.wait_ge(pad2_zero.sem, pad2_zero.at(b))
                for k in range(3):
                    act.wait_ge(c1_psum.sem, c1_psum.at(b, k + 1))
                    f(interior(u(PAD2[k], PADN)), ps_rows(128), ACT.Relu, bias=small(B1C + k, 128),
                      scale=small(S1 + k, 128)).then_inc(c1_pad.sem, 1)
                for k in range(3):
                    act.wait_ge(c2_psum.sem, c2_psum.at(b, k + 1))
                    f(chunked(u(MIX[k])), ps6(128), ACT.Relu, bias=small(B2C + k, 128),
                      scale=small(S2 + k, 128)).then_inc(mix_ready.sem, 1)
                act.wait_ge(c3_psum.sem, c3_psum.at(b))
                f(chunked(u(T3, L, C)), ps6(C), ACT.Identity, bias=one("c3b"),
                  accum_out=small(TSUM)).then_inc(t3_ready.sem, 1)
                act.wait_ge(t3_ready.sem, t3_ready.at(b))
                f(small(TMEAN), small(TSUM), ACT.Copy, scale=1.0 / L).then_inc(tmean.sem, 1)
                act.wait_ge(se1_psum.sem, se1_psum.at(b))
                f(small(SE1, E // 4), PS[0:E // 4, 7, 2:3], ACT.Relu, bias=one("se1b", E // 4))\
                    .then_inc(se1_ready.sem, 1)
                act.wait_ge(se2_psum.sem, se2_psum.at(b))
                f(small(SE2), PS[0:C, 7, 3:4], ACT.Sigmoid, bias=one("se2b")).then_inc(se2_ready.sem, 1)

        @block.tensor
        def _(pe):
            mm = nc.tensor.matmul
            ident = w("ident")
            pe.wait_ge(loaded.sem, LOADS)
            pe.wait_ge(ready.sem, CONSTS)

            def plane(lhs_rhs, rows, done, lo=0):
                for c in range(NCH):
                    for k, (lhs, rhs) in enumerate(lhs_rhs):
                        last = mm(PS[lo:lo + rows, c, 0:CH], lhs, rhs(c), start=(k == 0),
                                  stop=(k == len(lhs_rhs) - 1))
                last.then_inc(done.sem, 1)

            def cut(ap):
                return lambda c: ap[:, c * CH:(c + 1) * CH]

            def turned(ap):
                v = ap.rearrange("p (w h) -> p h w", h=H)
                return lambda c: v[:, c * ROWS:(c + 1) * ROWS, :]

            def taps(pad, diag):
                v = pad.rearrange("p (h w) -> p h w", w=PADW)
                return [(diag[:, k * 128:(k + 1) * 128],
                         lambda c, k=k: v[:, c * ROWS + k // 3:c * ROWS + k // 3 + ROWS, k % 3:k % 3 + W])
                        for k in range(9)]

            with pe.Fori(0, BATCH) as b:
                def group_norm(l):
                    pe.wait_ge(gn_mv.sem, gn_mv.at(b, l + 1))
                    mm(PS[0:C, 7, 0:1], w("gmean", C), small(MV), start=True, stop=True).then_inc(gn_mean.sem, 1)
                    pe.wait_ge(gn_vc.sem, gn_vc.at(b, l + 1))
                    mm(PS[0:C, 7, 1:2], w("gmean", C), small(VC), start=True, stop=True).then_inc(gn_var.sem, 1)

                group_norm(0)
                pe.wait_ge(sq_ready.sem, sq_ready.at(b))
                plane([(w("sum96", C), cut(u(SQ, L, C)))], C, ssq_ready)
                pe.wait_ge(nrm_ready.sem, nrm_ready.at(b))
                plane([(w("mean96", C), cut(u(XG, L, C)))], C, mu_ready)
                pe.wait_ge(dsq_ready.sem, dsq_ready.at(b))
                plane([(w("mean96", C), cut(u(SQ, L, C)))], C, lvar_ready)

                xn_img = image(u(XN, L, C))
                pe.wait_ge(mask_in.sem, b * 16 + 16)
                pe.wait_ge(lstd_ready.sem, lstd_ready.at(b))
                for t in range(TILES + 1):
                    if t < TILES:
                        i, j = divmod(t, NT_X)
                        ky, kx = key_origin(i, j)
                        mask = (kind(i, NT_Y) * 3 + kind(j, NT_X)) * KEYS
                        pe.wait_ge(k_ready.sem, k_ready.at(b, t + 1))
                        if t >= 2:
                            pe.wait_ge(exp_ready.sem, exp_ready.at(b, t - 1))
                            pe.wait_ge(rest_ready.sem, rest_ready.at(b, t - 1))
                        for hf in range(2):
                            sims = PS[:, 2 * (t % 2) + hf, 0:KEYS // 2]
                            mm(sims, tb("query", t, C),
                               xn_img[:, ky + 10 * hf:ky + 10 * hf + 10, kx:kx + KEY_X], start=True, stop=False)
                            last = mm(sims, MQ[:, :], MK[:, mask + hf * KEYS // 2:mask + (hf + 1) * KEYS // 2],
                                      start=False, stop=True)
                        last.then_inc(s_ready.sem, 1)
                        if t >= 1:
                            pe.wait_ge(kt_sb.sem, kt_sb.at(b, t))
                        for k in range(NKC):
                            last = nc.tensor.transpose(PS[0:KC, 6, k * C:(k + 1) * C],
                                                       tb("keys", t, C)[:, k * KC:(k + 1) * KC],
                                                       w("ident", C, 0, C))
                        last.then_inc(kt_psum.sem, 1)
                    if t >= 1:
                        r = t - 1
                        pe.wait_ge(wts_ready.sem, wts_ready.at(b, r + 1))
                        pe.wait_ge(diag_ready.sem, diag_ready.at(b, r + 1))
                        if r >= 1:
                            pe.wait_ge(wt_sb.sem, wt_sb.at(b, r))
                        for k in range(NKC):
                            last = mm(PS[0:KC, 4 + k // 4, (k % 4) * 128:(k % 4) * 128 + 128],
                                      tb("wts", r)[:, k * KC:(k + 1) * KC], tb("diag", r), start=True, stop=True)
                        last.then_inc(wt_psum.sem, 1)
                        pe.wait_ge(wt_sb.sem, wt_sb.at(b, r + 1))
                        pe.wait_ge(kt_sb.sem, kt_sb.at(b, r + 1))
                        if r >= 1:
                            pe.wait_ge(enh_ready.sem, enh_ready.at(b, r))
                        for k in range(NKC):
                            last = mm(PS[0:C, 7, 0:128], tb("keysT", r, KC)[:, k * C:(k + 1) * C],
                                      tb("wtsT", r, KC)[:, k * 128:(k + 1) * 128], start=(k == 0),
                                      stop=(k == NKC - 1))
                        last.then_inc(agg_psum.sem, 1)

                pe.wait_ge(enh_ready.sem, enh_ready.at(b))
                for k in range(2):
                    if k:
                        pe.wait_ge(hid_ready.sem, hid_ready.at(b, 1))
                    plane([(w("w1", C, k * C, C), cut(u(XL, L, C)))], C, hid_psum)
                pe.wait_ge(hid_ready.sem, hid_ready.at(b, 2))
                plane([(w("w2", C, k * C, C), cut(u(HID[k], L, C))) for k in range(2)], C, ffn_psum)

                group_norm(1)
                pe.wait_ge(xg_ready.sem, xg_ready.at(b, 2))
                plane([(w("in_a", C), cut(u(FG, L, C)))], 128, xi_psum)
                pe.wait_ge(xi_pad.sem, xi_pad.at(b, 1))
                plane([(w("in_b", C), cut(u(FG, L, C)))], 128, xi_psum)
                pe.wait_ge(xi_pad.sem, xi_pad.at(b, 2))
                pe.wait_ge(fdiag.sem, fdiag.at(b))
                plane(taps(u(PAD[0], PADN), u(FDIAG, 9 * 128)), 128, conv_psum)
                pe.wait_ge(xs_ready.sem, xs_ready.at(b, 2))
                plane(taps(u(PAD[1], PADN), u(FDIAG + 9 * 128, 9 * 128)), 128, conv_psum)
                pe.wait_ge(xs_ready.sem, xs_ready.at(b, 4))
                pe.wait_ge(xpw_in.sem, b * 16 + 16)
                for k in range(4):
                    m = XPM if k % 2 == 0 else 96
                    if k >= 1:
                        pe.wait_ge(r1_ready.sem, r1_ready.at(b, k))
                        pe.wait_ge(rd_ready.sem, rd_ready.at(b, (k + 1) // 2))
                    plane([(u(XP + (g * 4 + k) * XPM, m), cut(XS[g][:, :])) for g in range(3)], m, xp_psum)

                y = [PS[:, j, 0:cw] for j, (_, cw) in enumerate(CUTS)]

                def dt_product(q):
                    g, s = divmod(q, 2)
                    for j, (c0, cw) in enumerate(CUTS):
                        if j >= 3:
                            pe.wait_ge(dt_sb.sem, dt_sb.at(b, q * NCUT + j - 2))
                        mm(PS[:, 5 + SLOT_B[j], 0:cw],
                           PK[32 * s:32 * s + XR, PCOL["dtw"][0] + g * 128:PCOL["dtw"][0] + (g + 1) * 128],
                           RD[32 * s:32 * s + XR, c0:c0 + cw], start=True, stop=True).then_inc(dt_psum.sem, 1)
                    pe.wait_ge(dt_sb.sem, dt_sb.at(b, (q + 1) * NCUT))

                def broadcast(q, n, t, which, j):
                    g, s = divmod(q, 2)
                    c0, cw = CUTS[j]
                    slot = (SLOT_C if which else SLOT_B)[j]
                    need = (FREE_C if which else FREE_B)[j]
                    pe.wait_ge(ring_used.sem, t * PER_TILE + (need + RING_CREDIT))
                    mm(PS[:, 5 + slot, 0:cw], SEL[:, bass.ds((g * NSTATE + n) * 128, 128)],
                       PBC[:, 2 * s + which, c0:c0 + cw], start=True, stop=True).then_inc(ring_full.sem, 1)

                def add_y(e, t, j, first, last):
                    c0, cw = CUTS[j]
                    pe.wait_ge(ring_used.sem, t * PER_TILE + (RING_CREDIT - NCUT + j + 1))
                    ins = mm(y[j], ident, U[:, G[e] + c0:G[e] + c0 + cw], start=first, stop=last,
                             skip_group_check=True)
                    if j == NCUT - 1:
                        ins.then_inc(z_used.sem, 1)

                def tile(q, n, e, before=None):
                    t = b * NT + q * NSTATE + n
                    steps = [("b", 0), ("b", 1), ("b", 2), ("y", 0), ("b", 3), ("y", 1), ("b", 4), ("y", 2),
                             ("c", 0), ("y", 3), ("c", 1), ("y", 4), ("c", 2), ("c", 3), ("c", 4)]
                    for what, j in steps:
                        if what != "y":
                            broadcast(q, n, t, int(what == "c"), j)
                        elif before is not None:
                            add_y((e - 1) % 4, t, j, *before)

                pe.wait_ge(rd_ready.sem, rd_ready.at(b))
                pe.wait_ge(lo_ready.sem, lo_ready.at(b))
                pe.wait_ge(mid_moved.sem, mid_moved.at(b))
                dt_product(0)
                for q in range(QS):
                    if q + 1 < QS:
                        if q >= 1:
                            pe.wait_ge(ring_used.sem, (b * NT + q * NSTATE) * PER_TILE + RING_CREDIT)
                        dt_product(q + 1)
                    for n in range(4):
                        if n == 0:
                            tile(q, 0, 0, None if q == 0 else (False, q % 2 == 0))
                        else:
                            if n == 1 and q % 2 == 0 and q:
                                pe.wait_ge(y_sb.sem, y_sb.at(b, q // 2))
                            tile(q, n, n, (n == 1 and q % 2 == 0, False))
                    with pe.Fori(1, 4) as m:
                        for e in range(4):
                            tile(q, m * 4 + e, e, (False, False))
                for j in range(NCUT):
                    add_y(3, (b + 1) * NT, j, False, True)

                pe.wait_ge(y_sb.sem, y_sb.at(b))
                plane([(ident, cut(XS[0][:, :])), (ident, turned(XS[1][:, :]))], 128, ys_psum)
                pe.wait_ge(ys_sb.sem, ys_sb.at(b, 1))
                plane([(ident[:, 0:64], cut(XS[2][:, :])), (ident[:, 64:128], turned(XS[2][:, :]))], 64, ys_psum)
                pe.wait_ge(ys_sb.sem, ys_sb.at(b, 2))
                plane([(w("mean192"), cut(u(YA))), (w("mean192", 64), cut(u(YB, L, 64)))], 128, ymu_psum)
                pe.wait_ge(yd_ready.sem, yd_ready.at(b))
                pe.wait_ge(ysq_ready.sem, ysq_ready.at(b))
                plane([(w("mean192"), cut(u(SA))), (w("mean192", 64), cut(u(SBQ, L, 64)))], 128, yvar_psum)
                pe.wait_ge(ystd.sem, ystd.at(b))
                pe.wait_ge(zg_ready.sem, zg_ready.at(b))
                plane([(w("z_a", C), cut(u(ZG, L, C)))], 128, z_psum)
                pe.wait_ge(u_ready.sem, u_ready.at(b, 1))
                plane([(w("z_b", C), cut(u(ZG, L, C)))], 64, z_psum)
                pe.wait_ge(u_ready.sem, u_ready.at(b, 2))
                pe.wait_ge(back_in.sem, b * 16 + 16)
                for k in range(3):
                    if k:
                        pe.wait_ge(c1_pad.sem, c1_pad.at(b, k))
                    plane([(wb("c1a", 128, k * 128, 128), cut(u(YA))),
                           (wb("c1bm", 64, k * 128, 128), cut(u(YB, L, 64)))], 128, c1_psum)
                pe.wait_ge(c1_pad.sem, c1_pad.at(b, 3))
                pe.wait_ge(bdiag.sem, bdiag.at(b))
                for k in range(3):
                    if k:
                        pe.wait_ge(mix_ready.sem, mix_ready.at(b, k))
                    plane(taps(u(PAD2[k], PADN), u(BDIAG + k * 9 * 128, 9 * 128)), 128, c2_psum)
                pe.wait_ge(mix_ready.sem, mix_ready.at(b, 3))
                plane([(wb("c3", 128, k * C, C), cut(u(MIX[k]))) for k in range(3)], C, c3_psum)
                pe.wait_ge(tmean.sem, tmean.at(b))
                mm(PS[0:E // 4, 7, 2:3], wb("se1", C), small(TMEAN), start=True, stop=True)\
                    .then_inc(se1_psum.sem, 1)
                pe.wait_ge(se1_ready.sem, se1_ready.at(b))
                mm(PS[0:C, 7, 3:4], wb("se2", E // 4), small(SE1, E // 4), start=True, stop=True)\
                    .then_inc(se2_psum.sem, 1)

        @block.vector
        def _(dve):
            v = nc.vector
            v.memset(small(EPS5, 128), 1e-5)
            v.memset(small(ONE, 128), 1.0)
            v.memset(small(CUBB, 128), -0.75 * CUB_SCALE)
            v.memset(small(CUBC, 128), 13 / 16)
            v.memset(small(LNC, 128), LN_1E12).then_inc(setup_v.sem, 1)
            dve.wait_ge(loaded.sem, LOADS)
            dve.wait_ge(setup_a.sem, 3)
            steps = 1
            for k, (cb, g, bb, m, sc, off) in enumerate((("c1b", "bn1g", "bn1b", "bn1m", S1, B1C),
                                                         ("c2b", "bn2g", "bn2b", "bn2m", S2, B2C))):
                inv, dif = small(CT + 6, 128, 3), small(CT + 9, 128, 3)
                v.reciprocal(inv, small(CT + 3 * k, 128, 3)).then_inc(setup_v.sem, 1)
                v.tensor_tensor(dif, w(cb), w(m), ALU.subtract).then_inc(setup_v.sem, 1)
                steps += 2
                dve.wait_ge(setup_v.sem, steps)
                v.tensor_tensor(small(sc, 128, 3), w(g), inv, ALU.mult).then_inc(setup_v.sem, 1)
                steps += 1
                dve.wait_ge(setup_v.sem, steps)
                v.tensor_tensor(dif, dif, small(sc, 128, 3), ALU.mult).then_inc(setup_v.sem, 1)
                steps += 1
                dve.wait_ge(setup_v.sem, steps)
                v.tensor_tensor(small(off, 128, 3), dif, w(bb), ALU.add).then_inc(setup_v.sem, 1)
                steps += 1
                dve.wait_ge(setup_v.sem, steps)
            v.tensor_reduce(small(DSUM, 128, 2), w("ds").rearrange("p (a k) -> p a k", k=4), AX.X, ALU.add)\
                .then_inc(ready.sem, 1)
            dve.wait_ge(ready.sem, CONSTS)

            with dve.Fori(0, BATCH) as b:
                def group_norm(l, src, dst):
                    stats = small(BN_STATS, C, 6 * NCH).rearrange("p (a k) -> p a k", k=6)
                    for c in range(NCH):
                        v.bn_stats(stats[:, c, :], src[:, c * CH:(c + 1) * CH]).then_inc(gn_stat.sem, 1)
                    alone(dve, (gn_stat, gn_stat.at(b, (l + 1) * NCH)))
                    v.bn_aggr(small(MV, C, 2), stats).then_inc(gn_mv.sem, 1)
                    dve.wait_ge(gn_mean.sem, gn_mean.at(b, l + 1))
                    v.tensor_copy(small(MG + l), PS[0:C, 7, 0:1]).then_inc(gn_mg.sem, 1)
                    dve.wait_ge(gn_mg.sem, gn_mg.at(b, l + 1))
                    v.tensor_tensor(small(DM), small(MV), small(MG + l), ALU.subtract).then_inc(gn_dev.sem, 1)
                    dve.wait_ge(gn_dev.sem, gn_dev.at(b, l + 1))
                    v.scalar_tensor_tensor(out=small(VC), in0=small(DM), scalar=small(DM), in1=small(MV + 1),
                                           op0=ALU.mult, op1=ALU.add).then_inc(gn_vc.sem, 1)
                    dve.wait_ge(gn_std.sem, gn_std.at(b, l + 1))
                    v.reciprocal(small(RSTD + l), small(STD)).then_inc(gn_rstd.sem, 1)
                    dve.wait_ge(gn_rstd.sem, gn_rstd.at(b, l + 1))
                    v.tensor_scalar(dst, src, small(MG + l), small(RSTD + l), ALU.subtract, ALU.mult)\
                        .then_inc(xg_ready.sem, 1)

                dve.wait_ge(x_in.sem, b * 16 + 16)
                group_norm(0, X0, u(XG, L, C))
                dve.wait_ge(nrm_ready.sem, nrm_ready.at(b))
                v.tensor_scalar(u(NR, L, C), u(NR, L, C), 1e-12, None, ALU.max).then_inc(nrm_max.sem, 1)
                dve.wait_ge(nrm_max.sem, nrm_max.at(b))
                v.reciprocal(u(NR, L, C), u(NR, L, C)).then_inc(nrm_inv.sem, 1)
                dve.wait_ge(nrm_inv.sem, nrm_inv.at(b))
                dve.wait_ge(xg_ready.sem, xg_ready.at(b, 1))
                v.tensor_tensor(u(XN, L, C), u(XG, L, C), u(NR, L, C), ALU.mult).then_inc(xn_ready.sem, 1)
                dve.wait_ge(mu_ready.sem, mu_ready.at(b))
                v.tensor_tensor(chunked(u(DD, L, C)), chunked(u(XG, L, C)), ps6(C), ALU.subtract)\
                    .then_inc(dev_ready.sem, 1)
                dve.wait_ge(lstd_ready.sem, lstd_ready.at(b))
                v.reciprocal(u(NR, L, C), u(NR, L, C)).then_inc(linv.sem, 1)
                dve.wait_ge(linv.sem, linv.at(b))
                v.tensor_tensor(u(XL, L, C), u(DD, L, C), u(NR, L, C), ALU.mult).then_inc(lnorm.sem, 1)
                dve.wait_ge(lnorm.sem, lnorm.at(b))
                v.tensor_scalar(u(XL, L, C), u(XL, L, C), one("ln0w"), one("ln0b"), ALU.mult, ALU.add)\
                    .then_inc(xl_ready.sem, 1)
                dve.wait_ge(xl_ready.sem, xl_ready.at(b))

                xl_img = image(u(XL, L, C))
                for t in range(TILES + 1):
                    if t < TILES:
                        p = t % 2
                        sims = PS[:, 2 * p:2 * p + 2, 0:KEYS // 2]
                        m8 = small(T_M8 + 8 * p, 128, 8)
                        alone(dve, (s_ready, s_ready.at(b, t + 1)), *([(z_ready, z_ready.at(b, t - 1))] if t >= 2 else []))
                        v.max(m8, sims).then_inc(m8_ready.sem, 1)
                        alone(dve, (m8_ready, m8_ready.at(b, t + 1)), *([(exp2_ready, exp2_ready.at(b, t - 1))] if t >= 2 else []))
                        v.match_replace(out=tb("rest", t).rearrange("p (a n) -> p a n", a=2), in_to_replace=m8,
                                        in_values=sims, imm_value=NEG).then_inc(rest_ready.sem, 1)
                    if t >= 1:
                        r = t - 1
                        p = r % 2
                        i, j = divmod(r, NT_X)
                        dve.wait_ge(z_ready.sem, z_ready.at(b, r + 1))
                        v.reciprocal(small(T_RZ + p, 128), small(T_Z + p, 128)).then_inc(rz_ready.sem, 1)
                        dve.wait_ge(rz_ready.sem, rz_ready.at(b, r + 1))
                        if r >= 2:
                            dve.wait_ge(wt_psum.sem, wt_psum.at(b, r - 1))
                        v.tensor_scalar(tb("diag", r), w("ident"), small(T_RZ + p, 128), None, ALU.mult)\
                            .then_inc(diag_ready.sem, 1)
                        dve.wait_ge(wt_psum.sem, wt_psum.at(b, r + 1))
                        if r >= 2:
                            dve.wait_ge(agg_psum.sem, agg_psum.at(b, r - 1))
                        v.tensor_copy(tb("wtsT", r, KC), PS[0:KC, 4:6, :].rearrange("p a n -> p (a n)")
                                      [:, 0:NKC * 128]).then_inc(wt_sb.sem, 1)
                        dve.wait_ge(agg_psum.sem, agg_psum.at(b, r + 1))
                        dst = xl_img[:, TQ_Y * i:TQ_Y * (i + 1), TQ_X * j:TQ_X * (j + 1)]
                        v.tensor_tensor(dst, dst, PS[0:C, 7, 0:128].rearrange("p (h w) -> p h w", w=TQ_X),
                                        ALU.add).then_inc(enh_ready.sem, 1)

                dve.wait_ge(enh_ready.sem, enh_ready.at(b))
                dve.wait_ge(ffn_psum.sem, ffn_psum.at(b))
                v.scalar_tensor_tensor(out=chunked(X1[:, :]), in0=ps6(C), scalar=one("b2"), in1=chunked(u(XL, L, C)),
                                       op0=ALU.add, op1=ALU.add).then_inc(x1_part.sem, 1)
                dve.wait_ge(x1_part.sem, x1_part.at(b))
                v.tensor_tensor(X1[:, :], X1[:, :], X0, ALU.add).then_inc(x1_ready.sem, 1)
                dve.wait_ge(x1_ready.sem, x1_ready.at(b))

                def diagonals(at, n, weights, done):
                    v.tensor_tensor(u(at, n * 128).rearrange("p (k m) -> p k m", k=n),
                                    w("ident").unsqueeze(1).broadcast_to([128, n, 128]),
                                    w(weights).unsqueeze(2).broadcast_to([128, n, 128]), ALU.mult)\
                        .then_inc(done.sem, 1)

                group_norm(1, X1[:, :], u(FG, L, C))
                diagonals(FDIAG, 18, "convw", fdiag)
                for k in range(4):
                    dve.wait_ge(hi_ready.sem, hi_ready.at(b, k + 1))
                    if k >= 1:
                        dve.wait_ge(mid_ready.sem, mid_ready.at(b, k))
                        dve.wait_ge(lo_ready.sem, lo_ready.at(b, k))
                    v.tensor_tensor(chunked(u(R1, L, 96)), ps6(96), chunked(PBC[:, k, :]), ALU.subtract)\
                        .then_inc(r1_ready.sem, 1)
                    dve.wait_ge(mid_ready.sem, mid_ready.at(b, k + 1))
                    dve.wait_ge(r1_ready.sem, r1_ready.at(b, k + 1))
                    v.tensor_tensor(PBC[64:96, k, :], U[64:96, R1:R1 + L], mid[64:96, :], ALU.subtract)\
                        .then_inc(lo_ready.sem, 1)

                def log1p(q):
                    dve.wait_ge(sp_cubic.sem, sp_cubic.at(b, q + 1))
                    dve.wait_ge(sp_ln.sem, sp_ln.at(b, q + 1))
                    v.scalar_tensor_tensor(out=TL[:, :], in0=TL[:, :], scalar=LOG_MARGIN, in1=TW[:, :],
                                           op0=ALU.add, op1=ALU.min).then_inc(sp_log1p.sem, 1)

                def dlt_and_cumsum(q):
                    p = q % 2
                    dve.wait_ge(sp_log1p.sem, sp_log1p.at(b, q + 1))
                    v.scalar_tensor_tensor(out=u(DL[p]), in0=u(DL[p]), scalar=0.0, in1=TL[:, :],
                                           op0=ALU.max, op1=ALU.add).then_inc(dlt_ready.sem, 1)
                    dve.wait_ge(dlt_ready.sem, dlt_ready.at(b, q + 1))
                    d, o = u(DL[p]), u(CS[p])
                    if q % 2:
                        d, o = d[:, ::-1], o[:, ::-1]
                    v.tensor_tensor_scan(o, d, d, 0.0, ALU.add, ALU.max).then_inc(cs_ready.sem, 1)

                def tiles(q, m, es=range(4), y_out=None):
                    for e in es:
                        t = b * NT + q * NSTATE + m * 4 + e
                        base = t * PER_TILE
                        dve.wait_ge(gu_ready.sem, t + 1)
                        for j, (c0, cw) in enumerate(CUTS):
                            gc = U[:, G[e] + c0:G[e] + c0 + cw]
                            dve.wait_ge(ring_full.sem, base + j + 1)
                            v.tensor_tensor(gc, gc, PS[:, 5 + SLOT_B[j], 0:cw], ALU.mult).then_inc(ring_used.sem, 1)
                        dve.wait_ge(ring_used.sem, base + NCUT + RING_CREDIT)
                        dve.wait_ge(a_ready.sem, t + 1)
                        h, a = u(G[e]), u(A[e % 2])
                        if q % 2:
                            h, a = h[:, ::-1], a[:, ::-1]
                        v.tensor_tensor_scan(h, a, h, 0.0, ALU.mult, ALU.add).then_inc(scanned.sem, 1)
                        if y_out is not None and e == 0:
                            y_out()
                        dve.wait_ge(scanned.sem, t + 3)
                        for j, (c0, cw) in enumerate(CUTS):
                            gc = U[:, G[e] + c0:G[e] + c0 + cw]
                            dve.wait_ge(ring_full.sem, base + NCUT + j + 1)
                            v.tensor_tensor(gc, gc, PS[:, 5 + SLOT_C[j], 0:cw], ALU.mult).then_inc(ring_used.sem, 1)

                def y_group(g):
                    dve.wait_ge(z_used.sem, b * NT + (g + 1) * 2 * NSTATE + 4)
                    v.tensor_copy(XS[g][:, :], PS[:, 0:NCUT, :].rearrange("p a n -> p (a n)")[:, 0:L])\
                        .then_inc(y_sb.sem, 1)

                log1p(0)
                dlt_and_cumsum(0)
                for q in range(QS):
                    tiles(q, 0, y_out=(lambda: y_group(q // 2 - 1)) if q and q % 2 == 0 else None)
                    if q + 1 < QS:
                        log1p(q + 1)
                    with dve.Fori(1, 3) as m:
                        tiles(q, m)
                    if q + 1 < QS:
                        dlt_and_cumsum(q + 1)
                    tiles(q, 3)
                y_group(2)

                dve.wait_ge(ys_psum.sem, ys_psum.at(b, 1))
                v.tensor_scalar(u(ZG, L, C), X1[:, :], small(MG + 1), small(RSTD + 1), ALU.subtract, ALU.mult)\
                    .then_inc(zg_ready.sem, 1)
                diagonals(BDIAG, 27, "c2w", bdiag)
                dve.wait_ge(ymu_psum.sem, ymu_psum.at(b))
                v.tensor_tensor(chunked(u(YA)), chunked(u(YA)), ps6(128), ALU.subtract).then_inc(yd_ready.sem, 1)
                v.tensor_tensor(chunked(u(YB, L, 64)), chunked(u(YB, L, 64)), ps6(64), ALU.subtract)\
                    .then_inc(yd_ready.sem, 1)
                dve.wait_ge(ystd.sem, ystd.at(b))
                v.reciprocal(u(SD), u(SD)).then_inc(yinv.sem, 1)
                dve.wait_ge(yinv.sem, yinv.at(b))
                parts = ((YA, 128, 0), (YB, 64, 1))
                for at, rows, k in parts:
                    v.tensor_tensor(u(at, L, rows), u(at, L, rows), u(SD, L, rows), ALU.mult).then_inc(yunit.sem, 1)
                for at, rows, k in parts:
                    dve.wait_ge(yunit.sem, yunit.at(b, k + 1))
                    v.tensor_scalar(u(at, L, rows), u(at, L, rows), one("lng", rows, k), one("lnb", rows, k),
                                    ALU.mult, ALU.add).then_inc(yn_ready.sem, 1)
                for at, rows, k in parts:
                    dve.wait_ge(yn_ready.sem, yn_ready.at(b, k + 1))
                    dve.wait_ge(z_psum.sem, z_psum.at(b, k + 1))
                    v.tensor_tensor(chunked(u(at, L, rows)), chunked(u(at, L, rows)), ps6(rows), ALU.mult)\
                        .then_inc(u_ready.sem, 1)
                dve.wait_ge(se2_ready.sem, se2_ready.at(b))
                v.tensor_scalar(small(SE2), small(SE2), 1.0, None, ALU.add).then_inc(se_plus.sem, 1)
                dve.wait_ge(se_plus.sem, se_plus.at(b))
                v.scalar_tensor_tensor(out=u(OUT, L, C), in0=u(T3, L, C), scalar=small(SE2), in1=X1[:, :],
                                       op0=ALU.mult, op1=ALU.add).then_inc(out_ready.sem, 1)


def kernel(**inputs):
    import numpy as np
    import ml_dtypes
    import concourse.bacc as bacc
    from concourse import mybir
    from concourse.bass_utils import run_bass_kernel_spmd

    a = {k: np.ascontiguousarray(v) for k, v in inputs.items()}
    l0 = {k[8:]: v for k, v in a.items() if k.startswith("L0_conv_")}
    l1 = {k[8:]: v for k, v in a.items() if k.startswith("L1_conv_")}

    pk = np.zeros((128, PWIDTH), np.float32)

    def put(table, arr, name, value, lo=0, row=0):
        value = value.reshape(value.shape[0], -1)
        at, width = table[name]
        assert lo + value.shape[1] <= width
        arr[row:row + value.shape[0], at + lo:at + lo + value.shape[1]] = value

    def P(name, value, lo=0, row=0):
        put(PCOL, pk, name, value, lo, row)

    P("ident", np.eye(128, dtype=np.float32))
    same = (np.arange(C)[:, None] // 3 == np.arange(C)[None, :] // 3)
    P("gmean", np.where(same, np.float32(1 / 3), np.float32(0)))
    P("mean96", np.full((C, C), 1 / 96, np.float32))
    P("sum96", np.ones((C, C), np.float32))
    P("mean192", np.full((128, 128), 1 / 192, np.float32))
    P("w1", l0["w1"].T)
    P("w2", l0["w2"][:, 0:C].T)
    P("w2", l0["w2"][:, C:2 * C].T, C)
    ip = l1["in_proj_w"]
    P("in_a", ip[0:128].T)
    P("in_b", ip[128:192].T)
    P("in_b", ip[128:192].T, 64)
    P("z_a", ip[E:E + 128].T)
    P("z_b", ip[E + 128:2 * E].T)
    for s in range(2):
        for i, k in enumerate((s, 2 + s)):
            wt = l1["dt_proj_w"][k].T
            row = 32 * s + RANK * i
            P("dtw", wt[:, 0:128], i * 128, row)
            P("dtw", wt[:, 128:192], 256 + 64 * i, row)
    P("b1", l0["b1"].reshape(2, C).T)
    P("b2", l0["b2"][:, None])
    P("ln0w", l0["ln_w"][:, None])
    P("ln0b", l0["ln_b"][:, None])
    cw = l1["conv_w"].reshape(E, 9)
    P("convw", cw[0:128])
    P("convw", cw[128:192], 9)
    P("convw", cw[128:192], 9, 64)
    P("convb", l1["conv_b"][0:128, None])
    P("convb", l1["conv_b"][128:192, None], 1)
    P("convb", l1["conv_b"][128:192, None], 1, 64)
    for s in range(2):
        for i, k in enumerate((s, 2 + s)):
            P("dtb", l1["dt_proj_b"][k, 0:128, None], i * 2 + s)
            P("dtb", l1["dt_proj_b"][k, 128:192, None], 4 + s, 64 * i)
            P("alog", l1["A_log"][k, 0:128], (i * 2 + s) * NSTATE)
            P("alog", l1["A_log"][k, 128:192], (4 + s) * NSTATE, 64 * i)
    P("ds", l1["Ds"][:, 0:128].T)
    P("ds", l1["Ds"][:, 128:192].T, 4)
    for name, src in (("lng", "ln_g"), ("lnb", "ln_b")):
        P(name, l1[src][0:128, None])
        P(name, l1[src][128:192, None], 1)
    for name, src in (("c1b", "c1_b"), ("bn1g", "bn1_g"), ("bn1b", "bn1_b"), ("bn1m", "bn1_m"), ("bn1v", "bn1_v"),
                      ("c2b", "c2_b"), ("bn2g", "bn2_g"), ("bn2b", "bn2_b"), ("bn2m", "bn2_m"), ("bn2v", "bn2_v")):
        P(name, l1[src].reshape(3, 128).T)
    P("c2w", l1["c2_w"].reshape(3, 128, 9).transpose(1, 0, 2))
    P("c3b", l1["c3_b"][:, None])
    P("se1b", l1["se1_b"][:, None])
    P("se2b", l1["se2_b"][:, None])

    bk = np.zeros((128, BWIDTH), np.float32)
    c1 = l1["c1_w"].reshape(2 * E, E).T
    put(BCOL, bk, "c1a", c1[0:128])
    put(BCOL, bk, "c1bm", c1[128:192])
    put(BCOL, bk, "c3", l1["c3_w"].reshape(C, 3, 128).transpose(2, 1, 0))
    put(BCOL, bk, "se1", l1["se1_w"].T)
    put(BCOL, bk, "se2", l1["se2_w"].T)

    xp = np.zeros((128, 3, 4, XPM), np.float32)
    for s in range(2):
        for i, k in enumerate((s, 2 + s)):
            wt = l1["x_proj_w"][k].T
            for bc in range(2):
                cols = wt[:, RANK + NSTATE * bc:RANK + NSTATE * (bc + 1)]
                places = [(32 * r + 16 * i, cols) for r in range(3)]
                if bc == 0:
                    places.append((96 + RANK * i, wt[:, 0:RANK]))
                for at, part in places:
                    xp[:, i, 2 * s + bc, at:at + part.shape[1]] = part[0:128]
                    xp[64 * i:64 * i + 64, 2, 2 * s + bc, at:at + part.shape[1]] = part[128:192]

    sel = np.zeros((96, 3, NSTATE, 128), np.float32)
    for r in range(3):
        for n in range(NSTATE):
            sel[32 * r + n, 0, n, :] = 1
            sel[32 * r + 16 + n, 1, n, :] = 1
            sel[32 * r + n, 2, n, 0:64] = 1
            sel[32 * r + 16 + n, 2, n, 64:128] = 1
    mq = np.zeros((24, 128), np.float32)
    for y in range(TQ_Y):
        for xx in range(TQ_X):
            mq[y, y * TQ_X + xx] = 1
            mq[TQ_Y + xx, y * TQ_X + xx] = 1
    mk = np.zeros((24, 3, 3, KEY_Y, KEY_X), np.float32)
    tiles_y, tiles_x = (0, 1, NT_Y - 1), (0, 1, NT_X - 1)
    for a_, i in enumerate(tiles_y):
        for b_, j in enumerate(tiles_x):
            ky, kx = key_origin(i, j)
            for y in range(TQ_Y):
                far = np.abs(ky + np.arange(KEY_Y) - (TQ_Y * i + y)) > HALF_WIN
                mk[y, a_, b_][far, :] = -1024
            for xx in range(TQ_X):
                far = np.abs(kx + np.arange(KEY_X) - (TQ_X * j + xx)) > HALF_WIN
                mk[TQ_Y + xx, a_, b_][:, far] = -1024

    arrays = {
        "x": a["x"].reshape(BATCH * C, L), "pack": pk, "back": bk, "xpw": xp.reshape(128, XPW),
        "masks": mk.reshape(24, 9 * KEYS).astype(ml_dtypes.bfloat16), "maskq": mq.astype(ml_dtypes.bfloat16),
        "sels": sel.reshape(96, -1).astype(ml_dtypes.bfloat16),
    }
    nc = bacc.Bacc("TRN2", target_bir_lowering=False, num_devices=1)
    args = [nc.dram_tensor(f"in_{n}", v.shape, mybir.dt.from_np(v.dtype), kind="ExternalInput").ap()
            for n, v in arrays.items()]
    out = nc.dram_tensor("out", (BATCH * C, L), mybir.dt.float32, kind="ExternalOutput").ap()
    build(nc, *args, out)
    r = run_bass_kernel_spmd(nc, [{f"in_{n}": v for n, v in arrays.items()}], core_ids=[0])
    return r.results[0]["out"].reshape(BATCH, C, H, W)
```

```python
from contextlib import ExitStack

import concourse.bass as bass
from concourse import mybir

BATCH, C, H, W = 4, 96, 48, 48
L = H * W
E = 192
NSTATE = 16
RANK = 6
TOPK = 8
HALF_WIN = 6
ROWS = 8
CH = ROWS * W
NCH = L // CH
TQ_Y, TQ_X = 8, 16
KEY_Y, KEY_X = TQ_Y + 2 * HALF_WIN, TQ_X + 2 * HALF_WIN
KEYS = KEY_Y * KEY_X
KC = 4 * KEY_X
NKC = KEYS // KC
NT_Y, NT_X = H // TQ_Y, W // TQ_X
TILES = NT_Y * NT_X
PADW = W + 2
PADN = PADW * PADW
QS = 6
PC = L // 3
PC_CUTS = [(0, 512), (512, PC - 512)]
RUNS = 3 * QS
PIECES = RUNS * NSTATE
RING = 8
BLOCK = 4
Y_BANK, B_BANK, C_BANK = 0, 2, (4, 6)
DT_AT = 4
LN_1E12 = 27.631021115928547
CUB_SCALE = 3 ** -0.5
LOG_MARGIN = 6e-8
NEG = -1e30
XR = 2 * RANK


def key_origin(i, j):
    return (min(max(TQ_Y * i - HALF_WIN, 0), H - KEY_Y), min(max(TQ_X * j - HALF_WIN, 0), W - KEY_X))


def kind(i, n):
    return 0 if i == 0 else (2 if i == n - 1 else 1)


PACK = [("ident", 128), ("gmean", C), ("mean96", C), ("sum96", C), ("mean192", 128),
        ("w1", 2 * C), ("w2", 2 * C), ("in_a", 128), ("in_b", 128), ("z_a", 128), ("z_b", 64),
        ("dtw", 3 * 128), ("b1", 2), ("b2", 1), ("ln0w", 1), ("ln0b", 1),
        ("convw", 18), ("convb", 2), ("dtb", QS), ("alog", QS * NSTATE), ("ds", 8),
        ("lng", 2), ("lnb", 2), ("c1b", 3), ("bn1g", 3), ("bn1b", 3), ("bn1m", 3), ("bn1v", 3),
        ("c2w", 27), ("c2b", 3), ("bn2g", 3), ("bn2b", 3), ("bn2m", 3), ("bn2v", 3),
        ("c3b", 1), ("se1b", 1), ("se2b", 1)]
BACK = [("c1a", 2 * E), ("c1bm", 2 * E), ("c3", 3 * C), ("se1", E // 4), ("se2", E // 2)]


def columns(table):
    at, out = 0, {}
    for name, width in table:
        out[name] = (at, width)
        at += width
    return out, at


PCOL, PWIDTH = columns(PACK)
BCOL, BWIDTH = columns(BACK)
XPM = 96 + XR
XPW = 3 * 4 * XPM


class Signal:

    def __init__(self, ctx, nc, name, per=1):
        self.sem = ctx.enter_context(nc.semaphore(name))
        self.per = per

    def at(self, b, k=None):
        return b * self.per + (self.per if k is None else k)


def build(nc, x, pack, back, xpw, masks, maskq, sels, out):
    f32, bf16 = mybir.dt.float32, mybir.dt.bfloat16
    ALU, ACT, AX = mybir.AluOpType, mybir.ActivationFunctionType, mybir.AxisListType

    with ExitStack() as ctx:
        def sb(name, shape, dt=f32):
            return ctx.enter_context(nc.sbuf_tensor(name, shape, dt))

        def sig(name, per=1):
            return Signal(ctx, nc, name, per)

        PK = sb("packed_weights", [128, PWIDTH])
        SEL = sb("state_selectors", [96, 3 * NSTATE * 128], bf16)
        MQ = sb("window_query_rows", [24, 128], bf16)
        X1 = sb("x_after_layer0", [C, L])
        XS = [sb(f"scan_input_{g}", [128, L]) for g in range(3)]
        PBC = sb("b_c_split_rows", [96, 4, L], bf16)
        RD = sb("dt_rows", [32 + XR, L])
        U = sb("work", [128, 5 * L + 2 * RING * PC + L])
        TW = sb("softplus_w", [128, L])
        TL = sb("softplus_l", [128, L])
        SM = sb("small", [128, 128])
        CARRY = sb("scan_state", [128, NSTATE])
        NA = sb("neg_a", [128, QS * NSTATE])
        PS = ctx.enter_context(nc.psum_tensor("psum", [128, 8, 512], f32))

        def w(name, rows=128, lo=0, n=None):
            at, width = PCOL[name]
            return PK[0:rows, at + lo:at + lo + (width - lo if n is None else n)]

        def wb(name, rows=128, lo=0, n=None):
            at, width = BCOL[name]
            return TW[0:rows, at + lo:at + lo + (width - lo if n is None else n)]

        def u(at, width=L, rows=128):
            return U[0:rows, at:at + width]

        def two_banks(bank):
            return PS[:, bank:bank + 2, :].rearrange("p a n -> p (a n)")[:, 0:PC]

        def piece_at(r):
            q, i = divmod(r, 3)
            return (2 - i if q % 2 else i) * PC

        def chunked(ap):
            return ap.rearrange("p (a b) -> p a b", b=CH)

        def image(ap):
            return ap.rearrange("p (h w) -> p h w", w=W)

        def image_t(ap):
            return ap.rearrange("p (w h) -> p h w", h=H)

        def ps6(rows, lo=0):
            return PS[lo:lo + rows, 0:NCH, 0:CH]

        def ps_rows(rows, lo=0):
            return ps6(rows, lo).rearrange("p a (r w) -> p a r w", w=W)

        def interior(pad):
            v = pad.rearrange("p (h w) -> p h w", w=PADW)[:, 1:1 + H, 1:1 + W]
            return v.rearrange("p (a r) w -> p a r w", r=ROWS)

        def one(name, rows=C, at=0):
            return w(name, rows, at, 1)

        def small(k, rows=C, n=1):
            return SM[0:rows, k:k + n]

        BN_STATS = 0
        MV, VC, DM, MG, STD, RSTD = 36, 38, 39, 40, 42, 44
        T_M8, T_NM, T_E8, T_Z, T_RZ = 46, 62, 64, 80, 82
        S1, B1C, S2, B2C, DSUM = 84, 87, 90, 93, 96
        TSUM, TMEAN, SE1, SE2, LNC = 98, 99, 100, 101, 102
        CT = 104
        EPS5, ONE, CUBB, CUBC, LEAST = 120, 121, 122, 123, 124

        XG, XN, XL, SQ, NR, DD = (k * L for k in range(6))
        HID = [3 * L, 4 * L]
        at = 6 * L
        tile_at = {}
        for name, width in [("query", 128), ("keys", KEYS), ("rest", KEYS), ("exp", KEYS), ("wts", KEYS),
                            ("keysT", NKC * C), ("wtsT", NKC * 128), ("diag", 128)]:
            tile_at[name] = (at, width)
            at += 2 * width
        assert at <= 11 * L

        def tb(name, t, rows=128):
            a, width = tile_at[name]
            return u(a + (t % 2) * width, width, rows)

        MK = PBC[0:24, 0:3, :].rearrange("p a n -> p (a n)")[:, 0:9 * KEYS]
        X0 = XS[0][0:C, :]

        FG = 0
        PAD = [L, L + PADN]
        FDIAG = L + 2 * PADN
        ACC = FDIAG + 9 * 128
        R1 = ACC + L
        T2 = R1 + L
        XP = T2 + L // 2
        assert XP + XPW <= 11 * L
        mid = u(T2, L // 2, 96).bitcast(bf16)

        G = [k * PC for k in range(RING)]
        A = [(RING + k) * PC for k in range(RING)]
        top = 2 * RING * PC
        DL = [top, top + L]
        CS = [top + 2 * L, top + 3 * L]
        UX = top + 4 * L
        YS = top + 5 * L

        YA, YB, SA, SBQ, SD = (k * L for k in range(5))
        PAD2 = [5 * L + k * PADN for k in range(3)]
        ZG = PAD2[2] + PADN
        BDIAG = ZG + L
        assert BDIAG + 9 * 128 <= 6 * L + 2 * RING * PC
        MIX = [4 * L, 3 * L, 2 * L]
        T3, OUT = 0, L

        loaded = sig("weights_loaded")
        ready = sig("constants_ready")
        batch_free = sig("image_done")
        x_in, mask_in, xpw_in, back_in, stored = (sig(n) for n in
                                                  ("x_in", "masks_in", "xpw_in", "back_weights_in", "stored"))
        gn_stat, gn_mv, gn_mean, gn_mg, gn_dev, gn_vc, gn_var, gn_std, gn_rstd, xg_ready = (
            sig(n, p) for n, p in (("gn_stats", 2 * NCH), ("gn_channel", 2), ("gn_mean", 2), ("gn_mean_sb", 2),
                                   ("gn_dev", 2), ("gn_second", 2), ("gn_var", 2), ("gn_std", 2),
                                   ("gn_rstd", 2), ("gn_out", 2)))
        sq_ready, ssq_ready, nrm_ln, nrm_inv, xn_ready = (sig(n) for n in (
            "squares", "norm2_psum", "norm_ln", "norm_inv", "unit_vectors"))
        mu_ready, dev_ready, dsq_ready, lvar_ready, lvar_ln, linv, lnorm, xl_ready = (sig(n) for n in (
            "ln0_mean", "ln0_dev", "ln0_dev2", "ln0_var", "ln0_var_ln", "ln0_inv", "ln0_unit", "ln0_out"))
        q_ready, k_ready, s_ready, kt_psum, kt_sb, m8_ready, rest_ready, nm_ready, z_ready, exp_ready, exp2_ready, \
            wts_ready, rz_ready, diag_ready, wt_psum, wt_sb, agg_psum, enh_ready = (
                sig(n, TILES) for n in ("queries_copied", "keys_copied", "sims_psum", "keysT_psum", "keysT_sb",
                                        "top8", "rest_of_sims", "neg_max", "exp_sum", "exp_all", "exp_rest",
                                        "weights", "sum_inv", "diag_ready", "weightsT_psum", "weightsT_sb",
                                        "agg_psum", "enhanced"))
        hid_psum, hid_ready, ffn_psum, x1_part, x1_ready = (sig(n, p) for n, p in (
            ("hidden_psum", 2), ("hidden", 2), ("ffn_psum", 1), ("x1_partial", 1), ("x1", 1)))
        pad_zero, fdiag, xi_psum, xi_pad, conv_psum, xs_ready = (sig(n, p) for n, p in (
            ("pads_zero", 1), ("conv_diag", 1), ("xi_psum", 2), ("xi_padded", 2), ("conv_psum", 1),
            ("scan_inputs", 4)))
        xp_psum, hi_ready, r1_ready, mid_ready, mid_moved, lo_ready, rd_ready = (sig(n, p) for n, p in (
            ("x_proj_psum", 4), ("split_hi", 4), ("split_rest", 4), ("split_mid", 4), ("split_mid_moved", 4),
            ("split_lo", 4), ("dt_rows_ready", 2)))
        dt_psum, dt_sb, sp_abs, sp_exp, sp_square, sp_ln, sp_quad, sp_cubic, sp_log1p, dlt_ready, cs_ready, \
            ux_ready = (sig(n, p) for n, p in (
                ("dt_psum", QS * 3), ("dt_raw", QS * 3), ("softplus_abs", QS), ("softplus_exp", QS),
                ("softplus_square", QS), ("softplus_ln", QS), ("softplus_quadratic", QS), ("softplus_cubic", QS),
                ("softplus_log1p", QS), ("dlt", QS), ("dlt_cumsum", QS), ("dlt_x", QS)))
        a_ready, g_ready, gu_ready, b_full, b_used, scanned, carried, c_full, ch_ready, y_added = (
            sig(n, PIECES) for n in ("decay", "guard", "guard_dlt_x", "b_in_psum", "b_used", "scanned",
                                     "state_saved", "c_in_psum", "c_h", "y_added"))
        y_out = sig("y_run_out", RUNS)
        ys_psum, ys_sb, ymu_psum, yd_ready, ysq_ready, yvar_psum, yvar_ln, yinv, yunit = (
            sig(n, p) for n, p in (("ys_psum", 2), ("ys", 2), ("y_mean", 1), ("y_dev", 2), ("y_dev2", 2),
                                   ("y_var", 1), ("y_var_ln", 1), ("y_inv", 1), ("y_unit", 2)))
        zg_ready, z_psum, u_ready, pad2_zero, bdiag, c1_psum, c1_pad, c2_psum, mix_ready, c3_psum, t3_ready = (
            sig(n, p) for n, p in (("z_input", 1), ("z_psum", 2), ("gated", 2), ("pads2_zero", 1),
                                   ("conv2_diag", 1), ("c1_psum", 3), ("c1_padded", 3), ("c2_psum", 1),
                                   ("c2_out", 3), ("c3_psum", 1), ("c3_out", 1)))
        ftap, btap = sig("conv_taps", 8), sig("conv2_taps", 16)
        fconv, bconv = sig("conv_sum", 1), sig("conv2_sum", 2)
        tmean, se1_psum, se1_ready, se2_psum, se2_ready, se_plus, out_ready = (sig(n) for n in (
            "t_mean", "se1_psum", "se1_out", "se2_psum", "se2_out", "se_factor", "out_ready"))
        settled = {e.engine: sig(f"settled_{k}") for k, e in
                   enumerate((nc.sync, nc.gpsimd, nc.scalar, nc.vector))}
        setup_v, setup_a = sig("setup_vector"), sig("setup_scalar")

        LOADS = 3 * 16
        CONSTS = 2

        def alone(eng, *waits):
            for signal, count in waits:
                eng.wait_ge(signal.sem, count)
            eng.sem_inc(settled[eng.engine].sem, 1)

        block = ctx.enter_context(nc.Block())

        @block.sync
        def _(sp):
            sp.dma_start(PK[:, :], pack).then_inc(loaded.sem, 16)
            sp.dma_start(SEL[:, :], sels).then_inc(loaded.sem, 16)
            sp.dma_start(MQ[:, :], maskq).then_inc(loaded.sem, 16)
            with sp.Fori(0, BATCH) as b:
                alone(sp, (batch_free, batch_free.at(b)))
                sp.dma_start(X0, x[bass.ds(b * C, C), :]).then_inc(x_in.sem, 16)
                sp.dma_start(MK, masks).then_inc(mask_in.sem, 16)
                sp.wait_ge(x1_ready.sem, x1_ready.at(b))
                sp.dma_start(u(XP, XPW), xpw).then_inc(xpw_in.sem, 16)
                sp.wait_ge(y_out.sem, y_out.at(b))
                sp.dma_start(TW[:, 0:BWIDTH], back).then_inc(back_in.sem, 16)
                alone(sp, (out_ready, out_ready.at(b)))
                sp.dma_start(out[bass.ds(b * C, C), :], u(OUT, L, C)).then_inc(stored.sem, 16)
                sp.wait_ge(stored.sem, b * 16 + 16)
                sp.sem_inc(batch_free.sem, 1)
            sp.wait_ge(stored.sem, 16 * BATCH)

        @block.gpsimd
        def _(pool):
            pool.sem_inc(batch_free.sem, 1)
            pool.sem_inc(carried.sem, RING)
            pool.sem_inc(y_added.sem, RING)
            pool.sem_inc(ready.sem, 1)
            with pool.Fori(0, BATCH) as b:
                xn_img, xg_img = image(u(XN, L, C)), image(u(XG, L, C))

                def copies(t):
                    i, j = divmod(t, NT_X)
                    ky, kx = key_origin(i, j)
                    alone(pool, *([(kt_psum, kt_psum.at(b, t - 1))] if t >= 2 else []))
                    nc.gpsimd.tensor_copy(tb("query", t, C).rearrange("p (h w) -> p h w", w=TQ_X),
                                          xn_img[:, TQ_Y * i:TQ_Y * (i + 1), TQ_X * j:TQ_X * (j + 1)])\
                        .then_inc(q_ready.sem, 1)
                    nc.gpsimd.tensor_copy(tb("keys", t, C).rearrange("p (h w) -> p h w", w=KEY_X),
                                          xg_img[:, ky:ky + KEY_Y, kx:kx + KEY_X]).then_inc(k_ready.sem, 1)

                pool.wait_ge(xn_ready.sem, xn_ready.at(b))
                copies(0)
                for t in range(TILES):
                    if t + 1 < TILES:
                        copies(t + 1)
                    pool.wait_ge(exp2_ready.sem, exp2_ready.at(b, t + 1))
                    nc.gpsimd.tensor_tensor(tb("wts", t), tb("exp", t), tb("wts", t), ALU.subtract)\
                        .then_inc(wts_ready.sem, 1)
                alone(pool, (x1_ready, x1_ready.at(b)))
                nc.gpsimd.memset(u(PAD[0], 2 * PADN), 0.0).then_inc(pad_zero.sem, 1)
                for k in range(4):
                    alone(pool, (mid_ready, mid_ready.at(b, k + 1)))
                    nc.gpsimd.tensor_copy(PBC[32:64, k, :], mid[32:64, :]).then_inc(mid_moved.sem, 1)

                def cubic(q):
                    pool.wait_ge(sp_quad.sem, sp_quad.at(b, q + 1))
                    nc.gpsimd.tensor_tensor(TW[:, :], TW[:, :], u(CS[q % 2]), ALU.mult).then_inc(sp_cubic.sem, 1)

                def save_state(r, n):
                    q, i = divmod(r, 3)
                    t = b * PIECES + r * NSTATE + n
                    k = n % RING
                    alone(pool, (scanned, t + 1))
                    last = G[k] + (0 if q % 2 else PC - 1)
                    nc.gpsimd.tensor_copy(CARRY[:, n:n + 1], U[:, last:last + 1]).then_inc(carried.sem, 1)

                cubic(0)
                pending = []
                for r in range(RUNS):
                    q, i = divmod(r, 3)
                    if i == 0:
                        pool.wait_ge(dlt_ready.sem, dlt_ready.at(b, q + 1))
                        if q >= 1:
                            pool.wait_ge(gu_ready.sem, gu_ready.at(b, r * NSTATE))
                        nc.gpsimd.tensor_tensor(u(UX), u(DL[q % 2]), XS[q // 2][:, :], ALU.mult)\
                            .then_inc(ux_ready.sem, 1)
                        pool.wait_ge(ux_ready.sem, ux_ready.at(b, q + 1))
                    if i == 1 and q + 1 < QS:
                        cubic(q + 1)
                    at = piece_at(r)
                    for n in range(NSTATE):
                        t = b * PIECES + r * NSTATE + n
                        pool.wait_ge(g_ready.sem, t + 1)
                        gk = u(G[n % RING], PC)
                        nc.gpsimd.tensor_tensor(gk, gk, u(UX + at, PC), ALU.mult).then_inc(gu_ready.sem, 1)
                        pending.append((r, n))
                        if len(pending) > 3:
                            save_state(*pending.pop(0))
                for r, n in pending:
                    save_state(r, n)
                alone(pool, (ys_psum, ys_psum.at(b, 1)))
                nc.gpsimd.memset(u(PAD2[0], 3 * PADN), 0.0).then_inc(pad2_zero.sem, 1)

        @block.scalar
        def _(act):
            f = nc.scalar.activation
            act.wait_ge(loaded.sem, LOADS)
            act.wait_ge(setup_v.sem, 1)
            f(small(CT, 128, 3), w("bn1v"), ACT.Sqrt, bias=small(EPS5, 128)).then_inc(setup_a.sem, 1)
            f(small(CT + 3, 128, 3), w("bn2v"), ACT.Sqrt, bias=small(EPS5, 128)).then_inc(setup_a.sem, 1)
            f(NA[:, :], w("alog"), ACT.Copy, scale=-1.0).then_inc(setup_a.sem, 1)
            act.wait_ge(ready.sem, CONSTS)
            act.wait_ge(setup_a.sem, 3)

            with act.Fori(0, BATCH) as b:
                def group_norm(l):
                    act.wait_ge(gn_var.sem, gn_var.at(b, l + 1))
                    f(small(STD), PS[0:C, 7, 1:2], ACT.Sqrt, bias=small(EPS5)).then_inc(gn_std.sem, 1)

                def inverse_root(dst, src, bias, ln, done):
                    f(chunked(dst), src, ACT.Ln, bias=bias).then_inc(ln.sem, 1)
                    act.wait_ge(ln.sem, ln.at(b))
                    f(dst, dst, ACT.Exp, scale=-0.5).then_inc(done.sem, 1)

                group_norm(0)
                act.wait_ge(xg_ready.sem, xg_ready.at(b, 1))
                f(u(SQ, L, C), u(XG, L, C), ACT.Square).then_inc(sq_ready.sem, 1)
                act.wait_ge(ssq_ready.sem, ssq_ready.at(b))
                inverse_root(u(NR, L, C), ps6(C), small(LEAST), nrm_ln, nrm_inv)
                act.wait_ge(dev_ready.sem, dev_ready.at(b))
                f(u(SQ, L, C), u(DD, L, C), ACT.Square).then_inc(dsq_ready.sem, 1)
                act.wait_ge(lvar_ready.sem, lvar_ready.at(b))
                act.wait_ge(xn_ready.sem, xn_ready.at(b))
                inverse_root(u(NR, L, C), ps6(C), small(EPS5), lvar_ln, linv)

                for t in range(TILES):
                    p = t % 2
                    m8, nm = small(T_M8 + 8 * p, 128, 8), small(T_NM + p, 128)
                    act.wait_ge(m8_ready.sem, m8_ready.at(b, t + 1))
                    f(nm, m8[:, 0:1], ACT.Copy, scale=-1.0).then_inc(nm_ready.sem, 1)
                    act.wait_ge(nm_ready.sem, nm_ready.at(b, t + 1))
                    if t >= 2:
                        act.wait_ge(rz_ready.sem, rz_ready.at(b, t - 1))
                    f(small(T_E8 + 8 * p, 128, 8), m8, ACT.Exp, bias=nm,
                      accum_out=small(T_Z + p, 128)).then_inc(z_ready.sem, 1)
                    act.wait_ge(rest_ready.sem, rest_ready.at(b, t + 1))
                    if t >= 2:
                        act.wait_ge(wts_ready.sem, wts_ready.at(b, t - 1))
                    f(tb("exp", t).rearrange("p (a n) -> p a n", a=2), PS[:, 2 * p:2 * p + 2, 0:KEYS // 2],
                      ACT.Exp, bias=nm).then_inc(exp_ready.sem, 1)
                    if t >= 2:
                        act.wait_ge(wt_psum.sem, wt_psum.at(b, t - 1))
                    f(tb("wts", t), tb("rest", t), ACT.Exp, bias=nm).then_inc(exp2_ready.sem, 1)
                    act.wait_ge(kt_psum.sem, kt_psum.at(b, t + 1))
                    if t >= 2:
                        act.wait_ge(agg_psum.sem, agg_psum.at(b, t - 1))
                    f(tb("keysT", t, KC), PS[0:KC, 6, 0:NKC * C], ACT.Copy).then_inc(kt_sb.sem, 1)

                for k in range(2):
                    act.wait_ge(hid_psum.sem, hid_psum.at(b, k + 1))
                    f(chunked(u(HID[k], L, C)), ps6(C), ACT.Relu, bias=one("b1", C, k)).then_inc(hid_ready.sem, 1)

                group_norm(1)
                act.wait_ge(pad_zero.sem, pad_zero.at(b))
                for k in range(2):
                    act.wait_ge(xi_psum.sem, xi_psum.at(b, k + 1))
                    f(interior(u(PAD[k], PADN)), ps_rows(128), ACT.Copy).then_inc(xi_pad.sem, 1)
                act.wait_ge(fconv.sem, fconv.at(b))
                f(XS[2][0:64, :], u(ACC, L, 64), ACT.Silu, bias=one("convb", 64, 1)).then_inc(xs_ready.sem, 1)
                f(image_t(XS[2][64:128, :]), image(U[64:128, ACC:ACC + L]), ACT.Silu,
                  bias=PK[64:128, PCOL["convb"][0] + 1:PCOL["convb"][0] + 2]).then_inc(xs_ready.sem, 1)
                act.wait_ge(conv_psum.sem, conv_psum.at(b))
                f(chunked(XS[0][:, :]), ps6(128), ACT.Silu, bias=one("convb", 128, 0)).then_inc(xs_ready.sem, 1)
                f(XS[1][:, :].rearrange("p (w a r) -> p a r w", a=NCH, r=ROWS), ps_rows(128), ACT.Silu,
                  bias=one("convb", 128, 0)).then_inc(xs_ready.sem, 1)
                for k in range(4):
                    act.wait_ge(xp_psum.sem, xp_psum.at(b, k + 1))
                    f(chunked(PBC[:, k, :]), ps6(96), ACT.Copy).then_inc(hi_ready.sem, 1)
                    if k % 2 == 0:
                        s = k // 2
                        f(chunked(RD[32 * s:32 * s + XR, :]), ps6(XR, 96), ACT.Copy).then_inc(rd_ready.sem, 1)
                    act.wait_ge(r1_ready.sem, r1_ready.at(b, k + 1))
                    if k >= 1:
                        act.wait_ge(mid_moved.sem, mid_moved.at(b, k))
                        act.wait_ge(lo_ready.sem, lo_ready.at(b, k))
                    f(mid, u(R1, L, 96), ACT.Copy).then_inc(mid_ready.sem, 1)

                def softplus(q):
                    p = q % 2
                    for j in range(3):
                        act.wait_ge(dt_psum.sem, dt_psum.at(b, q * 3 + j + 1))
                        f(u(DL[p] + j * PC, PC), two_banks(C_BANK[j % 2]), ACT.Identity,
                          bias=one("dtb", 128, q)).then_inc(dt_sb.sem, 1)
                    act.wait_ge(dt_sb.sem, dt_sb.at(b, (q + 1) * 3))
                    if q >= 2:
                        act.wait_ge(cs_ready.sem, cs_ready.at(b, q - 1))
                    f(u(CS[p]), u(DL[p]), ACT.Abs).then_inc(sp_abs.sem, 1)
                    act.wait_ge(sp_abs.sem, sp_abs.at(b, q + 1))
                    f(u(CS[p]), u(CS[p]), ACT.Exp, scale=-1.0).then_inc(sp_exp.sem, 1)
                    act.wait_ge(sp_exp.sem, sp_exp.at(b, q + 1))
                    if q >= 1:
                        act.wait_ge(dlt_ready.sem, dlt_ready.at(b, q))
                    f(TW[:, :], u(CS[p]), ACT.Square, bias=small(CUBB, 128), scale=CUB_SCALE)\
                        .then_inc(sp_square.sem, 1)
                    f(TL[:, :], u(CS[p]), ACT.Ln, bias=small(ONE, 128)).then_inc(sp_ln.sem, 1)
                    act.wait_ge(sp_square.sem, sp_square.at(b, q + 1))
                    f(TW[:, :], TW[:, :], ACT.Identity, bias=small(CUBC, 128)).then_inc(sp_quad.sem, 1)

                act.wait_ge(lo_ready.sem, lo_ready.at(b))
                softplus(0)
                for r in range(RUNS):
                    q, i = divmod(r, 3)
                    at = piece_at(r)
                    if i == 0:
                        act.wait_ge(dlt_ready.sem, dlt_ready.at(b, q + 1))
                        act.wait_ge(cs_ready.sem, cs_ready.at(b, q + 1))

                    def decay(n):
                        t = b * PIECES + r * NSTATE + n
                        act.wait_ge(y_added.sem, t + 1)
                        f(u(A[n % RING], PC), u(DL[q % 2] + at, PC), ACT.Exp,
                          scale=NA[:, q * NSTATE + n:q * NSTATE + n + 1]).then_inc(a_ready.sem, 1)

                    def guard(n):
                        t = b * PIECES + r * NSTATE + n
                        act.wait_ge(carried.sem, t + 1)
                        if r * NSTATE + n >= RING:
                            act.wait_ge(ch_ready.sem, ch_ready.at(b, r * NSTATE + n + 1 - RING))
                        f(u(G[n % RING], PC), u(CS[q % 2] + at, PC), ACT.Sigmoid,
                          scale=NA[:, q * NSTATE + n:q * NSTATE + n + 1], bias=small(LNC, 128))\
                            .then_inc(g_ready.sem, 1)

                    for block_no in range(NSTATE // BLOCK):
                        if i == 0 and block_no == NSTATE // BLOCK - 1 and q + 1 < QS:
                            softplus(q + 1)
                        parts = (guard, decay) if block_no % 2 == 0 else (decay, guard)
                        for part in parts:
                            for n in range(block_no * BLOCK, (block_no + 1) * BLOCK):
                                part(n)

                act.wait_ge(y_out.sem, y_out.at(b))
                act.wait_ge(carried.sem, carried.at(b) + RING)
                act.wait_ge(ys_psum.sem, ys_psum.at(b, 1))
                f(chunked(u(YA)), ps6(128), ACT.Identity, bias=small(DSUM, 128)).then_inc(ys_sb.sem, 1)
                act.wait_ge(ys_psum.sem, ys_psum.at(b, 2))
                f(chunked(u(YB, L, 64)), ps6(64), ACT.Identity, bias=small(DSUM + 1, 64)).then_inc(ys_sb.sem, 1)
                act.wait_ge(yd_ready.sem, yd_ready.at(b, 1))
                f(u(SA), u(YA), ACT.Square).then_inc(ysq_ready.sem, 1)
                act.wait_ge(yd_ready.sem, yd_ready.at(b, 2))
                f(u(SBQ, L, 64), u(YB, L, 64), ACT.Square).then_inc(ysq_ready.sem, 1)
                act.wait_ge(yvar_psum.sem, yvar_psum.at(b))
                inverse_root(u(SD), ps6(128), small(EPS5, 128), yvar_ln, yinv)
                act.wait_ge(pad2_zero.sem, pad2_zero.at(b))
                for k in range(3):
                    act.wait_ge(c1_psum.sem, c1_psum.at(b, k + 1))
                    f(interior(u(PAD2[k], PADN)), ps_rows(128), ACT.Relu, bias=small(B1C + k, 128),
                      scale=small(S1 + k, 128)).then_inc(c1_pad.sem, 1)
                for k in range(3):
                    if k < 2:
                        act.wait_ge(bconv.sem, bconv.at(b, k + 1))
                    else:
                        act.wait_ge(c2_psum.sem, c2_psum.at(b))
                    f(chunked(u(MIX[k])), chunked(u(MIX[k])) if k < 2 else ps6(128), ACT.Relu, bias=small(B2C + k, 128),
                      scale=small(S2 + k, 128)).then_inc(mix_ready.sem, 1)
                act.wait_ge(c3_psum.sem, c3_psum.at(b))
                f(chunked(u(T3, L, C)), ps6(C), ACT.Identity, bias=one("c3b"),
                  accum_out=small(TSUM)).then_inc(t3_ready.sem, 1)
                act.wait_ge(t3_ready.sem, t3_ready.at(b))
                f(small(TMEAN), small(TSUM), ACT.Copy, scale=1.0 / L).then_inc(tmean.sem, 1)
                act.wait_ge(se1_psum.sem, se1_psum.at(b))
                f(small(SE1, E // 4), PS[0:E // 4, 7, 2:3], ACT.Relu, bias=one("se1b", E // 4))\
                    .then_inc(se1_ready.sem, 1)
                act.wait_ge(se2_psum.sem, se2_psum.at(b))
                f(small(SE2), PS[0:C, 7, 3:4], ACT.Sigmoid, bias=one("se2b")).then_inc(se2_ready.sem, 1)

        @block.tensor
        def _(pe):
            mm = nc.tensor.matmul
            ident = w("ident")
            pe.wait_ge(loaded.sem, LOADS)
            pe.wait_ge(ready.sem, CONSTS)

            def plane(lhs_rhs, rows, done, lo=0):
                for c in range(NCH):
                    for k, (lhs, rhs) in enumerate(lhs_rhs):
                        last = mm(PS[lo:lo + rows, c, 0:CH], lhs, rhs(c), start=(k == 0),
                                  stop=(k == len(lhs_rhs) - 1))
                last.then_inc(done.sem, 1)

            def cut(ap):
                return lambda c: ap[:, c * CH:(c + 1) * CH]

            def turned(ap):
                v = ap.rearrange("p (w h) -> p h w", h=H)
                return lambda c: v[:, c * ROWS:(c + 1) * ROWS, :]

            def taps(pad, diag):
                v = pad.rearrange("p (h w) -> p h w", w=PADW)
                return [(diag[:, k * 128:(k + 1) * 128],
                         lambda c, k=k: v[:, c * ROWS + k // 3:c * ROWS + k // 3 + ROWS, k % 3:k % 3 + W])
                        for k in range(9)]

            with pe.Fori(0, BATCH) as b:
                def group_norm(l):
                    pe.wait_ge(gn_mv.sem, gn_mv.at(b, l + 1))
                    mm(PS[0:C, 7, 0:1], w("gmean", C), small(MV), start=True, stop=True).then_inc(gn_mean.sem, 1)
                    pe.wait_ge(gn_vc.sem, gn_vc.at(b, l + 1))
                    mm(PS[0:C, 7, 1:2], w("gmean", C), small(VC), start=True, stop=True).then_inc(gn_var.sem, 1)

                group_norm(0)
                pe.wait_ge(sq_ready.sem, sq_ready.at(b))
                plane([(w("sum96", C), cut(u(SQ, L, C)))], C, ssq_ready)
                pe.wait_ge(nrm_ln.sem, nrm_ln.at(b))
                plane([(w("mean96", C), cut(u(XG, L, C)))], C, mu_ready)
                pe.wait_ge(dsq_ready.sem, dsq_ready.at(b))
                plane([(w("mean96", C), cut(u(SQ, L, C)))], C, lvar_ready)

                xn_img = image(u(XN, L, C))
                pe.wait_ge(mask_in.sem, b * 16 + 16)
                pe.wait_ge(lvar_ln.sem, lvar_ln.at(b))
                for t in range(TILES + 1):
                    if t < TILES:
                        i, j = divmod(t, NT_X)
                        ky, kx = key_origin(i, j)
                        mask = (kind(i, NT_Y) * 3 + kind(j, NT_X)) * KEYS
                        pe.wait_ge(k_ready.sem, k_ready.at(b, t + 1))
                        if t >= 2:
                            pe.wait_ge(exp_ready.sem, exp_ready.at(b, t - 1))
                            pe.wait_ge(rest_ready.sem, rest_ready.at(b, t - 1))
                        for hf in range(2):
                            sims = PS[:, 2 * (t % 2) + hf, 0:KEYS // 2]
                            mm(sims, tb("query", t, C),
                               xn_img[:, ky + 10 * hf:ky + 10 * hf + 10, kx:kx + KEY_X], start=True, stop=False)
                            last = mm(sims, MQ[:, :], MK[:, mask + hf * KEYS // 2:mask + (hf + 1) * KEYS // 2],
                                      start=False, stop=True)
                        last.then_inc(s_ready.sem, 1)
                    if t >= 1:
                        r = t - 1
                        pe.wait_ge(wts_ready.sem, wts_ready.at(b, r + 1))
                        pe.wait_ge(diag_ready.sem, diag_ready.at(b, r + 1))
                        if r >= 1:
                            pe.wait_ge(wt_sb.sem, wt_sb.at(b, r))
                        for k in range(NKC):
                            last = mm(PS[0:KC, 4 + k // 4, (k % 4) * 128:(k % 4) * 128 + 128],
                                      tb("wts", r)[:, k * KC:(k + 1) * KC], tb("diag", r), start=True, stop=True)
                        last.then_inc(wt_psum.sem, 1)
                    if t < TILES:
                        if t >= 1:
                            pe.wait_ge(kt_sb.sem, kt_sb.at(b, t))
                        for k in range(NKC):
                            last = nc.tensor.transpose(PS[0:KC, 6, k * C:(k + 1) * C],
                                                       tb("keys", t, C)[:, k * KC:(k + 1) * KC],
                                                       w("ident", C, 0, C))
                        last.then_inc(kt_psum.sem, 1)
                    if t >= 1:
                        pe.wait_ge(wt_sb.sem, wt_sb.at(b, r + 1))
                        pe.wait_ge(kt_sb.sem, kt_sb.at(b, r + 1))
                        if r >= 1:
                            pe.wait_ge(enh_ready.sem, enh_ready.at(b, r))
                        for k in range(NKC):
                            last = mm(PS[0:C, 7, 0:128], tb("keysT", r, KC)[:, k * C:(k + 1) * C],
                                      tb("wtsT", r, KC)[:, k * 128:(k + 1) * 128], start=(k == 0),
                                      stop=(k == NKC - 1))
                        last.then_inc(agg_psum.sem, 1)

                pe.wait_ge(enh_ready.sem, enh_ready.at(b))
                for k in range(2):
                    if k:
                        pe.wait_ge(hid_ready.sem, hid_ready.at(b, 1))
                    plane([(w("w1", C, k * C, C), cut(u(XL, L, C)))], C, hid_psum)
                pe.wait_ge(hid_ready.sem, hid_ready.at(b, 2))
                plane([(w("w2", C, k * C, C), cut(u(HID[k], L, C))) for k in range(2)], C, ffn_psum)

                group_norm(1)
                pe.wait_ge(xg_ready.sem, xg_ready.at(b, 2))
                plane([(w("in_a", C), cut(u(FG, L, C)))], 128, xi_psum)
                pe.wait_ge(xi_pad.sem, xi_pad.at(b, 1))
                plane([(w("in_b", C), cut(u(FG, L, C)))], 128, xi_psum)
                pe.wait_ge(xi_pad.sem, xi_pad.at(b, 2))
                pe.wait_ge(fdiag.sem, fdiag.at(b))
                plane(taps(u(PAD[0], PADN), u(FDIAG, 9 * 128)), 128, conv_psum)
                pe.wait_ge(xs_ready.sem, xs_ready.at(b, 4))
                pe.wait_ge(xpw_in.sem, b * 16 + 16)
                for k in range(4):
                    m = XPM if k % 2 == 0 else 96
                    if k >= 1:
                        pe.wait_ge(r1_ready.sem, r1_ready.at(b, k))
                        pe.wait_ge(rd_ready.sem, rd_ready.at(b, (k + 1) // 2))
                    plane([(u(XP + (g * 4 + k) * XPM, m), cut(XS[g][:, :])) for g in range(3)], m, xp_psum)

                def dt_product(q, j):
                    g, s = divmod(q, 2)
                    for c0, cw in PC_CUTS:
                        last = mm(PS[:, C_BANK[j % 2] + c0 // 512, 0:cw],
                                  PK[32 * s:32 * s + XR, PCOL["dtw"][0] + g * 128:PCOL["dtw"][0] + (g + 1) * 128],
                                  RD[32 * s:32 * s + XR, j * PC + c0:j * PC + c0 + cw], start=True, stop=True)
                    last.then_inc(dt_psum.sem, 1)

                def broadcast(r, n, which, bank, done):
                    g, s = divmod(r // 3, 2)
                    at = piece_at(r)
                    for c0, cw in PC_CUTS:
                        last = mm(PS[:, bank + c0 // 512, 0:cw],
                                  SEL[:, (g * NSTATE + n) * 128:(g * NSTATE + n + 1) * 128],
                                  PBC[:, 2 * s + which, at + c0:at + c0 + cw], start=True, stop=True)
                    last.then_inc(done.sem, 1)

                pe.wait_ge(rd_ready.sem, rd_ready.at(b))
                pe.wait_ge(lo_ready.sem, lo_ready.at(b))
                pe.wait_ge(mid_moved.sem, mid_moved.at(b))
                for j in range(3):
                    if j == 2:
                        pe.wait_ge(dt_sb.sem, dt_sb.at(b, 1))
                    dt_product(0, j)
                broadcast(0, 0, 0, B_BANK, b_full)
                pe.wait_ge(dt_sb.sem, dt_sb.at(b, 3))
                broadcast(0, 0, 1, C_BANK[0], c_full)
                for r in range(RUNS):
                    q, i = divmod(r, 3)
                    for n in range(NSTATE):
                        t = r * NSTATE + n
                        if t + 1 < PIECES:
                            r1, n1 = divmod(t + 1, NSTATE)
                            pe.wait_ge(b_used.sem, b_used.at(b, t + 1))
                            broadcast(r1, n1, 0, B_BANK, b_full)
                            if t >= 1:
                                pe.wait_ge(ch_ready.sem, ch_ready.at(b, t))
                            j = n - DT_AT - 1
                            if i == 0 and q + 1 < QS and 0 <= j < 3:
                                pe.wait_ge(dt_sb.sem, dt_sb.at(b, (q + 1) * 3 + j + 1))
                            broadcast(r1, n1, 1, C_BANK[(t + 1) % 2], c_full)
                        pe.wait_ge(ch_ready.sem, ch_ready.at(b, t + 1))
                        if n == 0 and r >= 1:
                            pe.wait_ge(y_out.sem, y_out.at(b, r))
                        for c0, cw in PC_CUTS:
                            last = mm(PS[:, Y_BANK + c0 // 512, 0:cw], ident,
                                      u(A[n % RING] + c0, cw), start=(n == 0), stop=(n == NSTATE - 1),
                                      skip_group_check=True)
                        last.then_inc(y_added.sem, 1)
                        if i == 0 and q + 1 < QS and DT_AT <= n < DT_AT + 3:
                            dt_product(q + 1, n - DT_AT)

                pe.wait_ge(y_out.sem, y_out.at(b))
                plane([(ident, cut(XS[0][:, :])), (ident, turned(XS[1][:, :]))], 128, ys_psum)
                pe.wait_ge(ys_sb.sem, ys_sb.at(b, 1))
                plane([(ident[:, 0:64], cut(XS[2][:, :])), (ident[:, 64:128], turned(XS[2][:, :]))], 64, ys_psum)
                pe.wait_ge(ys_sb.sem, ys_sb.at(b, 2))
                plane([(w("mean192"), cut(u(YA))), (w("mean192", 64), cut(u(YB, L, 64)))], 128, ymu_psum)
                pe.wait_ge(yd_ready.sem, yd_ready.at(b))
                pe.wait_ge(ysq_ready.sem, ysq_ready.at(b))
                plane([(w("mean192"), cut(u(SA))), (w("mean192", 64), cut(u(SBQ, L, 64)))], 128, yvar_psum)
                pe.wait_ge(yvar_ln.sem, yvar_ln.at(b))
                pe.wait_ge(zg_ready.sem, zg_ready.at(b))
                plane([(w("z_a", C), cut(u(ZG, L, C)))], 128, z_psum)
                pe.wait_ge(u_ready.sem, u_ready.at(b, 1))
                plane([(w("z_b", C), cut(u(ZG, L, C)))], 64, z_psum)
                pe.wait_ge(u_ready.sem, u_ready.at(b, 2))
                pe.wait_ge(back_in.sem, b * 16 + 16)
                for k in range(3):
                    if k:
                        pe.wait_ge(c1_pad.sem, c1_pad.at(b, k))
                    plane([(wb("c1a", 128, k * 128, 128), cut(u(YA))),
                           (wb("c1bm", 64, k * 128, 128), cut(u(YB, L, 64)))], 128, c1_psum)
                pe.wait_ge(c1_pad.sem, c1_pad.at(b, 3))
                pe.wait_ge(bdiag.sem, bdiag.at(b))
                plane(taps(u(PAD2[2], PADN), u(BDIAG, 9 * 128)), 128, c2_psum)
                pe.wait_ge(mix_ready.sem, mix_ready.at(b, 3))
                plane([(wb("c3", 128, k * C, C), cut(u(MIX[k]))) for k in range(3)], C, c3_psum)
                pe.wait_ge(tmean.sem, tmean.at(b))
                mm(PS[0:E // 4, 7, 2:3], wb("se1", C), small(TMEAN), start=True, stop=True)\
                    .then_inc(se1_psum.sem, 1)
                pe.wait_ge(se1_ready.sem, se1_ready.at(b))
                mm(PS[0:C, 7, 3:4], wb("se2", E // 4), small(SE1, E // 4), start=True, stop=True)\
                    .then_inc(se2_psum.sem, 1)

        @block.vector
        def _(dve):
            v = nc.vector
            v.memset(small(EPS5, 128), 1e-5)
            v.memset(small(ONE, 128), 1.0)
            v.memset(small(CUBB, 128), -0.75 * CUB_SCALE)
            v.memset(small(CUBC, 128), 13 / 16)
            v.memset(small(LEAST, 128), 1e-36)
            v.memset(small(LNC, 128), LN_1E12).then_inc(setup_v.sem, 1)
            dve.wait_ge(loaded.sem, LOADS)
            dve.wait_ge(setup_a.sem, 3)
            steps = 1
            for k, (cb, g, bb, m, sc, off) in enumerate((("c1b", "bn1g", "bn1b", "bn1m", S1, B1C),
                                                         ("c2b", "bn2g", "bn2b", "bn2m", S2, B2C))):
                inv, dif = small(CT + 6, 128, 3), small(CT + 9, 128, 3)
                v.reciprocal(inv, small(CT + 3 * k, 128, 3)).then_inc(setup_v.sem, 1)
                v.tensor_tensor(dif, w(cb), w(m), ALU.subtract).then_inc(setup_v.sem, 1)
                steps += 2
                dve.wait_ge(setup_v.sem, steps)
                v.tensor_tensor(small(sc, 128, 3), w(g), inv, ALU.mult).then_inc(setup_v.sem, 1)
                steps += 1
                dve.wait_ge(setup_v.sem, steps)
                v.tensor_tensor(dif, dif, small(sc, 128, 3), ALU.mult).then_inc(setup_v.sem, 1)
                steps += 1
                dve.wait_ge(setup_v.sem, steps)
                v.tensor_tensor(small(off, 128, 3), dif, w(bb), ALU.add).then_inc(setup_v.sem, 1)
                steps += 1
                dve.wait_ge(setup_v.sem, steps)
            v.tensor_reduce(small(DSUM, 128, 2), w("ds").rearrange("p (a k) -> p a k", k=4), AX.X, ALU.add)\
                .then_inc(ready.sem, 1)
            dve.wait_ge(ready.sem, CONSTS)

            with dve.Fori(0, BATCH) as b:
                def group_norm(l, src, dst):
                    stats = small(BN_STATS, C, 6 * NCH).rearrange("p (a k) -> p a k", k=6)
                    for c in range(NCH):
                        v.bn_stats(stats[:, c, :], src[:, c * CH:(c + 1) * CH]).then_inc(gn_stat.sem, 1)
                    alone(dve, (gn_stat, gn_stat.at(b, (l + 1) * NCH)))
                    v.bn_aggr(small(MV, C, 2), stats).then_inc(gn_mv.sem, 1)
                    dve.wait_ge(gn_mean.sem, gn_mean.at(b, l + 1))
                    v.tensor_copy(small(MG + l), PS[0:C, 7, 0:1]).then_inc(gn_mg.sem, 1)
                    dve.wait_ge(gn_mg.sem, gn_mg.at(b, l + 1))
                    v.tensor_tensor(small(DM), small(MV), small(MG + l), ALU.subtract).then_inc(gn_dev.sem, 1)
                    dve.wait_ge(gn_dev.sem, gn_dev.at(b, l + 1))
                    v.scalar_tensor_tensor(out=small(VC), in0=small(DM), scalar=small(DM), in1=small(MV + 1),
                                           op0=ALU.mult, op1=ALU.add).then_inc(gn_vc.sem, 1)
                    dve.wait_ge(gn_std.sem, gn_std.at(b, l + 1))
                    v.reciprocal(small(RSTD + l), small(STD)).then_inc(gn_rstd.sem, 1)
                    dve.wait_ge(gn_rstd.sem, gn_rstd.at(b, l + 1))
                    v.tensor_scalar(dst, src, small(MG + l), small(RSTD + l), ALU.subtract, ALU.mult)\
                        .then_inc(xg_ready.sem, 1)

                dve.wait_ge(x_in.sem, b * 16 + 16)
                group_norm(0, X0, u(XG, L, C))
                dve.wait_ge(mu_ready.sem, mu_ready.at(b))
                dve.wait_ge(xg_ready.sem, xg_ready.at(b, 1))
                v.tensor_tensor(chunked(u(DD, L, C)), chunked(u(XG, L, C)), ps6(C), ALU.subtract)\
                    .then_inc(dev_ready.sem, 1)
                dve.wait_ge(nrm_inv.sem, nrm_inv.at(b))
                v.scalar_tensor_tensor(out=u(XN, L, C), in0=u(NR, L, C), scalar=1e12, in1=u(XG, L, C),
                                       op0=ALU.min, op1=ALU.mult).then_inc(xn_ready.sem, 1)
                dve.wait_ge(linv.sem, linv.at(b))
                v.tensor_tensor(u(XL, L, C), u(DD, L, C), u(NR, L, C), ALU.mult).then_inc(lnorm.sem, 1)
                dve.wait_ge(lnorm.sem, lnorm.at(b))
                v.tensor_scalar(u(XL, L, C), u(XL, L, C), one("ln0w"), one("ln0b"), ALU.mult, ALU.add)\
                    .then_inc(xl_ready.sem, 1)
                dve.wait_ge(xl_ready.sem, xl_ready.at(b))

                xl_img = image(u(XL, L, C))
                for t in range(TILES + 1):
                    if t < TILES:
                        p = t % 2
                        sims = PS[:, 2 * p:2 * p + 2, 0:KEYS // 2]
                        m8 = small(T_M8 + 8 * p, 128, 8)
                        alone(dve, (s_ready, s_ready.at(b, t + 1)), *([(z_ready, z_ready.at(b, t - 1))] if t >= 2 else []))
                        v.max(m8, sims).then_inc(m8_ready.sem, 1)
                        alone(dve, (m8_ready, m8_ready.at(b, t + 1)), *([(exp2_ready, exp2_ready.at(b, t - 1))] if t >= 2 else []))
                        v.match_replace(out=tb("rest", t).rearrange("p (a n) -> p a n", a=2), in_to_replace=m8,
                                        in_values=sims, imm_value=NEG).then_inc(rest_ready.sem, 1)
                    if t >= 1:
                        r = t - 1
                        i, j = divmod(r, NT_X)
                        dve.wait_ge(wt_psum.sem, wt_psum.at(b, r + 1))
                        if r >= 2:
                            dve.wait_ge(agg_psum.sem, agg_psum.at(b, r - 1))
                        v.tensor_copy(tb("wtsT", r, KC), PS[0:KC, 4:6, :].rearrange("p a n -> p (a n)")
                                      [:, 0:NKC * 128]).then_inc(wt_sb.sem, 1)
                    if t < TILES:
                        dve.wait_ge(z_ready.sem, z_ready.at(b, t + 1))
                        v.reciprocal(small(T_RZ + p, 128), small(T_Z + p, 128)).then_inc(rz_ready.sem, 1)
                        dve.wait_ge(rz_ready.sem, rz_ready.at(b, t + 1))
                        if t >= 2:
                            dve.wait_ge(wt_psum.sem, wt_psum.at(b, t - 1))
                        v.tensor_scalar(tb("diag", t), w("ident"), small(T_RZ + p, 128), None, ALU.mult)\
                            .then_inc(diag_ready.sem, 1)
                    if t >= 1:
                        dve.wait_ge(agg_psum.sem, agg_psum.at(b, r + 1))
                        dst = xl_img[:, TQ_Y * i:TQ_Y * (i + 1), TQ_X * j:TQ_X * (j + 1)]
                        v.tensor_tensor(dst, dst, PS[0:C, 7, 0:128].rearrange("p (h w) -> p h w", w=TQ_X),
                                        ALU.add).then_inc(enh_ready.sem, 1)

                dve.wait_ge(enh_ready.sem, enh_ready.at(b))
                dve.wait_ge(ffn_psum.sem, ffn_psum.at(b))
                v.scalar_tensor_tensor(out=chunked(X1[:, :]), in0=ps6(C), scalar=one("b2"), in1=chunked(u(XL, L, C)),
                                       op0=ALU.add, op1=ALU.add).then_inc(x1_part.sem, 1)
                dve.wait_ge(x1_part.sem, x1_part.at(b))
                v.tensor_tensor(X1[:, :], X1[:, :], X0, ALU.add).then_inc(x1_ready.sem, 1)
                dve.wait_ge(x1_ready.sem, x1_ready.at(b))

                def diagonals(at, weights, done):
                    v.tensor_tensor(u(at, 9 * 128).rearrange("p (k m) -> p k m", k=9),
                                    w("ident").unsqueeze(1).broadcast_to([128, 9, 128]),
                                    weights.unsqueeze(2).broadcast_to([128, 9, 128]), ALU.mult)\
                        .then_inc(done.sem, 1)

                def depthwise(acc, pad, weights, lo, tap, done):
                    pv = pad.rearrange("p (h w) -> p h w", w=PADW)
                    for k in range(9):
                        src, wk = pv[:, k // 3:k // 3 + H, k % 3:k % 3 + W], weights[:, k:k + 1]
                        if k == 0:
                            v.tensor_scalar(image(acc), src, wk, None, ALU.mult).then_inc(tap.sem, 1)
                        else:
                            dve.wait_ge(tap.sem, tap.at(b, lo + k))
                            v.scalar_tensor_tensor(out=image(acc), in0=src, scalar=wk, in1=image(acc),
                                                   op0=ALU.mult, op1=ALU.add)\
                                .then_inc(tap.sem if k < 8 else done.sem, 1)

                group_norm(1, X1[:, :], u(FG, L, C))
                diagonals(FDIAG, w("convw", 128, 0, 9), fdiag)
                dve.wait_ge(xi_pad.sem, xi_pad.at(b, 2))
                depthwise(u(ACC), u(PAD[1], PADN), w("convw", 128, 9, 9), 0, ftap, fconv)
                for k in range(4):
                    dve.wait_ge(hi_ready.sem, hi_ready.at(b, k + 1))
                    if k >= 1:
                        dve.wait_ge(mid_ready.sem, mid_ready.at(b, k))
                        dve.wait_ge(lo_ready.sem, lo_ready.at(b, k))
                    v.tensor_tensor(chunked(u(R1, L, 96)), ps6(96), chunked(PBC[:, k, :]), ALU.subtract)\
                        .then_inc(r1_ready.sem, 1)
                    dve.wait_ge(mid_ready.sem, mid_ready.at(b, k + 1))
                    dve.wait_ge(r1_ready.sem, r1_ready.at(b, k + 1))
                    v.tensor_tensor(PBC[64:96, k, :], U[64:96, R1:R1 + L], mid[64:96, :], ALU.subtract)\
                        .then_inc(lo_ready.sem, 1)

                def log1p(q):
                    dve.wait_ge(sp_cubic.sem, sp_cubic.at(b, q + 1))
                    dve.wait_ge(sp_ln.sem, sp_ln.at(b, q + 1))
                    v.scalar_tensor_tensor(out=TL[:, :], in0=TL[:, :], scalar=LOG_MARGIN, in1=TW[:, :],
                                           op0=ALU.add, op1=ALU.min).then_inc(sp_log1p.sem, 1)

                def dlt_and_cumsum(q):
                    p = q % 2
                    dve.wait_ge(sp_log1p.sem, sp_log1p.at(b, q + 1))
                    v.scalar_tensor_tensor(out=u(DL[p]), in0=u(DL[p]), scalar=0.0, in1=TL[:, :],
                                           op0=ALU.max, op1=ALU.add).then_inc(dlt_ready.sem, 1)
                    dve.wait_ge(dlt_ready.sem, dlt_ready.at(b, q + 1))
                    d, o = u(DL[p]), u(CS[p])
                    if q % 2:
                        d, o = d[:, ::-1], o[:, ::-1]
                    v.tensor_tensor_scan(o, d, d, 0.0, ALU.add, ALU.max).then_inc(cs_ready.sem, 1)

                def y_run(r):
                    at = piece_at(r)
                    dve.wait_ge(y_added.sem, b * PIECES + (r + 1) * NSTATE + RING)
                    if r // 3 % 2 == 0:
                        v.tensor_copy(u(YS + at, PC), two_banks(Y_BANK)).then_inc(y_out.sem, 1)
                    else:
                        dve.wait_ge(y_out.sem, y_out.at(b, 3 * (r // 3)))
                        v.tensor_tensor(XS[r // 6][:, at:at + PC], u(YS + at, PC), two_banks(Y_BANK), ALU.add)\
                            .then_inc(y_out.sem, 1)

                log1p(0)
                dlt_and_cumsum(0)
                for r in range(RUNS):
                    q, i = divmod(r, 3)
                    for n in range(NSTATE):
                        t = r * NSTATE + n
                        gk, ak = u(G[n % RING], PC), u(A[n % RING], PC)
                        dve.wait_ge(gu_ready.sem, gu_ready.at(b, t + 1))
                        dve.wait_ge(b_full.sem, b_full.at(b, t + 1))
                        v.tensor_tensor(gk, gk, two_banks(B_BANK), ALU.mult).then_inc(b_used.sem, 1)
                        dve.wait_ge(b_used.sem, b_used.at(b, t + 1))
                        dve.wait_ge(a_ready.sem, a_ready.at(b, t + 1))
                        if i > 0:
                            dve.wait_ge(carried.sem, b * PIECES + t - NSTATE + 1 + RING)
                        hk, dk = (gk[:, ::-1], ak[:, ::-1]) if q % 2 else (gk, ak)
                        v.tensor_tensor_scan(hk, dk, hk, CARRY[:, n:n + 1] if i > 0 else 0.0, ALU.mult, ALU.add)\
                            .then_inc(scanned.sem, 1)
                        if n == 0 and r >= 1:
                            y_run(r - 1)
                        dve.wait_ge(scanned.sem, scanned.at(b, t + 1))
                        dve.wait_ge(c_full.sem, c_full.at(b, t + 1))
                        v.tensor_tensor(ak, gk, two_banks(C_BANK[t % 2]), ALU.mult).then_inc(ch_ready.sem, 1)
                        if q + 1 < QS and i == 1 and n == NSTATE // 2:
                            log1p(q + 1)
                    if q + 1 < QS and i == 1:
                        dlt_and_cumsum(q + 1)
                y_run(RUNS - 1)

                dve.wait_ge(ys_psum.sem, ys_psum.at(b, 1))
                v.tensor_scalar(u(ZG, L, C), X1[:, :], small(MG + 1), small(RSTD + 1), ALU.subtract, ALU.mult)\
                    .then_inc(zg_ready.sem, 1)
                diagonals(BDIAG, w("c2w", 128, 18, 9), bdiag)
                dve.wait_ge(ymu_psum.sem, ymu_psum.at(b))
                v.tensor_tensor(chunked(u(YA)), chunked(u(YA)), ps6(128), ALU.subtract).then_inc(yd_ready.sem, 1)
                v.tensor_tensor(chunked(u(YB, L, 64)), chunked(u(YB, L, 64)), ps6(64), ALU.subtract)\
                    .then_inc(yd_ready.sem, 1)
                dve.wait_ge(yinv.sem, yinv.at(b))
                parts = ((YA, 128, 0), (YB, 64, 1))
                for at, rows, k in parts:
                    v.scalar_tensor_tensor(out=u(at, L, rows), in0=u(at, L, rows), scalar=one("lng", rows, k),
                                           in1=u(SD, L, rows), op0=ALU.mult, op1=ALU.mult).then_inc(yunit.sem, 1)
                for at, rows, k in parts:
                    dve.wait_ge(yunit.sem, yunit.at(b, k + 1))
                    dve.wait_ge(z_psum.sem, z_psum.at(b, k + 1))
                    v.scalar_tensor_tensor(out=chunked(u(at, L, rows)), in0=chunked(u(at, L, rows)),
                                           scalar=one("lnb", rows, k), in1=ps6(rows), op0=ALU.add, op1=ALU.mult)\
                        .then_inc(u_ready.sem, 1)
                for k in range(2):
                    dve.wait_ge(c1_pad.sem, c1_pad.at(b, k + 1))
                    depthwise(u(MIX[k]), u(PAD2[k], PADN), w("c2w", 128, 9 * k, 9), 8 * k, btap, bconv)
                dve.wait_ge(se2_ready.sem, se2_ready.at(b))
                v.tensor_scalar(small(SE2), small(SE2), 1.0, None, ALU.add).then_inc(se_plus.sem, 1)
                dve.wait_ge(se_plus.sem, se_plus.at(b))
                v.scalar_tensor_tensor(out=u(OUT, L, C), in0=u(T3, L, C), scalar=small(SE2), in1=X1[:, :],
                                       op0=ALU.mult, op1=ALU.add).then_inc(out_ready.sem, 1)


def kernel(**inputs):
    import numpy as np
    import ml_dtypes
    import concourse.bacc as bacc
    from concourse import mybir
    from concourse.bass_utils import run_bass_kernel_spmd

    a = {k: np.ascontiguousarray(v) for k, v in inputs.items()}
    l0 = {k[8:]: v for k, v in a.items() if k.startswith("L0_conv_")}
    l1 = {k[8:]: v for k, v in a.items() if k.startswith("L1_conv_")}

    pk = np.zeros((128, PWIDTH), np.float32)

    def put(table, arr, name, value, lo=0, row=0):
        value = value.reshape(value.shape[0], -1)
        at, width = table[name]
        assert lo + value.shape[1] <= width
        arr[row:row + value.shape[0], at + lo:at + lo + value.shape[1]] = value

    def P(name, value, lo=0, row=0):
        put(PCOL, pk, name, value, lo, row)

    P("ident", np.eye(128, dtype=np.float32))
    same = (np.arange(C)[:, None] // 3 == np.arange(C)[None, :] // 3)
    P("gmean", np.where(same, np.float32(1 / 3), np.float32(0)))
    P("mean96", np.full((C, C), 1 / 96, np.float32))
    P("sum96", np.ones((C, C), np.float32))
    P("mean192", np.full((128, 128), 1 / 192, np.float32))
    P("w1", l0["w1"].T)
    P("w2", l0["w2"][:, 0:C].T)
    P("w2", l0["w2"][:, C:2 * C].T, C)
    ip = l1["in_proj_w"]
    P("in_a", ip[0:128].T)
    P("in_b", ip[128:192].T)
    P("in_b", ip[128:192].T, 64)
    P("z_a", ip[E:E + 128].T)
    P("z_b", ip[E + 128:2 * E].T)
    for s in range(2):
        for i, k in enumerate((s, 2 + s)):
            wt = l1["dt_proj_w"][k].T
            row = 32 * s + RANK * i
            P("dtw", wt[:, 0:128], i * 128, row)
            P("dtw", wt[:, 128:192], 256 + 64 * i, row)
    P("b1", l0["b1"].reshape(2, C).T)
    P("b2", l0["b2"][:, None])
    P("ln0w", l0["ln_w"][:, None])
    P("ln0b", l0["ln_b"][:, None])
    cw = l1["conv_w"].reshape(E, 9)
    P("convw", cw[0:128])
    P("convw", cw[128:192], 9)
    P("convw", cw[128:192], 9, 64)
    P("convb", l1["conv_b"][0:128, None])
    P("convb", l1["conv_b"][128:192, None], 1)
    P("convb", l1["conv_b"][128:192, None], 1, 64)
    for s in range(2):
        for i, k in enumerate((s, 2 + s)):
            P("dtb", l1["dt_proj_b"][k, 0:128, None], i * 2 + s)
            P("dtb", l1["dt_proj_b"][k, 128:192, None], 4 + s, 64 * i)
            P("alog", l1["A_log"][k, 0:128], (i * 2 + s) * NSTATE)
            P("alog", l1["A_log"][k, 128:192], (4 + s) * NSTATE, 64 * i)
    P("ds", l1["Ds"][:, 0:128].T)
    P("ds", l1["Ds"][:, 128:192].T, 4)
    for name, src in (("lng", "ln_g"), ("lnb", "ln_b")):
        P(name, l1[src][0:128, None])
        P(name, l1[src][128:192, None], 1)
    for name, src in (("c1b", "c1_b"), ("bn1g", "bn1_g"), ("bn1b", "bn1_b"), ("bn1m", "bn1_m"), ("bn1v", "bn1_v"),
                      ("c2b", "c2_b"), ("bn2g", "bn2_g"), ("bn2b", "bn2_b"), ("bn2m", "bn2_m"), ("bn2v", "bn2_v")):
        P(name, l1[src].reshape(3, 128).T)
    P("c2w", l1["c2_w"].reshape(3, 128, 9).transpose(1, 0, 2))
    P("c3b", l1["c3_b"][:, None])
    P("se1b", l1["se1_b"][:, None])
    P("se2b", l1["se2_b"][:, None])

    bk = np.zeros((128, BWIDTH), np.float32)
    c1 = l1["c1_w"].reshape(2 * E, E).T
    put(BCOL, bk, "c1a", c1[0:128])
    put(BCOL, bk, "c1bm", c1[128:192])
    put(BCOL, bk, "c3", l1["c3_w"].reshape(C, 3, 128).transpose(2, 1, 0))
    put(BCOL, bk, "se1", l1["se1_w"].T)
    put(BCOL, bk, "se2", l1["se2_w"].T)

    xp = np.zeros((128, 3, 4, XPM), np.float32)
    for s in range(2):
        for i, k in enumerate((s, 2 + s)):
            wt = l1["x_proj_w"][k].T
            for bc in range(2):
                cols = wt[:, RANK + NSTATE * bc:RANK + NSTATE * (bc + 1)]
                places = [(32 * r + 16 * i, cols) for r in range(3)]
                if bc == 0:
                    places.append((96 + RANK * i, wt[:, 0:RANK]))
                for at, part in places:
                    xp[:, i, 2 * s + bc, at:at + part.shape[1]] = part[0:128]
                    xp[64 * i:64 * i + 64, 2, 2 * s + bc, at:at + part.shape[1]] = part[128:192]

    sel = np.zeros((96, 3, NSTATE, 128), np.float32)
    for r in range(3):
        for n in range(NSTATE):
            sel[32 * r + n, 0, n, :] = 1
            sel[32 * r + 16 + n, 1, n, :] = 1
            sel[32 * r + n, 2, n, 0:64] = 1
            sel[32 * r + 16 + n, 2, n, 64:128] = 1
    mq = np.zeros((24, 128), np.float32)
    for y in range(TQ_Y):
        for xx in range(TQ_X):
            mq[y, y * TQ_X + xx] = 1
            mq[TQ_Y + xx, y * TQ_X + xx] = 1
    mk = np.zeros((24, 3, 3, KEY_Y, KEY_X), np.float32)
    tiles_y, tiles_x = (0, 1, NT_Y - 1), (0, 1, NT_X - 1)
    for a_, i in enumerate(tiles_y):
        for b_, j in enumerate(tiles_x):
            ky, kx = key_origin(i, j)
            for y in range(TQ_Y):
                far = np.abs(ky + np.arange(KEY_Y) - (TQ_Y * i + y)) > HALF_WIN
                mk[y, a_, b_][far, :] = -1024
            for xx in range(TQ_X):
                far = np.abs(kx + np.arange(KEY_X) - (TQ_X * j + xx)) > HALF_WIN
                mk[TQ_Y + xx, a_, b_][:, far] = -1024

    arrays = {
        "x": a["x"].reshape(BATCH * C, L), "pack": pk, "back": bk, "xpw": xp.reshape(128, XPW),
        "masks": mk.reshape(24, 9 * KEYS).astype(ml_dtypes.bfloat16), "maskq": mq.astype(ml_dtypes.bfloat16),
        "sels": sel.reshape(96, -1).astype(ml_dtypes.bfloat16),
    }
    nc = bacc.Bacc("TRN2", target_bir_lowering=False, num_devices=1)
    args = [nc.dram_tensor(f"in_{n}", v.shape, mybir.dt.from_np(v.dtype), kind="ExternalInput").ap()
            for n, v in arrays.items()]
    out = nc.dram_tensor("out", (BATCH * C, L), mybir.dt.float32, kind="ExternalOutput").ap()
    build(nc, *args, out)
    r = run_bass_kernel_spmd(nc, [{f"in_{n}": v for n, v in arrays.items()}], core_ids=[0])
    return r.results[0]["out"].reshape(BATCH, C, H, W)
```

```python
from contextlib import ExitStack

import concourse.bass as bass
from concourse import mybir

BATCH, C, H, W = 4, 96, 48, 48
L = H * W
E = 192
NSTATE = 16
RANK = 6
HALF_WIN = 6
ROWS = 8
CH = ROWS * W
NCH = L // CH
TQ_Y, TQ_X = 8, 16
KEY_Y, KEY_X = TQ_Y + 2 * HALF_WIN, TQ_X + 2 * HALF_WIN
KEYS = KEY_Y * KEY_X
KC = 4 * KEY_X
NKC = KEYS // KC
NT_Y, NT_X = H // TQ_Y, W // TQ_X
TILES = NT_Y * NT_X
PADW = W + 2
PADN = PADW * PADW
QS = 6
PC = L // 3
PC_CUTS = [(0, 512), (512, PC - 512)]
RUNS = 3 * QS
PIECES = RUNS * NSTATE
PASS = 3 * NSTATE
RING = 8
BLOCK = 4
Y_BANK, B_BANK, C_BANK = 0, 2, (4, 6)
DT_BANK = 6
DT_AT = (6, 10, 14)
CUBIC_AT, LOG1P_AT, CUMSUM_AT = 28, 32, 34
LN_1E12 = 27.631021115928547
CUB_SCALE = 3 ** -0.5
LOG_MARGIN = 6e-8
NEG = -1e30
XR = 2 * RANK


def key_origin(i, j):
    return (min(max(TQ_Y * i - HALF_WIN, 0), H - KEY_Y), min(max(TQ_X * j - HALF_WIN, 0), W - KEY_X))


def kind(i, n):
    return 0 if i == 0 else (2 if i == n - 1 else 1)


PACK = [("ident", 128), ("gmean", C), ("mean96", C), ("sum96", C), ("mean192", 128),
        ("w1", 2 * C), ("w2", 2 * C), ("in_a", 128), ("in_b", 128), ("z_a", 128), ("z_b", 64),
        ("dtw", 3 * 128), ("b1", 2), ("b2", 1), ("ln0w", 1), ("ln0b", 1),
        ("convw", 18), ("convb", 2), ("dtb", QS), ("alog", QS * NSTATE), ("ds", 8),
        ("lng", 2), ("lnb", 2), ("c1b", 3), ("bn1g", 3), ("bn1b", 3), ("bn1m", 3), ("bn1v", 3),
        ("c2w", 27), ("c2b", 3), ("bn2g", 3), ("bn2b", 3), ("bn2m", 3), ("bn2v", 3),
        ("c3b", 1), ("se1b", 1), ("se2b", 1)]
BACK = [("c1a", 2 * E), ("c1bm", 2 * E), ("c3", 3 * C), ("se1", E // 4), ("se2", E // 2)]


def columns(table):
    at, out = 0, {}
    for name, width in table:
        out[name] = (at, width)
        at += width
    return out, at


PCOL, PWIDTH = columns(PACK)
BCOL, BWIDTH = columns(BACK)
XPM = 96 + XR
XPW = 3 * 4 * XPM


class Signal:

    def __init__(self, ctx, nc, name, per=1):
        self.sem = ctx.enter_context(nc.semaphore(name))
        self.per = per

    def at(self, b, k=None):
        return b * self.per + (self.per if k is None else k)


def build(nc, x, pack, back, xpw, masks, maskq, sels, out):
    f32, bf16 = mybir.dt.float32, mybir.dt.bfloat16
    ALU, ACT, AX = mybir.AluOpType, mybir.ActivationFunctionType, mybir.AxisListType

    with ExitStack() as ctx:
        def sb(name, shape, dt=f32):
            return ctx.enter_context(nc.sbuf_tensor(name, shape, dt))

        def sig(name, per=1):
            return Signal(ctx, nc, name, per)

        PK = sb("packed_weights", [128, PWIDTH])
        SEL = sb("state_selectors", [96, 3 * NSTATE * 128], bf16)
        MQ = sb("window_query_rows", [24, 128], bf16)
        X1 = sb("x_after_layer0", [C, L])
        XS = [sb(f"scan_input_{g}", [128, L]) for g in range(3)]
        PBC = sb("b_c_split_rows", [96, 4, L], bf16)
        RD = sb("dt_rows", [32 + XR, L])
        U = sb("work", [128, 5 * L + 2 * RING * PC + L])
        TW = sb("softplus_w", [128, L])
        TL = sb("softplus_l", [128, L])
        SM = sb("small", [128, 128])
        CARRY = sb("scan_state", [128, NSTATE])
        NA = sb("neg_a", [128, QS * NSTATE])
        PS = ctx.enter_context(nc.psum_tensor("psum", [128, 8, 512], f32))

        def w(name, rows=128, lo=0, n=None):
            at, width = PCOL[name]
            return PK[0:rows, at + lo:at + lo + (width - lo if n is None else n)]

        def wb(name, rows=128, lo=0, n=None):
            at, width = BCOL[name]
            return TW[0:rows, at + lo:at + lo + (width - lo if n is None else n)]

        def u(at, width=L, rows=128):
            return U[0:rows, at:at + width]

        def two_banks(bank):
            return PS[:, bank:bank + 2, :].rearrange("p a n -> p (a n)")[:, 0:PC]

        def piece_at(r):
            q, i = divmod(r, 3)
            return (2 - i if q % 2 else i) * PC

        def chunked(ap):
            return ap.rearrange("p (a b) -> p a b", b=CH)

        def image(ap):
            return ap.rearrange("p (h w) -> p h w", w=W)

        def half(h):
            return slice(h * L // 2, (h + 1) * L // 2)

        def ps3(rows, h, lo=0):
            return PS[lo:lo + rows, 3 * h:3 * h + 3, 0:CH]

        def image_t(ap):
            return ap.rearrange("p (w h) -> p h w", h=H)

        def ps6(rows, lo=0):
            return PS[lo:lo + rows, 0:NCH, 0:CH]

        def ps_rows(rows, lo=0):
            return ps6(rows, lo).rearrange("p a (r w) -> p a r w", w=W)

        def interior(pad):
            v = pad.rearrange("p (h w) -> p h w", w=PADW)[:, 1:1 + H, 1:1 + W]
            return v.rearrange("p (a r) w -> p a r w", r=ROWS)

        def one(name, rows=C, at=0):
            return w(name, rows, at, 1)

        def small(k, rows=C, n=1):
            return SM[0:rows, k:k + n]

        BN_STATS = 0
        MV, VC, DM, MG, STD, RSTD = 36, 38, 39, 40, 42, 44
        T_M8, T_NM, T_E8, T_Z, T_RZ = 46, 62, 64, 80, 82
        S1, B1C, S2, B2C, DSUM = 84, 87, 90, 93, 96
        TSUM, TMEAN, SE1, SE2, LNC = 98, 99, 100, 101, 102
        CT = 104
        EPS5, ONE, CUBB, CUBC, LEAST = 120, 121, 122, 123, 124

        XG, XN, XL, SQ, NR, DD = (k * L for k in range(6))
        HID = [3 * L, 4 * L]
        at = 6 * L
        tile_at = {}
        for name, width in [("query", 128), ("keys", KEYS), ("rest", KEYS), ("exp", KEYS), ("wts", KEYS),
                            ("keysT", NKC * C), ("wtsT", NKC * 128), ("diag", 128)]:
            tile_at[name] = (at, width)
            at += 2 * width
        assert at <= 11 * L

        def tb(name, t, rows=128):
            a, width = tile_at[name]
            return u(a + (t % 2) * width, width, rows)

        MK = PBC[0:24, 0:3, :].rearrange("p a n -> p (a n)")[:, 0:9 * KEYS]
        X0 = XS[0][0:C, :]

        FG = 0
        PAD = [L, L + PADN]
        FDIAG = L + 2 * PADN
        ACC = FDIAG + 9 * 128
        R1 = 0
        T2 = ACC + L
        mid = u(T2, L // 2, 96).bitcast(bf16)

        G = [k * PC for k in range(RING)]
        A = [(RING + k) * PC for k in range(RING)]
        top = 2 * RING * PC
        DL = [top, top + L]
        CS = [top + 2 * L, top + 3 * L]
        UX = top + 4 * L
        YS = top + 5 * L
        XP = YS
        assert T2 + L // 2 <= top

        YA, YB, SA, SBQ, SD = (k * L for k in range(5))
        PAD2 = [5 * L + k * PADN for k in range(3)]
        ZG = PAD2[2] + PADN
        BDIAG = ZG + L
        assert BDIAG + 9 * 128 <= 6 * L + 2 * RING * PC
        MIX = [4 * L, 3 * L, 2 * L]
        T3, OUT = 0, L

        loaded = sig("weights_loaded")
        ready = sig("constants_ready")
        x_free = sig("x_plane_free")
        x_in, mask_in, xpw_in, back_in, stored = (sig(n) for n in
                                                  ("x_in", "masks_in", "xpw_in", "back_weights_in", "stored"))
        gn_stat, gn_mv, gn_mean, gn_mg, gn_dev, gn_vc, gn_var, gn_std, gn_rstd, xg_ready = (
            sig(n, p) for n, p in (("gn_stats", 2 * NCH), ("gn_channel", 2), ("gn_mean", 2), ("gn_mean_sb", 2),
                                   ("gn_dev", 2), ("gn_second", 2), ("gn_var", 2), ("gn_std", 2),
                                   ("gn_rstd", 2), ("gn_out", 2)))
        sq_ready, ssq_ready, nrm_ln, nrm_inv, xn_ready = (sig(n) for n in (
            "squares", "norm2_psum", "norm_ln", "norm_inv", "unit_vectors"))
        mu_ready, dev_ready, dsq_ready, lvar_ready, lvar_ln, linv, lnorm = (sig(n) for n in (
            "ln0_mean", "ln0_dev", "ln0_dev2", "ln0_var", "ln0_var_ln", "ln0_inv", "ln0_scaled"))
        q_ready, k_ready, s_ready, kt_psum, kt_sb, m8_ready, rest_ready, nm_ready, z_ready, exp_ready, exp2_ready, \
            wts_ready, rz_ready, diag_ready, wt_psum, wt_sb, agg_psum, enh_ready = (
                sig(n, TILES) for n in ("queries_copied", "keys_copied", "sims_psum", "keysT_psum", "keysT_sb",
                                        "top8", "rest_of_sims", "neg_max", "exp_sum", "exp_all", "exp_rest",
                                        "weights", "sum_inv", "diag_ready", "weightsT_psum", "weightsT_sb",
                                        "agg_psum", "enhanced"))
        hid_psum, hid_ready, ffn_psum, x1_part, x1_ready = (sig(n, p) for n, p in (
            ("hidden_psum", 4), ("hidden", 4), ("ffn_psum", 2), ("x1_partial", 1), ("x1", 1)))
        pad_zero, fdiag, xi_psum, xi_pad, conv_psum, xs_ready = (sig(n, p) for n, p in (
            ("pads_zero", 1), ("conv_diag", 1), ("xi_psum", 4), ("xi_padded", 4), ("conv_psum", 1),
            ("scan_inputs", 4)))
        xp_psum, hi_ready, r1_ready, mid_ready, mid_placed, lo_ready, rd_ready = (sig(n, p) for n, p in (
            ("x_proj_psum", 8), ("split_hi", 8), ("split_rest", 8), ("split_mid", 8), ("split_mid_placed", 8),
            ("split_lo", 8), ("dt_rows_ready", 4)))
        dt_psum, dt_sb, sp_abs, sp_exp, sp_square, sp_ln, sp_quad, sp_cubic, sp_log1p, dlt_ready, cs_ready, \
            ux_ready = (sig(n, p) for n, p in (
                ("dt_psum", QS * 3), ("dt_raw", QS * 3), ("softplus_abs", QS), ("softplus_exp", QS),
                ("softplus_square", QS), ("softplus_ln", QS), ("softplus_quadratic", QS), ("softplus_cubic", QS),
                ("softplus_log1p", QS), ("dlt", QS), ("dlt_cumsum", QS), ("dlt_x", QS)))
        a_ready, g_ready, gu_ready, b_full, b_used, scanned, carried, c_full, ch_ready, y_added = (
            sig(n, PIECES) for n in ("decay", "guard", "guard_dlt_x", "b_in_psum", "b_used", "scanned",
                                     "state_saved", "c_in_psum", "c_h", "y_added"))
        y_out = sig("y_run_out", RUNS)
        ys_psum, ys_sb, ymu_psum, yd_ready, ysq_ready, yvar_psum, yvar_ln, yinv, yunit = (
            sig(n, p) for n, p in (("ys_psum", 2), ("ys", 2), ("y_mean", 1), ("y_dev", 2), ("y_dev2", 2),
                                   ("y_var", 1), ("y_var_ln", 1), ("y_inv", 1), ("y_unit", 2)))
        zg_ready, z_psum, u_ready, pad2_zero, bdiag, c1_psum, c1_pad, c2_psum, mix_ready, c3_psum, t3_ready = (
            sig(n, p) for n, p in (("z_input", 1), ("z_psum", 2), ("gated", 2), ("pads2_zero", 1),
                                   ("conv2_diag", 1), ("c1_psum", 6), ("c1_padded", 6), ("c2_psum", 2),
                                   ("c2_out", 4), ("c3_psum", 2), ("c3_out", 1)))
        ftap, btap = sig("conv_taps", 8), sig("conv2_taps", 16)
        fconv, bconv = sig("conv_sum", 1), sig("conv2_sum", 2)
        tmean, se1_psum, se1_ready, se2_psum, se2_ready, se_plus, out_ready = (sig(n) for n in (
            "t_mean", "se1_psum", "se1_out", "se2_psum", "se2_out", "se_factor", "out_ready"))
        settled = {e.engine: sig(f"settled_{k}") for k, e in
                   enumerate((nc.sync, nc.gpsimd, nc.scalar, nc.vector))}
        setup_v, setup_a = sig("setup_vector"), sig("setup_scalar")

        LOADS = 3 * 16
        CONSTS = 2

        def alone(eng, *waits):
            for signal, count in waits:
                eng.wait_ge(signal.sem, count)
            eng.sem_inc(settled[eng.engine].sem, 1)

        block = ctx.enter_context(nc.Block())

        @block.sync
        def _(sp):
            sp.dma_start(PK[:, :], pack).then_inc(loaded.sem, 16)
            sp.dma_start(SEL[:, :], sels).then_inc(loaded.sem, 16)
            sp.dma_start(MQ[:, :], maskq).then_inc(loaded.sem, 16)
            with sp.Fori(0, BATCH) as b:
                alone(sp, (x_free, x_free.at(b)))
                sp.dma_start(X0, x[bass.ds(b * C, C), :]).then_inc(x_in.sem, 16)
                sp.dma_start(MK, masks).then_inc(mask_in.sem, 16)
                sp.wait_ge(x1_ready.sem, x1_ready.at(b))
                sp.dma_start(u(XP, XPW), xpw).then_inc(xpw_in.sem, 16)
                sp.wait_ge(y_out.sem, y_out.at(b))
                sp.dma_start(TW[:, 0:BWIDTH], back).then_inc(back_in.sem, 16)
                sp.wait_ge(ys_psum.sem, ys_psum.at(b))
                sp.sem_inc(x_free.sem, 1)
            sp.wait_ge(stored.sem, 16 * (BATCH + 1))

        @block.gpsimd
        def _(pool):
            pool.sem_inc(x_free.sem, 1)
            pool.sem_inc(stored.sem, 16)
            pool.sem_inc(carried.sem, RING)
            pool.sem_inc(y_added.sem, RING)
            pool.sem_inc(ready.sem, 1)
            with pool.Fori(0, BATCH) as b:
                xn_img, xg_img = image(u(XN, L, C)), image(u(XG, L, C))

                def copies(t):
                    i, j = divmod(t, NT_X)
                    ky, kx = key_origin(i, j)
                    alone(pool, *([(kt_psum, kt_psum.at(b, t - 1))] if t >= 2 else []))
                    nc.gpsimd.tensor_copy(tb("query", t, C).rearrange("p (h w) -> p h w", w=TQ_X),
                                          xn_img[:, TQ_Y * i:TQ_Y * (i + 1), TQ_X * j:TQ_X * (j + 1)])\
                        .then_inc(q_ready.sem, 1)
                    nc.gpsimd.tensor_copy(tb("keys", t, C).rearrange("p (h w) -> p h w", w=KEY_X),
                                          xg_img[:, ky:ky + KEY_Y, kx:kx + KEY_X]).then_inc(k_ready.sem, 1)

                pool.wait_ge(xn_ready.sem, xn_ready.at(b))
                copies(0)
                for t in range(TILES):
                    if t + 1 < TILES:
                        copies(t + 1)
                    pool.wait_ge(exp2_ready.sem, exp2_ready.at(b, t + 1))
                    nc.gpsimd.tensor_tensor(tb("wts", t), tb("exp", t), tb("wts", t), ALU.subtract)\
                        .then_inc(wts_ready.sem, 1)
                alone(pool, (x1_ready, x1_ready.at(b)))
                nc.gpsimd.memset(u(PAD[0], 2 * PADN), 0.0).then_inc(pad_zero.sem, 1)
                def cubic(q):
                    pool.wait_ge(sp_quad.sem, sp_quad.at(b, q + 1))
                    nc.gpsimd.tensor_tensor(TW[:, :], TW[:, :], u(CS[q % 2]), ALU.mult).then_inc(sp_cubic.sem, 1)

                def save_state(r, n):
                    q, i = divmod(r, 3)
                    t = b * PIECES + r * NSTATE + n
                    k = n % RING
                    alone(pool, (scanned, t + 1))
                    last = G[k] + (0 if q % 2 else PC - 1)
                    nc.gpsimd.tensor_copy(CARRY[:, n:n + 1], U[:, last:last + 1]).then_inc(carried.sem, 1)

                cubic(0)
                pending = []
                for r in range(RUNS):
                    q, i = divmod(r, 3)
                    if i == 0:
                        pool.wait_ge(dlt_ready.sem, dlt_ready.at(b, q + 1))
                        if q >= 1:
                            pool.wait_ge(gu_ready.sem, gu_ready.at(b, r * NSTATE))
                        nc.gpsimd.tensor_tensor(u(UX), u(DL[q % 2]), XS[q // 2][:, :], ALU.mult)\
                            .then_inc(ux_ready.sem, 1)
                        pool.wait_ge(ux_ready.sem, ux_ready.at(b, q + 1))
                    at = piece_at(r)
                    for n in range(NSTATE):
                        t = b * PIECES + r * NSTATE + n
                        if q + 1 < QS and i * NSTATE + n == CUBIC_AT:
                            cubic(q + 1)
                        pool.wait_ge(g_ready.sem, t + 1)
                        gk = u(G[n % RING], PC)
                        nc.gpsimd.tensor_tensor(gk, gk, u(UX + at, PC), ALU.mult).then_inc(gu_ready.sem, 1)
                        pending.append((r, n))
                        if len(pending) > 3:
                            save_state(*pending.pop(0))
                for r, n in pending:
                    save_state(r, n)
                alone(pool, (ys_psum, ys_psum.at(b, 1)))
                nc.gpsimd.memset(u(PAD2[0], 3 * PADN), 0.0).then_inc(pad2_zero.sem, 1)

        @block.scalar
        def _(act):
            f = nc.scalar.activation
            act.wait_ge(loaded.sem, LOADS)
            act.wait_ge(setup_v.sem, 1)
            f(small(CT, 128, 3), w("bn1v"), ACT.Sqrt, bias=small(EPS5, 128)).then_inc(setup_a.sem, 1)
            f(small(CT + 3, 128, 3), w("bn2v"), ACT.Sqrt, bias=small(EPS5, 128)).then_inc(setup_a.sem, 1)
            f(NA[:, :], w("alog"), ACT.Copy, scale=-1.0).then_inc(setup_a.sem, 1)
            act.wait_ge(ready.sem, CONSTS)
            act.wait_ge(setup_a.sem, 3)

            with act.Fori(0, BATCH) as b:
                def group_norm(l):
                    act.wait_ge(gn_var.sem, gn_var.at(b, l + 1))
                    f(small(STD), PS[0:C, 7, 1:2], ACT.Sqrt, bias=small(EPS5)).then_inc(gn_std.sem, 1)

                def inverse_root(dst, src, bias, ln, done):
                    f(chunked(dst), src, ACT.Ln, bias=bias).then_inc(ln.sem, 1)
                    act.wait_ge(ln.sem, ln.at(b))
                    f(dst, dst, ACT.Exp, scale=-0.5).then_inc(done.sem, 1)

                group_norm(0)
                act.wait_ge(xg_ready.sem, xg_ready.at(b, 1))
                f(u(SQ, L, C), u(XG, L, C), ACT.Square).then_inc(sq_ready.sem, 1)
                act.wait_ge(ssq_ready.sem, ssq_ready.at(b))
                inverse_root(u(NR, L, C), ps6(C), small(LEAST), nrm_ln, nrm_inv)
                act.wait_ge(dev_ready.sem, dev_ready.at(b))
                f(u(SQ, L, C), u(DD, L, C), ACT.Square).then_inc(dsq_ready.sem, 1)
                act.wait_ge(lvar_ready.sem, lvar_ready.at(b))
                act.wait_ge(xn_ready.sem, xn_ready.at(b))
                inverse_root(u(NR, L, C), ps6(C), small(EPS5), lvar_ln, linv)

                for t in range(TILES):
                    p = t % 2
                    m8, nm = small(T_M8 + 8 * p, 128, 8), small(T_NM + p, 128)
                    act.wait_ge(m8_ready.sem, m8_ready.at(b, t + 1))
                    f(nm, m8[:, 0:1], ACT.Copy, scale=-1.0).then_inc(nm_ready.sem, 1)
                    act.wait_ge(nm_ready.sem, nm_ready.at(b, t + 1))
                    if t >= 2:
                        act.wait_ge(rz_ready.sem, rz_ready.at(b, t - 1))
                    f(small(T_E8 + 8 * p, 128, 8), m8, ACT.Exp, bias=nm,
                      accum_out=small(T_Z + p, 128)).then_inc(z_ready.sem, 1)
                    act.wait_ge(rest_ready.sem, rest_ready.at(b, t + 1))
                    if t >= 2:
                        act.wait_ge(wts_ready.sem, wts_ready.at(b, t - 1))
                    f(tb("exp", t).rearrange("p (a n) -> p a n", a=2), PS[:, 2 * p:2 * p + 2, 0:KEYS // 2],
                      ACT.Exp, bias=nm).then_inc(exp_ready.sem, 1)
                    if t >= 2:
                        act.wait_ge(wt_psum.sem, wt_psum.at(b, t - 1))
                    f(tb("wts", t), tb("rest", t), ACT.Exp, bias=nm).then_inc(exp2_ready.sem, 1)
                    act.wait_ge(kt_psum.sem, kt_psum.at(b, t + 1))
                    if t >= 2:
                        act.wait_ge(agg_psum.sem, agg_psum.at(b, t - 1))
                    f(tb("keysT", t, KC), PS[0:KC, 6, 0:NKC * C], ACT.Copy).then_inc(kt_sb.sem, 1)

                for k in range(2):
                    for h in range(2):
                        act.wait_ge(hid_psum.sem, hid_psum.at(b, 2 * k + h + 1))
                        f(chunked(u(HID[k] + h * L // 2, L // 2, C)), ps3(C, h), ACT.Relu, bias=one("b1", C, k))\
                            .then_inc(hid_ready.sem, 1)

                group_norm(1)
                act.wait_ge(pad_zero.sem, pad_zero.at(b))
                for k in range(2):
                    for h in range(2):
                        act.wait_ge(xi_psum.sem, xi_psum.at(b, 2 * k + h + 1))
                        f(interior(u(PAD[k], PADN))[:, 3 * h:3 * h + 3], ps_rows(128)[:, 3 * h:3 * h + 3],
                          ACT.Copy).then_inc(xi_pad.sem, 1)
                act.wait_ge(fconv.sem, fconv.at(b))
                f(XS[2][0:64, :], u(ACC, L, 64), ACT.Silu, bias=one("convb", 64, 1)).then_inc(xs_ready.sem, 1)
                f(image_t(XS[2][64:128, :]), image(U[64:128, ACC:ACC + L]), ACT.Silu,
                  bias=PK[64:128, PCOL["convb"][0] + 1:PCOL["convb"][0] + 2]).then_inc(xs_ready.sem, 1)
                act.wait_ge(conv_psum.sem, conv_psum.at(b))
                f(chunked(XS[0][:, :]), ps6(128), ACT.Silu, bias=one("convb", 128, 0)).then_inc(xs_ready.sem, 1)
                f(XS[1][:, :].rearrange("p (w a r) -> p a r w", a=NCH, r=ROWS), ps_rows(128), ACT.Silu,
                  bias=one("convb", 128, 0)).then_inc(xs_ready.sem, 1)
                def raw_dt(q, j, bank):
                    act.wait_ge(dt_psum.sem, dt_psum.at(b, q * 3 + j + 1))
                    f(u(DL[q % 2] + j * PC, PC), two_banks(bank), ACT.Identity,
                      bias=one("dtb", 128, q)).then_inc(dt_sb.sem, 1)

                def softplus_abs(q):
                    p = q % 2
                    act.wait_ge(dt_sb.sem, dt_sb.at(b, (q + 1) * 3))
                    if q >= 2:
                        act.wait_ge(cs_ready.sem, cs_ready.at(b, q - 1))
                    f(u(CS[p]), u(DL[p]), ACT.Abs).then_inc(sp_abs.sem, 1)

                def softplus_exp(q):
                    act.wait_ge(sp_abs.sem, sp_abs.at(b, q + 1))
                    f(u(CS[q % 2]), u(CS[q % 2]), ACT.Exp, scale=-1.0).then_inc(sp_exp.sem, 1)

                def softplus_square(q):
                    act.wait_ge(sp_exp.sem, sp_exp.at(b, q + 1))
                    if q >= 1:
                        act.wait_ge(dlt_ready.sem, dlt_ready.at(b, q))
                    f(TW[:, :], u(CS[q % 2]), ACT.Square, bias=small(CUBB, 128), scale=CUB_SCALE)\
                        .then_inc(sp_square.sem, 1)
                    act.wait_ge(sp_square.sem, sp_square.at(b, q + 1))
                    f(TW[:, :], TW[:, :], ACT.Identity, bias=small(CUBC, 128)).then_inc(sp_quad.sem, 1)

                def softplus_ln(q):
                    act.wait_ge(sp_exp.sem, sp_exp.at(b, q + 1))
                    f(TL[:, :], u(CS[q % 2]), ACT.Ln, bias=small(ONE, 128)).then_inc(sp_ln.sem, 1)

                for j in range(9):
                    if j < 8:
                        k, h = divmod(j, 2)
                        act.wait_ge(xp_psum.sem, xp_psum.at(b, j + 1))
                        f(chunked(PBC[:, k, half(h)]), ps3(96, h), ACT.Copy).then_inc(hi_ready.sem, 1)
                        if k % 2 == 0:
                            f(chunked(RD[16 * k:16 * k + XR, half(h)]), ps3(XR, h, 96), ACT.Copy)\
                                .then_inc(rd_ready.sem, 1)
                    if j >= 1:
                        k, h = divmod(j - 1, 2)
                        act.wait_ge(r1_ready.sem, r1_ready.at(b, j))
                        if j >= 3:
                            act.wait_ge(lo_ready.sem, lo_ready.at(b, j - 2))
                            act.wait_ge(mid_placed.sem, mid_placed.at(b, j - 2))
                        f(mid[:, half(h)], u(R1 + h * L // 2, L // 2, 96), ACT.Copy).then_inc(mid_ready.sem, 1)
                    if 2 <= j < 5:
                        raw_dt(0, j - 2, DT_BANK)
                    if j == 4:
                        softplus_abs(0)
                        softplus_exp(0)
                    if j == 5:
                        softplus_square(0)
                    if j == 6:
                        softplus_ln(0)

                act.wait_ge(lo_ready.sem, lo_ready.at(b))
                act.wait_ge(mid_placed.sem, mid_placed.at(b))
                for r in range(RUNS):
                    q, i = divmod(r, 3)
                    at = piece_at(r)
                    if i == 0:
                        act.wait_ge(dlt_ready.sem, dlt_ready.at(b, q + 1))
                        act.wait_ge(cs_ready.sem, cs_ready.at(b, q + 1))

                    def decay(n):
                        t = b * PIECES + r * NSTATE + n
                        act.wait_ge(y_added.sem, t + 1)
                        f(u(A[n % RING], PC), u(DL[q % 2] + at, PC), ACT.Exp,
                          scale=NA[:, q * NSTATE + n:q * NSTATE + n + 1]).then_inc(a_ready.sem, 1)

                    def guard(n):
                        t = b * PIECES + r * NSTATE + n
                        act.wait_ge(carried.sem, t + 1)
                        if r * NSTATE + n >= RING:
                            act.wait_ge(ch_ready.sem, ch_ready.at(b, r * NSTATE + n + 1 - RING))
                        f(u(G[n % RING], PC), u(CS[q % 2] + at, PC), ACT.Sigmoid,
                          scale=NA[:, q * NSTATE + n:q * NSTATE + n + 1], bias=small(LNC, 128))\
                            .then_inc(g_ready.sem, 1)

                    for block_no in range(NSTATE // BLOCK):
                        blk = i * NSTATE // BLOCK + block_no if q + 1 < QS else None
                        if blk == 6:
                            softplus_square(q + 1)
                        if blk == 7:
                            softplus_ln(q + 1)
                        parts = (guard, decay) if block_no % 2 == 0 else (decay, guard)
                        for part in parts:
                            for n in range(block_no * BLOCK, (block_no + 1) * BLOCK):
                                part(n)
                            if blk == 5 and part == decay:
                                softplus_exp(q + 1)
                        if blk in (2, 3, 4):
                            raw_dt(q + 1, blk - 2, C_BANK[1])
                        if blk == 4:
                            softplus_abs(q + 1)

                act.wait_ge(y_out.sem, y_out.at(b))
                act.wait_ge(carried.sem, carried.at(b) + RING)
                act.wait_ge(ys_psum.sem, ys_psum.at(b, 1))
                f(chunked(u(YA)), ps6(128), ACT.Identity, bias=small(DSUM, 128)).then_inc(ys_sb.sem, 1)
                act.wait_ge(ys_psum.sem, ys_psum.at(b, 2))
                f(chunked(u(YB, L, 64)), ps6(64), ACT.Identity, bias=small(DSUM + 1, 64)).then_inc(ys_sb.sem, 1)
                act.wait_ge(yd_ready.sem, yd_ready.at(b, 1))
                f(u(SA), u(YA), ACT.Square).then_inc(ysq_ready.sem, 1)
                act.wait_ge(yd_ready.sem, yd_ready.at(b, 2))
                f(u(SBQ, L, 64), u(YB, L, 64), ACT.Square).then_inc(ysq_ready.sem, 1)
                act.wait_ge(yvar_psum.sem, yvar_psum.at(b))
                inverse_root(u(SD), ps6(128), small(EPS5, 128), yvar_ln, yinv)
                act.wait_ge(pad2_zero.sem, pad2_zero.at(b))
                for k in range(3):
                    for h in range(2):
                        act.wait_ge(c1_psum.sem, c1_psum.at(b, 2 * k + h + 1))
                        f(interior(u(PAD2[k], PADN))[:, 3 * h:3 * h + 3], ps_rows(128)[:, 3 * h:3 * h + 3],
                          ACT.Relu, bias=small(B1C + k, 128), scale=small(S1 + k, 128)).then_inc(c1_pad.sem, 1)
                for k in range(2):
                    act.wait_ge(bconv.sem, bconv.at(b, k + 1))
                    f(u(MIX[k]), u(MIX[k]), ACT.Relu, bias=small(B2C + k, 128),
                      scale=small(S2 + k, 128)).then_inc(mix_ready.sem, 1)
                for h in range(2):
                    act.wait_ge(c2_psum.sem, c2_psum.at(b, h + 1))
                    f(chunked(u(MIX[2] + h * L // 2, L // 2)), ps3(128, h), ACT.Relu, bias=small(B2C + 2, 128),
                      scale=small(S2 + 2, 128)).then_inc(mix_ready.sem, 1)
                act.wait_ge(c3_psum.sem, c3_psum.at(b))
                f(chunked(u(T3, L, C)), ps6(C), ACT.Identity, bias=one("c3b"),
                  accum_out=small(TSUM)).then_inc(t3_ready.sem, 1)
                act.wait_ge(t3_ready.sem, t3_ready.at(b))
                f(small(TMEAN), small(TSUM), ACT.Copy, scale=1.0 / L).then_inc(tmean.sem, 1)
                act.wait_ge(se1_psum.sem, se1_psum.at(b))
                f(small(SE1, E // 4), PS[0:E // 4, 7, 2:3], ACT.Relu, bias=one("se1b", E // 4))\
                    .then_inc(se1_ready.sem, 1)
                act.wait_ge(se2_psum.sem, se2_psum.at(b))
                f(small(SE2), PS[0:C, 7, 3:4], ACT.Sigmoid, bias=one("se2b")).then_inc(se2_ready.sem, 1)
                alone(act, (out_ready, out_ready.at(b)))
                act.dma_start(out[bass.ds(b * C, C), :], u(OUT, L, C)).then_inc(stored.sem, 16)

        @block.tensor
        def _(pe):
            mm = nc.tensor.matmul
            ident = w("ident")
            pe.wait_ge(loaded.sem, LOADS)
            pe.wait_ge(ready.sem, CONSTS)

            def plane(lhs_rhs, rows, done, lo=0, halves=None):
                for c in range(NCH):
                    if halves is not None and c % 3 == 0:
                        if c == 3:
                            last.then_inc(done.sem, 1)
                        if halves:
                            signal, count = halves[c // 3]
                            pe.wait_ge(signal.sem, count)
                    for k, (lhs, rhs) in enumerate(lhs_rhs):
                        last = mm(PS[lo:lo + rows, c, 0:CH], lhs, rhs(c), start=(k == 0),
                                  stop=(k == len(lhs_rhs) - 1))
                last.then_inc(done.sem, 1)

            def cut(ap):
                return lambda c: ap[:, c * CH:(c + 1) * CH]

            def turned(ap):
                v = ap.rearrange("p (w h) -> p h w", h=H)
                return lambda c: v[:, c * ROWS:(c + 1) * ROWS, :]

            def taps(pad, diag):
                v = pad.rearrange("p (h w) -> p h w", w=PADW)
                return [(diag[:, k * 128:(k + 1) * 128],
                         lambda c, k=k: v[:, c * ROWS + k // 3:c * ROWS + k // 3 + ROWS, k % 3:k % 3 + W])
                        for k in range(9)]

            with pe.Fori(0, BATCH) as b:
                def group_norm(l):
                    pe.wait_ge(gn_mv.sem, gn_mv.at(b, l + 1))
                    mm(PS[0:C, 7, 0:1], w("gmean", C), small(MV), start=True, stop=True).then_inc(gn_mean.sem, 1)
                    pe.wait_ge(gn_vc.sem, gn_vc.at(b, l + 1))
                    mm(PS[0:C, 7, 1:2], w("gmean", C), small(VC), start=True, stop=True).then_inc(gn_var.sem, 1)

                group_norm(0)
                pe.wait_ge(sq_ready.sem, sq_ready.at(b))
                plane([(w("sum96", C), cut(u(SQ, L, C)))], C, ssq_ready)
                pe.wait_ge(nrm_ln.sem, nrm_ln.at(b))
                plane([(w("mean96", C), cut(u(XG, L, C)))], C, mu_ready)
                pe.wait_ge(dsq_ready.sem, dsq_ready.at(b))
                plane([(w("mean96", C), cut(u(SQ, L, C)))], C, lvar_ready)

                xn_img = image(u(XN, L, C))
                pe.wait_ge(mask_in.sem, b * 16 + 16)
                pe.wait_ge(lvar_ln.sem, lvar_ln.at(b))
                for t in range(TILES + 1):
                    if t < TILES:
                        i, j = divmod(t, NT_X)
                        ky, kx = key_origin(i, j)
                        mask = (kind(i, NT_Y) * 3 + kind(j, NT_X)) * KEYS
                        pe.wait_ge(k_ready.sem, k_ready.at(b, t + 1))
                        if t >= 2:
                            pe.wait_ge(exp_ready.sem, exp_ready.at(b, t - 1))
                            pe.wait_ge(rest_ready.sem, rest_ready.at(b, t - 1))
                        for hf in range(2):
                            sims = PS[:, 2 * (t % 2) + hf, 0:KEYS // 2]
                            mm(sims, tb("query", t, C),
                               xn_img[:, ky + 10 * hf:ky + 10 * hf + 10, kx:kx + KEY_X], start=True, stop=False)
                            last = mm(sims, MQ[:, :], MK[:, mask + hf * KEYS // 2:mask + (hf + 1) * KEYS // 2],
                                      start=False, stop=True)
                        last.then_inc(s_ready.sem, 1)
                    if t >= 1:
                        r = t - 1
                        pe.wait_ge(wts_ready.sem, wts_ready.at(b, r + 1))
                        pe.wait_ge(diag_ready.sem, diag_ready.at(b, r + 1))
                        if r >= 1:
                            pe.wait_ge(wt_sb.sem, wt_sb.at(b, r))
                        for k in range(NKC):
                            last = mm(PS[0:KC, 4 + k // 4, (k % 4) * 128:(k % 4) * 128 + 128],
                                      tb("wts", r)[:, k * KC:(k + 1) * KC], tb("diag", r), start=True, stop=True)
                        last.then_inc(wt_psum.sem, 1)
                    if t < TILES:
                        if t >= 1:
                            pe.wait_ge(kt_sb.sem, kt_sb.at(b, t))
                        for k in range(NKC):
                            last = nc.tensor.transpose(PS[0:KC, 6, k * C:(k + 1) * C],
                                                       tb("keys", t, C)[:, k * KC:(k + 1) * KC],
                                                       w("ident", C, 0, C))
                        last.then_inc(kt_psum.sem, 1)
                    if t >= 1:
                        pe.wait_ge(wt_sb.sem, wt_sb.at(b, r + 1))
                        pe.wait_ge(kt_sb.sem, kt_sb.at(b, r + 1))
                        if r >= 1:
                            pe.wait_ge(enh_ready.sem, enh_ready.at(b, r))
                        for k in range(NKC):
                            last = mm(PS[0:C, 7, 0:128], tb("keysT", r, KC)[:, k * C:(k + 1) * C],
                                      tb("wtsT", r, KC)[:, k * 128:(k + 1) * 128], start=(k == 0),
                                      stop=(k == NKC - 1))
                        last.then_inc(agg_psum.sem, 1)

                pe.wait_ge(enh_ready.sem, enh_ready.at(b))
                for k in range(2):
                    plane([(w("w1", C, k * C, C), cut(u(XL, L, C)))], C, hid_psum,
                          halves=[(hid_ready, hid_ready.at(b, h + 1)) for h in range(2)] if k else ())
                plane([(w("w2", C, k * C, C), cut(u(HID[k], L, C))) for k in range(2)], C, ffn_psum,
                      halves=[(hid_ready, hid_ready.at(b, h + 3)) for h in range(2)])

                group_norm(1)
                pe.wait_ge(xg_ready.sem, xg_ready.at(b, 2))
                plane([(w("in_a", C), cut(u(FG, L, C)))], 128, xi_psum, halves=())
                plane([(w("in_b", C), cut(u(FG, L, C)))], 128, xi_psum,
                      halves=[(xi_pad, xi_pad.at(b, h + 1)) for h in range(2)])
                pe.wait_ge(xi_pad.sem, xi_pad.at(b))
                pe.wait_ge(fdiag.sem, fdiag.at(b))
                plane(taps(u(PAD[0], PADN), u(FDIAG, 9 * 128)), 128, conv_psum)
                pe.wait_ge(xs_ready.sem, xs_ready.at(b, 4))
                pe.wait_ge(xpw_in.sem, b * 16 + 16)
                def dt_product(q, j, bank):
                    g, s = divmod(q, 2)
                    for c0, cw in PC_CUTS:
                        last = mm(PS[:, bank + c0 // 512, 0:cw],
                                  PK[32 * s:32 * s + XR, PCOL["dtw"][0] + g * 128:PCOL["dtw"][0] + (g + 1) * 128],
                                  RD[32 * s:32 * s + XR, j * PC + c0:j * PC + c0 + cw], start=True, stop=True)
                    last.then_inc(dt_psum.sem, 1)

                for j in range(8):
                    k, h = divmod(j, 2)
                    m = XPM if k % 2 == 0 else 96
                    if j >= 2:
                        pe.wait_ge(r1_ready.sem, r1_ready.at(b, j - 1))
                        if k % 2 == 1:
                            pe.wait_ge(rd_ready.sem, rd_ready.at(b, j - 1 if k == 1 else j - 3))
                    for c in range(3 * h, 3 * h + 3):
                        for g in range(3):
                            last = mm(PS[0:m, c, 0:CH], u(XP + (g * 4 + k) * XPM, m),
                                      XS[g][:, c * CH:(c + 1) * CH], start=(g == 0), stop=(g == 2))
                    last.then_inc(xp_psum.sem, 1)
                    if 2 <= j < 5:
                        if j == 2:
                            pe.wait_ge(rd_ready.sem, rd_ready.at(b, 2))
                        else:
                            pe.wait_ge(dt_sb.sem, dt_sb.at(b, j - 2))
                        dt_product(0, j - 2, DT_BANK)

                def broadcast(r, n, which, bank, done):
                    g, s = divmod(r // 3, 2)
                    at = piece_at(r)
                    for c0, cw in PC_CUTS:
                        last = mm(PS[:, bank + c0 // 512, 0:cw],
                                  SEL[:, (g * NSTATE + n) * 128:(g * NSTATE + n + 1) * 128],
                                  PBC[:, 2 * s + which, at + c0:at + c0 + cw], start=True, stop=True)
                    last.then_inc(done.sem, 1)

                pe.wait_ge(lo_ready.sem, lo_ready.at(b))
                pe.wait_ge(mid_placed.sem, mid_placed.at(b))
                pe.wait_ge(dt_sb.sem, dt_sb.at(b, 3))
                broadcast(0, 0, 0, B_BANK, b_full)
                broadcast(0, 0, 1, C_BANK[0], c_full)

                def add_y(t):
                    r, n = divmod(t, NSTATE)
                    pe.wait_ge(ch_ready.sem, ch_ready.at(b, t + 1))
                    if n == 0 and r >= 1:
                        pe.wait_ge(y_out.sem, y_out.at(b, r))
                    for c0, cw in PC_CUTS:
                        last = mm(PS[:, Y_BANK + c0 // 512, 0:cw], ident,
                                  u(A[n % RING] + c0, cw), start=(n == 0), stop=(n == NSTATE - 1),
                                  skip_group_check=True)
                    last.then_inc(y_added.sem, 1)

                late_c = None
                for t in range(PIECES - 1):
                    r, n = divmod(t, NSTATE)
                    q, i = divmod(r, 3)
                    r1, n1 = divmod(t + 1, NSTATE)
                    pe.wait_ge(b_used.sem, b_used.at(b, t + 1))
                    broadcast(r1, n1, 0, B_BANK, b_full)
                    if late_c:
                        piece, count = late_c
                        pe.wait_ge(dt_sb.sem, dt_sb.at(b, count))
                        broadcast(*divmod(piece, NSTATE), 1, C_BANK[piece % 2], c_full)
                        late_c = None
                    if t >= 1:
                        add_y(t - 1)
                    if q + 1 < QS and t % PASS in DT_AT:
                        j = DT_AT.index(t % PASS)
                        dt_product(q + 1, j, C_BANK[(n + 1) % 2])
                        late_c = (t + 1, (q + 1) * 3 + j + 1)
                    else:
                        broadcast(r1, n1, 1, C_BANK[(t + 1) % 2], c_full)
                add_y(PIECES - 2)
                add_y(PIECES - 1)

                pe.wait_ge(y_out.sem, y_out.at(b))
                plane([(ident, cut(XS[0][:, :])), (ident, turned(XS[1][:, :]))], 128, ys_psum)
                pe.wait_ge(ys_sb.sem, ys_sb.at(b, 1))
                plane([(ident[:, 0:64], cut(XS[2][:, :])), (ident[:, 64:128], turned(XS[2][:, :]))], 64, ys_psum)
                pe.wait_ge(ys_sb.sem, ys_sb.at(b, 2))
                plane([(w("mean192"), cut(u(YA))), (w("mean192", 64), cut(u(YB, L, 64)))], 128, ymu_psum)
                pe.wait_ge(yd_ready.sem, yd_ready.at(b))
                pe.wait_ge(ysq_ready.sem, ysq_ready.at(b))
                plane([(w("mean192"), cut(u(SA))), (w("mean192", 64), cut(u(SBQ, L, 64)))], 128, yvar_psum)
                pe.wait_ge(yvar_ln.sem, yvar_ln.at(b))
                pe.wait_ge(zg_ready.sem, zg_ready.at(b))
                plane([(w("z_a", C), cut(u(ZG, L, C)))], 128, z_psum)
                pe.wait_ge(u_ready.sem, u_ready.at(b, 1))
                plane([(w("z_b", C), cut(u(ZG, L, C)))], 64, z_psum)
                pe.wait_ge(u_ready.sem, u_ready.at(b, 2))
                pe.wait_ge(back_in.sem, b * 16 + 16)
                for k in range(3):
                    plane([(wb("c1a", 128, k * 128, 128), cut(u(YA))),
                           (wb("c1bm", 64, k * 128, 128), cut(u(YB, L, 64)))], 128, c1_psum,
                          halves=[(c1_pad, c1_pad.at(b, 2 * k + h - 1)) for h in range(2)] if k else ())
                pe.wait_ge(c1_pad.sem, c1_pad.at(b))
                pe.wait_ge(bdiag.sem, bdiag.at(b))
                plane(taps(u(PAD2[2], PADN), u(BDIAG, 9 * 128)), 128, c2_psum, halves=())
                plane([(wb("c3", 128, k * C, C), cut(u(MIX[k]))) for k in range(3)], C, c3_psum,
                      halves=[(mix_ready, mix_ready.at(b, h + 3)) for h in range(2)])
                pe.wait_ge(tmean.sem, tmean.at(b))
                mm(PS[0:E // 4, 7, 2:3], wb("se1", C), small(TMEAN), start=True, stop=True)\
                    .then_inc(se1_psum.sem, 1)
                pe.wait_ge(se1_ready.sem, se1_ready.at(b))
                mm(PS[0:C, 7, 3:4], wb("se2", E // 4), small(SE1, E // 4), start=True, stop=True)\
                    .then_inc(se2_psum.sem, 1)

        @block.vector
        def _(dve):
            v = nc.vector
            v.memset(small(EPS5, 128), 1e-5)
            v.memset(small(ONE, 128), 1.0)
            v.memset(small(CUBB, 128), -0.75 * CUB_SCALE)
            v.memset(small(CUBC, 128), 13 / 16)
            v.memset(small(LEAST, 128), 1e-36)
            v.memset(small(LNC, 128), LN_1E12).then_inc(setup_v.sem, 1)
            dve.wait_ge(loaded.sem, LOADS)
            dve.wait_ge(setup_a.sem, 3)
            steps = 1
            for k, (cb, g, bb, m, sc, off) in enumerate((("c1b", "bn1g", "bn1b", "bn1m", S1, B1C),
                                                         ("c2b", "bn2g", "bn2b", "bn2m", S2, B2C))):
                inv, dif = small(CT + 6, 128, 3), small(CT + 9, 128, 3)
                v.reciprocal(inv, small(CT + 3 * k, 128, 3)).then_inc(setup_v.sem, 1)
                v.tensor_tensor(dif, w(cb), w(m), ALU.subtract).then_inc(setup_v.sem, 1)
                steps += 2
                dve.wait_ge(setup_v.sem, steps)
                v.tensor_tensor(small(sc, 128, 3), w(g), inv, ALU.mult).then_inc(setup_v.sem, 1)
                steps += 1
                dve.wait_ge(setup_v.sem, steps)
                v.tensor_tensor(dif, dif, small(sc, 128, 3), ALU.mult).then_inc(setup_v.sem, 1)
                steps += 1
                dve.wait_ge(setup_v.sem, steps)
                v.tensor_tensor(small(off, 128, 3), dif, w(bb), ALU.add).then_inc(setup_v.sem, 1)
                steps += 1
                dve.wait_ge(setup_v.sem, steps)
            v.tensor_reduce(small(DSUM, 128, 2), w("ds").rearrange("p (a k) -> p a k", k=4), AX.X, ALU.add)\
                .then_inc(ready.sem, 1)
            dve.wait_ge(ready.sem, CONSTS)

            with dve.Fori(0, BATCH) as b:
                def group_norm(l, src, dst):
                    stats = small(BN_STATS, C, 6 * NCH).rearrange("p (a k) -> p a k", k=6)
                    for c in range(NCH):
                        v.bn_stats(stats[:, c, :], src[:, c * CH:(c + 1) * CH]).then_inc(gn_stat.sem, 1)
                    alone(dve, (gn_stat, gn_stat.at(b, (l + 1) * NCH)))
                    v.bn_aggr(small(MV, C, 2), stats).then_inc(gn_mv.sem, 1)
                    dve.wait_ge(gn_mean.sem, gn_mean.at(b, l + 1))
                    v.tensor_copy(small(MG + l), PS[0:C, 7, 0:1]).then_inc(gn_mg.sem, 1)
                    dve.wait_ge(gn_mg.sem, gn_mg.at(b, l + 1))
                    v.tensor_tensor(small(DM), small(MV), small(MG + l), ALU.subtract).then_inc(gn_dev.sem, 1)
                    dve.wait_ge(gn_dev.sem, gn_dev.at(b, l + 1))
                    v.scalar_tensor_tensor(out=small(VC), in0=small(DM), scalar=small(DM), in1=small(MV + 1),
                                           op0=ALU.mult, op1=ALU.add).then_inc(gn_vc.sem, 1)
                    dve.wait_ge(gn_std.sem, gn_std.at(b, l + 1))
                    v.reciprocal(small(RSTD + l), small(STD)).then_inc(gn_rstd.sem, 1)
                    dve.wait_ge(gn_rstd.sem, gn_rstd.at(b, l + 1))
                    v.tensor_scalar(dst, src, small(MG + l), small(RSTD + l), ALU.subtract, ALU.mult)\
                        .then_inc(xg_ready.sem, 1)

                dve.wait_ge(x_in.sem, b * 16 + 16)
                group_norm(0, X0, u(XG, L, C))
                dve.wait_ge(mu_ready.sem, mu_ready.at(b))
                dve.wait_ge(xg_ready.sem, xg_ready.at(b, 1))
                v.tensor_tensor(chunked(u(DD, L, C)), chunked(u(XG, L, C)), ps6(C), ALU.subtract)\
                    .then_inc(dev_ready.sem, 1)
                dve.wait_ge(nrm_inv.sem, nrm_inv.at(b))
                dve.wait_ge(stored.sem, b * 16 + 16)
                v.scalar_tensor_tensor(out=u(XN, L, C), in0=u(NR, L, C), scalar=1e12, in1=u(XG, L, C),
                                       op0=ALU.min, op1=ALU.mult).then_inc(xn_ready.sem, 1)
                dve.wait_ge(linv.sem, linv.at(b))
                v.scalar_tensor_tensor(out=u(XL, L, C), in0=u(DD, L, C), scalar=one("ln0w"), in1=u(NR, L, C),
                                       op0=ALU.mult, op1=ALU.mult).then_inc(lnorm.sem, 1)
                dve.wait_ge(lnorm.sem, lnorm.at(b))

                xl_img = image(u(XL, L, C))
                for t in range(TILES + 1):
                    if t < TILES:
                        p = t % 2
                        sims = PS[:, 2 * p:2 * p + 2, 0:KEYS // 2]
                        m8 = small(T_M8 + 8 * p, 128, 8)
                        alone(dve, (s_ready, s_ready.at(b, t + 1)), *([(z_ready, z_ready.at(b, t - 1))] if t >= 2 else []))
                        v.max(m8, sims).then_inc(m8_ready.sem, 1)
                        alone(dve, (m8_ready, m8_ready.at(b, t + 1)), *([(exp2_ready, exp2_ready.at(b, t - 1))] if t >= 2 else []))
                        v.match_replace(out=tb("rest", t).rearrange("p (a n) -> p a n", a=2), in_to_replace=m8,
                                        in_values=sims, imm_value=NEG).then_inc(rest_ready.sem, 1)
                    if t >= 1:
                        r = t - 1
                        i, j = divmod(r, NT_X)
                        dve.wait_ge(wt_psum.sem, wt_psum.at(b, r + 1))
                        if r >= 2:
                            dve.wait_ge(agg_psum.sem, agg_psum.at(b, r - 1))
                        v.tensor_copy(tb("wtsT", r, KC), PS[0:KC, 4:6, :].rearrange("p a n -> p (a n)")
                                      [:, 0:NKC * 128]).then_inc(wt_sb.sem, 1)
                    if t < TILES:
                        dve.wait_ge(z_ready.sem, z_ready.at(b, t + 1))
                        v.reciprocal(small(T_RZ + p, 128), small(T_Z + p, 128)).then_inc(rz_ready.sem, 1)
                        dve.wait_ge(rz_ready.sem, rz_ready.at(b, t + 1))
                        if t >= 2:
                            dve.wait_ge(wt_psum.sem, wt_psum.at(b, t - 1))
                        v.tensor_scalar(tb("diag", t), w("ident"), small(T_RZ + p, 128), None, ALU.mult)\
                            .then_inc(diag_ready.sem, 1)
                    if t >= 1:
                        dve.wait_ge(agg_psum.sem, agg_psum.at(b, r + 1))
                        dst = xl_img[:, TQ_Y * i:TQ_Y * (i + 1), TQ_X * j:TQ_X * (j + 1)]
                        v.scalar_tensor_tensor(out=dst, in0=dst, scalar=one("ln0b"),
                                               in1=PS[0:C, 7, 0:128].rearrange("p (h w) -> p h w", w=TQ_X),
                                               op0=ALU.add, op1=ALU.add).then_inc(enh_ready.sem, 1)

                dve.wait_ge(enh_ready.sem, enh_ready.at(b))
                v.tensor_tensor(X1[:, :], u(XL, L, C), X0, ALU.add).then_inc(x1_part.sem, 1)
                dve.wait_ge(ffn_psum.sem, ffn_psum.at(b))
                dve.wait_ge(x1_part.sem, x1_part.at(b))
                v.scalar_tensor_tensor(out=chunked(X1[:, :]), in0=ps6(C), scalar=one("b2"), in1=chunked(X1[:, :]),
                                       op0=ALU.add, op1=ALU.add).then_inc(x1_ready.sem, 1)
                dve.wait_ge(x1_ready.sem, x1_ready.at(b))

                def diagonals(at, weights, done):
                    v.tensor_tensor(u(at, 9 * 128).rearrange("p (k m) -> p k m", k=9),
                                    w("ident").unsqueeze(1).broadcast_to([128, 9, 128]),
                                    weights.unsqueeze(2).broadcast_to([128, 9, 128]), ALU.mult)\
                        .then_inc(done.sem, 1)

                def depthwise(acc, pad, weights, lo, tap, done):
                    pv = pad.rearrange("p (h w) -> p h w", w=PADW)
                    for k in range(9):
                        src, wk = pv[:, k // 3:k // 3 + H, k % 3:k % 3 + W], weights[:, k:k + 1]
                        if k == 0:
                            v.tensor_scalar(image(acc), src, wk, None, ALU.mult).then_inc(tap.sem, 1)
                        else:
                            dve.wait_ge(tap.sem, tap.at(b, lo + k))
                            v.scalar_tensor_tensor(out=image(acc), in0=src, scalar=wk, in1=image(acc),
                                                   op0=ALU.mult, op1=ALU.add)\
                                .then_inc(tap.sem if k < 8 else done.sem, 1)

                group_norm(1, X1[:, :], u(FG, L, C))
                diagonals(FDIAG, w("convw", 128, 0, 9), fdiag)
                dve.wait_ge(xi_pad.sem, xi_pad.at(b))
                depthwise(u(ACC), u(PAD[1], PADN), w("convw", 128, 9, 9), 0, ftap, fconv)
                for j in range(9):
                    if j < 8:
                        k, h = divmod(j, 2)
                        dve.wait_ge(hi_ready.sem, hi_ready.at(b, j + 1))
                        if j >= 2:
                            dve.wait_ge(mid_ready.sem, mid_ready.at(b, j - 1))
                            dve.wait_ge(lo_ready.sem, lo_ready.at(b, j - 1))
                        v.tensor_tensor(chunked(u(R1 + h * L // 2, L // 2, 96)), ps3(96, h),
                                        chunked(PBC[:, k, half(h)]), ALU.subtract).then_inc(r1_ready.sem, 1)
                    if j >= 1:
                        k, h = divmod(j - 1, 2)
                        dve.wait_ge(mid_ready.sem, mid_ready.at(b, j))
                        dve.wait_ge(r1_ready.sem, r1_ready.at(b, j))
                        v.tensor_tensor(PBC[64:96, k, half(h)], U[64:96, R1 + h * L // 2:R1 + (h + 1) * L // 2],
                                        mid[64:96, half(h)], ALU.subtract).then_inc(lo_ready.sem, 1)
                        v.tensor_copy(PBC[32:64, k, half(h)], mid[32:64, half(h)]).then_inc(mid_placed.sem, 1)

                def log1p(q):
                    dve.wait_ge(sp_cubic.sem, sp_cubic.at(b, q + 1))
                    dve.wait_ge(sp_ln.sem, sp_ln.at(b, q + 1))
                    v.scalar_tensor_tensor(out=TL[:, :], in0=TL[:, :], scalar=LOG_MARGIN, in1=TW[:, :],
                                           op0=ALU.add, op1=ALU.min).then_inc(sp_log1p.sem, 1)

                def dlt_and_cumsum(q):
                    p = q % 2
                    dve.wait_ge(sp_log1p.sem, sp_log1p.at(b, q + 1))
                    v.scalar_tensor_tensor(out=u(DL[p]), in0=u(DL[p]), scalar=0.0, in1=TL[:, :],
                                           op0=ALU.max, op1=ALU.add).then_inc(dlt_ready.sem, 1)
                    dve.wait_ge(dlt_ready.sem, dlt_ready.at(b, q + 1))
                    d, o = u(DL[p]), u(CS[p])
                    if q % 2:
                        d, o = d[:, ::-1], o[:, ::-1]
                    v.tensor_tensor_scan(o, d, d, 0.0, ALU.add, ALU.max).then_inc(cs_ready.sem, 1)

                def y_run(r):
                    at = piece_at(r)
                    dve.wait_ge(y_added.sem, b * PIECES + (r + 1) * NSTATE + RING)
                    if r // 3 % 2 == 0:
                        v.tensor_copy(u(YS + at, PC), two_banks(Y_BANK)).then_inc(y_out.sem, 1)
                    else:
                        dve.wait_ge(y_out.sem, y_out.at(b, 3 * (r // 3)))
                        v.tensor_tensor(XS[r // 6][:, at:at + PC], u(YS + at, PC), two_banks(Y_BANK), ALU.add)\
                            .then_inc(y_out.sem, 1)

                log1p(0)
                dlt_and_cumsum(0)

                def times_b(t):
                    gk = u(G[t % RING], PC)
                    dve.wait_ge(gu_ready.sem, gu_ready.at(b, t + 1))
                    dve.wait_ge(b_full.sem, b_full.at(b, t + 1))
                    v.tensor_tensor(gk, gk, two_banks(B_BANK), ALU.mult).then_inc(b_used.sem, 1)

                times_b(0)
                for r in range(RUNS):
                    q, i = divmod(r, 3)
                    for n in range(NSTATE):
                        t = r * NSTATE + n
                        gk, ak = u(G[n % RING], PC), u(A[n % RING], PC)
                        dve.wait_ge(b_used.sem, b_used.at(b, t + 1))
                        dve.wait_ge(a_ready.sem, a_ready.at(b, t + 1))
                        if i > 0:
                            dve.wait_ge(carried.sem, b * PIECES + t - NSTATE + 1 + RING)
                        hk, dk = (gk[:, ::-1], ak[:, ::-1]) if q % 2 else (gk, ak)
                        v.tensor_tensor_scan(hk, dk, hk, CARRY[:, n:n + 1] if i > 0 else 0.0, ALU.mult, ALU.add)\
                            .then_inc(scanned.sem, 1)
                        if t + 1 < PIECES:
                            times_b(t + 1)
                        if n == 0 and r >= 1:
                            y_run(r - 1)
                        dve.wait_ge(scanned.sem, scanned.at(b, t + 1))
                        dve.wait_ge(c_full.sem, c_full.at(b, t + 1))
                        v.tensor_tensor(ak, gk, two_banks(C_BANK[t % 2]), ALU.mult).then_inc(ch_ready.sem, 1)
                        if q + 1 < QS and t % PASS == LOG1P_AT:
                            log1p(q + 1)
                        if q + 1 < QS and t % PASS == CUMSUM_AT:
                            dlt_and_cumsum(q + 1)
                y_run(RUNS - 1)

                dve.wait_ge(ys_psum.sem, ys_psum.at(b, 1))
                v.tensor_scalar(u(ZG, L, C), X1[:, :], small(MG + 1), small(RSTD + 1), ALU.subtract, ALU.mult)\
                    .then_inc(zg_ready.sem, 1)
                diagonals(BDIAG, w("c2w", 128, 18, 9), bdiag)
                dve.wait_ge(ymu_psum.sem, ymu_psum.at(b))
                v.tensor_tensor(chunked(u(YA)), chunked(u(YA)), ps6(128), ALU.subtract).then_inc(yd_ready.sem, 1)
                v.tensor_tensor(chunked(u(YB, L, 64)), chunked(u(YB, L, 64)), ps6(64), ALU.subtract)\
                    .then_inc(yd_ready.sem, 1)
                dve.wait_ge(yinv.sem, yinv.at(b))
                parts = ((YA, 128, 0), (YB, 64, 1))
                for at, rows, k in parts:
                    v.scalar_tensor_tensor(out=u(at, L, rows), in0=u(at, L, rows), scalar=one("lng", rows, k),
                                           in1=u(SD, L, rows), op0=ALU.mult, op1=ALU.mult).then_inc(yunit.sem, 1)
                for at, rows, k in parts:
                    dve.wait_ge(yunit.sem, yunit.at(b, k + 1))
                    dve.wait_ge(z_psum.sem, z_psum.at(b, k + 1))
                    v.scalar_tensor_tensor(out=chunked(u(at, L, rows)), in0=chunked(u(at, L, rows)),
                                           scalar=one("lnb", rows, k), in1=ps6(rows), op0=ALU.add, op1=ALU.mult)\
                        .then_inc(u_ready.sem, 1)
                for k in range(2):
                    dve.wait_ge(c1_pad.sem, c1_pad.at(b, 2 * k + 2))
                    depthwise(u(MIX[k]), u(PAD2[k], PADN), w("c2w", 128, 9 * k, 9), 8 * k, btap, bconv)
                dve.wait_ge(se2_ready.sem, se2_ready.at(b))
                v.tensor_scalar(small(SE2), small(SE2), 1.0, None, ALU.add).then_inc(se_plus.sem, 1)
                dve.wait_ge(se_plus.sem, se_plus.at(b))
                v.scalar_tensor_tensor(out=u(OUT, L, C), in0=u(T3, L, C), scalar=small(SE2), in1=X1[:, :],
                                       op0=ALU.mult, op1=ALU.add).then_inc(out_ready.sem, 1)
                dve.wait_ge(out_ready.sem, out_ready.at(b))


def kernel(**inputs):
    import numpy as np
    import ml_dtypes
    import concourse.bacc as bacc
    from concourse import mybir
    from concourse.bass_utils import run_bass_kernel_spmd

    a = {k: np.ascontiguousarray(v) for k, v in inputs.items()}
    l0 = {k[8:]: v for k, v in a.items() if k.startswith("L0_conv_")}
    l1 = {k[8:]: v for k, v in a.items() if k.startswith("L1_conv_")}

    pk = np.zeros((128, PWIDTH), np.float32)

    def put(table, arr, name, value, lo=0, row=0):
        value = value.reshape(value.shape[0], -1)
        at, width = table[name]
        assert lo + value.shape[1] <= width
        arr[row:row + value.shape[0], at + lo:at + lo + value.shape[1]] = value

    def P(name, value, lo=0, row=0):
        put(PCOL, pk, name, value, lo, row)

    P("ident", np.eye(128, dtype=np.float32))
    same = (np.arange(C)[:, None] // 3 == np.arange(C)[None, :] // 3)
    P("gmean", np.where(same, np.float32(1 / 3), np.float32(0)))
    P("mean96", np.full((C, C), 1 / 96, np.float32))
    P("sum96", np.ones((C, C), np.float32))
    P("mean192", np.full((128, 128), 1 / 192, np.float32))
    P("w1", l0["w1"].T)
    P("w2", l0["w2"][:, 0:C].T)
    P("w2", l0["w2"][:, C:2 * C].T, C)
    ip = l1["in_proj_w"]
    P("in_a", ip[0:128].T)
    P("in_b", ip[128:192].T)
    P("in_b", ip[128:192].T, 64)
    P("z_a", ip[E:E + 128].T)
    P("z_b", ip[E + 128:2 * E].T)
    for s in range(2):
        for i, k in enumerate((s, 2 + s)):
            wt = l1["dt_proj_w"][k].T
            row = 32 * s + RANK * i
            P("dtw", wt[:, 0:128], i * 128, row)
            P("dtw", wt[:, 128:192], 256 + 64 * i, row)
    P("b1", l0["b1"].reshape(2, C).T)
    P("b2", l0["b2"][:, None])
    P("ln0w", l0["ln_w"][:, None])
    P("ln0b", l0["ln_b"][:, None])
    cw = l1["conv_w"].reshape(E, 9)
    P("convw", cw[0:128])
    P("convw", cw[128:192], 9)
    P("convw", cw[128:192], 9, 64)
    P("convb", l1["conv_b"][0:128, None])
    P("convb", l1["conv_b"][128:192, None], 1)
    P("convb", l1["conv_b"][128:192, None], 1, 64)
    for s in range(2):
        for i, k in enumerate((s, 2 + s)):
            P("dtb", l1["dt_proj_b"][k, 0:128, None], i * 2 + s)
            P("dtb", l1["dt_proj_b"][k, 128:192, None], 4 + s, 64 * i)
            P("alog", l1["A_log"][k, 0:128], (i * 2 + s) * NSTATE)
            P("alog", l1["A_log"][k, 128:192], (4 + s) * NSTATE, 64 * i)
    P("ds", l1["Ds"][:, 0:128].T)
    P("ds", l1["Ds"][:, 128:192].T, 4)
    for name, src in (("lng", "ln_g"), ("lnb", "ln_b")):
        P(name, l1[src][0:128, None])
        P(name, l1[src][128:192, None], 1)
    for name, src in (("c1b", "c1_b"), ("bn1g", "bn1_g"), ("bn1b", "bn1_b"), ("bn1m", "bn1_m"), ("bn1v", "bn1_v"),
                      ("c2b", "c2_b"), ("bn2g", "bn2_g"), ("bn2b", "bn2_b"), ("bn2m", "bn2_m"), ("bn2v", "bn2_v")):
        P(name, l1[src].reshape(3, 128).T)
    P("c2w", l1["c2_w"].reshape(3, 128, 9).transpose(1, 0, 2))
    P("c3b", l1["c3_b"][:, None])
    P("se1b", l1["se1_b"][:, None])
    P("se2b", l1["se2_b"][:, None])

    bk = np.zeros((128, BWIDTH), np.float32)
    c1 = l1["c1_w"].reshape(2 * E, E).T
    put(BCOL, bk, "c1a", c1[0:128])
    put(BCOL, bk, "c1bm", c1[128:192])
    put(BCOL, bk, "c3", l1["c3_w"].reshape(C, 3, 128).transpose(2, 1, 0))
    put(BCOL, bk, "se1", l1["se1_w"].T)
    put(BCOL, bk, "se2", l1["se2_w"].T)

    xp = np.zeros((128, 3, 4, XPM), np.float32)
    for s in range(2):
        for i, k in enumerate((s, 2 + s)):
            wt = l1["x_proj_w"][k].T
            for bc in range(2):
                cols = wt[:, RANK + NSTATE * bc:RANK + NSTATE * (bc + 1)]
                places = [(32 * r + 16 * i, cols) for r in range(3)]
                if bc == 0:
                    places.append((96 + RANK * i, wt[:, 0:RANK]))
                for at, part in places:
                    xp[:, i, 2 * s + bc, at:at + part.shape[1]] = part[0:128]
                    xp[64 * i:64 * i + 64, 2, 2 * s + bc, at:at + part.shape[1]] = part[128:192]

    sel = np.zeros((96, 3, NSTATE, 128), np.float32)
    for r in range(3):
        for n in range(NSTATE):
            sel[32 * r + n, 0, n, :] = 1
            sel[32 * r + 16 + n, 1, n, :] = 1
            sel[32 * r + n, 2, n, 0:64] = 1
            sel[32 * r + 16 + n, 2, n, 64:128] = 1
    mq = np.zeros((24, 128), np.float32)
    for y in range(TQ_Y):
        for xx in range(TQ_X):
            mq[y, y * TQ_X + xx] = 1
            mq[TQ_Y + xx, y * TQ_X + xx] = 1
    mk = np.zeros((24, 3, 3, KEY_Y, KEY_X), np.float32)
    tiles_y, tiles_x = (0, 1, NT_Y - 1), (0, 1, NT_X - 1)
    for a_, i in enumerate(tiles_y):
        for b_, j in enumerate(tiles_x):
            ky, kx = key_origin(i, j)
            for y in range(TQ_Y):
                far = np.abs(ky + np.arange(KEY_Y) - (TQ_Y * i + y)) > HALF_WIN
                mk[y, a_, b_][far, :] = -1024
            for xx in range(TQ_X):
                far = np.abs(kx + np.arange(KEY_X) - (TQ_X * j + xx)) > HALF_WIN
                mk[TQ_Y + xx, a_, b_][:, far] = -1024

    arrays = {
        "x": a["x"].reshape(BATCH * C, L), "pack": pk, "back": bk, "xpw": xp.reshape(128, XPW),
        "masks": mk.reshape(24, 9 * KEYS).astype(ml_dtypes.bfloat16), "maskq": mq.astype(ml_dtypes.bfloat16),
        "sels": sel.reshape(96, -1).astype(ml_dtypes.bfloat16),
    }
    nc = bacc.Bacc("TRN2", target_bir_lowering=False, num_devices=1)
    args = [nc.dram_tensor(f"in_{n}", v.shape, mybir.dt.from_np(v.dtype), kind="ExternalInput").ap()
            for n, v in arrays.items()]
    out = nc.dram_tensor("out", (BATCH * C, L), mybir.dt.float32, kind="ExternalOutput").ap()
    build(nc, *args, out)
    r = run_bass_kernel_spmd(nc, [{f"in_{n}": v for n, v in arrays.items()}], core_ids=[0])
    return r.results[0]["out"].reshape(BATCH, C, H, W)
```
